# Optimizing a Trainium2 kernel written in Bass

```python
import numpy as np
import jax
import jax.numpy as jnp

def _softmax(x, axis=-1):
    return jax.nn.softmax(x, axis=axis)

def _gelu(x):
    return jax.nn.gelu(x, approximate=True)

def _silu(x):
    return jax.nn.silu(x)

def _sigmoid(x):
    return jax.nn.sigmoid(x)

def _layernorm(x, axis=-1, eps=1e-05):
    m = jnp.mean(x, axis=axis, keepdims=True)
    v = jnp.var(x, axis=axis, keepdims=True)
    return (x - m) / jnp.sqrt(v + eps)

def _scatter_add(tgt, idx, src, axis=0):
    return tgt.at[idx].add(src)

def _segment_sum(src, seg, n):
    return jax.ops.segment_sum(src, seg, n)
kernel_name = 'mk_decoder_postln_d2_seqx_r8_7a09f6'

def setup_inputs(seed: int=0):
    np.random.seed(seed)
    _w = jnp.asarray

    def _rec_inputs():
        import jax
        import jax.numpy as jnp
        _rk = jax.random.key(seed)
        x = -0.0002928 + 1 * jax.random.normal(jax.random.fold_in(_rk, 1), (64, 64, 128), jnp.float32)
        _lenS = 64 - jax.random.randint(jax.random.fold_in(_rk, 7), (64,), 0, max(1, 64 // 4) + 1, jnp.int32)
        _lenS2 = 64 - jax.random.randint(jax.random.fold_in(_rk, 8), (64,), 0, max(1, 64 // 4) + 1, jnp.int32)
        _ctx_1024P = jax.random.normal(jax.random.fold_in(_rk, 11), (64, 16, 128), jnp.float32)
        _ctx_1024c = jax.random.dirichlet(jax.random.fold_in(_rk, 511), 0.3 * jnp.ones((16,), jnp.float32), (64, 64))
        _ctx_1024t = jnp.einsum('bsk,bkd->bsd', _ctx_1024c, _ctx_1024P)
        _ctx_1024t = _ctx_1024t * jax.lax.rsqrt(jnp.mean(jnp.square(_ctx_1024t)) + 1e-12) * 0.953939
        ctx_1024 = -1.39393e-06 + 0.999914 * (_ctx_1024t + 0.3 * jax.random.normal(jax.random.fold_in(_rk, 611), (64, 64, 128), jnp.float32))
        _validS = jnp.arange(64)[None, :] < _lenS[:, None]
        _validS2 = jnp.arange(64)[None, :] < _lenS2[:, None]
        _causal = jnp.tril(jnp.ones((64, 64), dtype=bool))
        mask_BxS2_bk0 = jnp.logical_not(jnp.broadcast_to(_validS2[:, :], (64, 64)))
        return (x, ctx_1024, mask_BxS2_bk0)
    x, ctx_1024, mask_BxS2_bk0 = _rec_inputs()

    def _L0_attn_setup():
        import jax, jax.numpy as jnp
        import numpy as np
        B, N, DIM = (2, 256, 128)
        H = 16
        HD = DIM // H
        key = jax.random.key(seed)
        ks = jax.random.split(key, 4)
        x = jax.random.normal(ks[0], (B, N, DIM), dtype=jnp.float32)
        w_qkv = jax.random.normal(ks[1], (DIM, 3 * DIM), dtype=jnp.float32) / np.sqrt(DIM)
        w_proj = jax.random.normal(ks[2], (DIM, DIM), dtype=jnp.float32) / np.sqrt(DIM)
        b_proj = jax.random.normal(ks[3], (DIM,), dtype=jnp.float32) * 0.01
        return {'x': x, 'w_qkv': w_qkv, 'w_proj': w_proj, 'b_proj': b_proj}
    _L0_attn_all = _L0_attn_setup()
    _L0_attn_in = {k: v for k, v in _L0_attn_all.items() if k in ('w_qkv', 'w_proj', 'b_proj')}
    del _L0_attn_all

    def _L0_xattn_setup():
        import jax, jax.numpy as jnp
        import numpy as np
        NUM_HEADS = 16
        key = jax.random.key(seed)
        ks = jax.random.split(key, 8)
        B, S, E = (2, 256, 128)
        std = 0.02
        return {'q': jax.random.normal(ks[0], (B, S, E), dtype=jnp.float32), 'k': jax.random.normal(ks[1], (B, S, E), dtype=jnp.float32), 'v': jax.random.normal(ks[2], (B, S, E), dtype=jnp.float32), 'Wq': jax.random.normal(ks[3], (E, E), dtype=jnp.float32) * std, 'Wk': jax.random.normal(ks[4], (E, E), dtype=jnp.float32) * std, 'Wv': jax.random.normal(ks[5], (E, E), dtype=jnp.float32) * std, 'Wo': jax.random.normal(ks[6], (E, E), dtype=jnp.float32) * std, 'bo': jnp.zeros((E,), dtype=jnp.float32)}
    _L0_xattn_all = _L0_xattn_setup()
    _L0_xattn_in = {k: v for k, v in _L0_xattn_all.items() if k in ('Wq', 'Wk', 'Wv', 'Wo', 'bo')}
    del _L0_xattn_all

    def _L0_ffn_setup():
        import jax, jax.numpy as jnp
        import numpy as np

        def _bitlinear(x, w_latent):
            scale = jax.lax.stop_gradient(jnp.clip(jnp.mean(jnp.abs(w_latent), axis=1, keepdims=True), 1e-05, None))
            tern = jnp.clip(jnp.round(w_latent / scale), -1.0, 1.0)
            w = w_latent + jax.lax.stop_gradient(tern - w_latent)
            return x @ (w * scale).T
        key = jax.random.key(seed)
        ks = jax.random.split(key, 6)
        dim, hidden, rank = (128, 512, 16)
        B, S = (4, 512)
        x = jax.random.normal(ks[0], (B, S, dim), dtype=jnp.float32)
        w_fc = 0.02 * jax.random.normal(ks[1], (hidden, dim), dtype=jnp.float32)
        w_proj = 0.02 * jax.random.normal(ks[2], (dim, hidden), dtype=jnp.float32)
        u = 0.02 * jax.random.normal(ks[3], (hidden, rank), dtype=jnp.float32)
        v = 0.02 * jax.random.normal(ks[4], (rank, dim), dtype=jnp.float32)
        fast_b = jax.random.normal(ks[5], (rank, rank), dtype=jnp.float32)
        gate = jnp.float32(0.05)
        return {'x': x, 'fast_b': fast_b, 'w_fc': w_fc, 'w_proj': w_proj, 'u': u, 'v': v, 'gate': gate}
    _L0_ffn_all = _L0_ffn_setup()
    _L0_ffn_in = {k: v for k, v in _L0_ffn_all.items() if k in ('fast_b', 'w_fc', 'w_proj', 'u', 'v', 'gate')}
    del _L0_ffn_all

    def _L1_attn_setup():
        import jax, jax.numpy as jnp
        import numpy as np
        D_MODEL = 128
        N_HEADS = 16
        D_HEAD = 64
        LAMBDA_INIT = 0.8
        key = jax.random.key(seed)
        ks = jax.random.split(key, 6)
        B, S = (2, 256)
        std = 0.02
        x = jax.random.normal(ks[0], (B, S, D_MODEL), dtype=jnp.float32)
        Wq = jax.random.normal(ks[1], (D_MODEL, 2 * N_HEADS * D_HEAD), dtype=jnp.float32) * std
        Wk = jax.random.normal(ks[2], (D_MODEL, 2 * N_HEADS * D_HEAD), dtype=jnp.float32) * std
        Wv = jax.random.normal(ks[3], (D_MODEL, 2 * N_HEADS * D_HEAD), dtype=jnp.float32) * std
        Wo = jax.random.normal(ks[4], (N_HEADS * D_HEAD, D_MODEL), dtype=jnp.float32) * std
        lq1 = jnp.zeros((D_HEAD,), dtype=jnp.float32)
        lk1 = jnp.zeros((D_HEAD,), dtype=jnp.float32)
        lq2 = jnp.zeros((D_HEAD,), dtype=jnp.float32)
        lk2 = jnp.zeros((D_HEAD,), dtype=jnp.float32)
        return {'x': x, 'Wq': Wq, 'Wk': Wk, 'Wv': Wv, 'Wo': Wo, 'lq1': lq1, 'lk1': lk1, 'lq2': lq2, 'lk2': lk2}
    _L1_attn_all = _L1_attn_setup()
    _L1_attn_in = {k: v for k, v in _L1_attn_all.items() if k in ('Wq', 'Wk', 'Wv', 'Wo', 'lq1', 'lk1', 'lq2', 'lk2')}
    del _L1_attn_all

    def _L1_xattn_setup():
        import jax, jax.numpy as jnp
        import numpy as np
        EPS = 1e-05

        def layer_norm(x, g, b):
            mu = jnp.mean(x, axis=-1, keepdims=True)
            var = jnp.mean((x - mu) ** 2, axis=-1, keepdims=True)
            return (x - mu) * jax.lax.rsqrt(var + EPS) * g + b
        key = jax.random.key(seed)
        ks = jax.random.split(key, 8)
        b, n, l, D = (8, 512, 64, 128)
        heads, dim_head = (16, 64)
        inner = heads * dim_head
        x = jax.random.normal(ks[0], (b, n, D), dtype=jnp.float32)
        latents = jax.random.normal(ks[1], (b, l, D), dtype=jnp.float32)
        mask = jax.random.randint(ks[2], (b, n), 0, 2) > 0
        Wq = jax.random.normal(ks[3], (D, inner), dtype=jnp.float32) * D ** (-0.5)
        Wkv = jax.random.normal(ks[4], (D, 2 * inner), dtype=jnp.float32) * D ** (-0.5)
        Wout = jax.random.normal(ks[5], (inner, D), dtype=jnp.float32) * inner ** (-0.5)
        g1 = jnp.ones((D,), jnp.float32)
        b1 = jnp.zeros((D,), jnp.float32)
        g2 = jnp.ones((D,), jnp.float32)
        b2 = jnp.zeros((D,), jnp.float32)
        return {'x': x, 'latents': latents, 'mask': mask, 'g1': g1, 'b1': b1, 'g2': g2, 'b2': b2, 'Wq': Wq, 'Wkv': Wkv, 'Wout': Wout}
    _L1_xattn_all = _L1_xattn_setup()
    _L1_xattn_in = {k: v for k, v in _L1_xattn_all.items() if k in ('g1', 'b1', 'g2', 'b2', 'Wq', 'Wkv', 'Wout')}
    del _L1_xattn_all

    def _L1_ffn_setup():
        import jax, jax.numpy as jnp
        import numpy as np
        MIN_EXPERT_CAPACITY = 4
        CAPACITY_FACTOR = 1.0

        def _moe_forward(x, router_w, w1, b1, w2, b2):
            B, S, D = x.shape
            E = router_w.shape[1]
            G = 1
            T = B * S
            C = max(int(round(CAPACITY_FACTOR * T / E)), MIN_EXPERT_CAPACITY)
            xt = x.reshape(G, T, D)
            logits = jnp.einsum('gtd,de->gte', xt, router_w)
            probs = jax.nn.softmax(logits, axis=-1)
            gate = jnp.max(probs, axis=-1)
            idx = jnp.argmax(probs, axis=-1)
            emask = jax.nn.one_hot(idx, E, dtype=x.dtype)
            pos = jnp.cumsum(emask, axis=1) * emask - 1.0
            pos = pos.astype(jnp.int32)
            slot = jax.nn.one_hot(pos, C, dtype=x.dtype)
            dispatch = emask[..., None] * slot
            combine = dispatch * gate[..., None, None]
            expert_inputs = jnp.einsum('gtd,gtec->gecd', xt, dispatch)
            h = jax.nn.relu(jnp.einsum('gecd,edf->gecf', expert_inputs, w1) + b1[None, :, None, :])
            expert_outputs = jnp.einsum('gecf,efd->gecd', h, w2) + b2[None, :, None, :]
            out = jnp.einsum('gecd,gtec->gtd', expert_outputs, combine)
            return out.reshape(B, S, D)
        key = jax.random.key(seed)
        k0, k1, k2, k3 = jax.random.split(key, 4)
        B, S, D, E, F = (4, 256, 128, 8, 512)
        x = jax.random.normal(k0, (B, S, D), dtype=jnp.float32)
        router_w = jax.random.normal(k1, (D, E), dtype=jnp.float32) * D ** (-0.5)
        w1 = jax.random.normal(k2, (E, D, F), dtype=jnp.float32) * D ** (-0.5)
        b1 = jnp.zeros((E, F), dtype=jnp.float32)
        w2 = jax.random.normal(k3, (E, F, D), dtype=jnp.float32) * F ** (-0.5)
        b2 = jnp.zeros((E, D), dtype=jnp.float32)
        return {'x': x, 'router_w': router_w, 'w1': w1, 'b1': b1, 'w2': w2, 'b2': b2}
    _L1_ffn_all = _L1_ffn_setup()
    _L1_ffn_in = {k: v for k, v in _L1_ffn_all.items() if k in ('router_w', 'w1', 'b1', 'w2', 'b2')}
    del _L1_ffn_all
    return {'x': x, 'ctx_1024': ctx_1024, 'mask_BxS2_bk0': mask_BxS2_bk0, 'L0_attn_w_qkv': _L0_attn_in['w_qkv'], 'L0_attn_w_proj': _L0_attn_in['w_proj'], 'L0_attn_b_proj': _L0_attn_in['b_proj'], 'L0_xattn_Wq': _L0_xattn_in['Wq'], 'L0_xattn_Wk': _L0_xattn_in['Wk'], 'L0_xattn_Wv': _L0_xattn_in['Wv'], 'L0_xattn_Wo': _L0_xattn_in['Wo'], 'L0_xattn_bo': _L0_xattn_in['bo'], 'L0_ffn_fast_b': _L0_ffn_in['fast_b'], 'L0_ffn_w_fc': _L0_ffn_in['w_fc'], 'L0_ffn_w_proj': _L0_ffn_in['w_proj'], 'L0_ffn_u': _L0_ffn_in['u'], 'L0_ffn_v': _L0_ffn_in['v'], 'L0_ffn_gate': _L0_ffn_in['gate'], 'L1_attn_Wq': _L1_attn_in['Wq'], 'L1_attn_Wk': _L1_attn_in['Wk'], 'L1_attn_Wv': _L1_attn_in['Wv'], 'L1_attn_Wo': _L1_attn_in['Wo'], 'L1_attn_lq1': _L1_attn_in['lq1'], 'L1_attn_lk1': _L1_attn_in['lk1'], 'L1_attn_lq2': _L1_attn_in['lq2'], 'L1_attn_lk2': _L1_attn_in['lk2'], 'L1_xattn_g1': _L1_xattn_in['g1'], 'L1_xattn_b1': _L1_xattn_in['b1'], 'L1_xattn_g2': _L1_xattn_in['g2'], 'L1_xattn_b2': _L1_xattn_in['b2'], 'L1_xattn_Wq': _L1_xattn_in['Wq'], 'L1_xattn_Wkv': _L1_xattn_in['Wkv'], 'L1_xattn_Wout': _L1_xattn_in['Wout'], 'L1_ffn_router_w': _L1_ffn_in['router_w'], 'L1_ffn_w1': _L1_ffn_in['w1'], 'L1_ffn_b1': _L1_ffn_in['b1'], 'L1_ffn_w2': _L1_ffn_in['w2'], 'L1_ffn_b2': _L1_ffn_in['b2']}

def reference(x, ctx_1024, mask_BxS2_bk0, L0_attn_w_qkv, L0_attn_w_proj, L0_attn_b_proj, L0_xattn_Wq, L0_xattn_Wk, L0_xattn_Wv, L0_xattn_Wo, L0_xattn_bo, L0_ffn_fast_b, L0_ffn_w_fc, L0_ffn_w_proj, L0_ffn_u, L0_ffn_v, L0_ffn_gate, L1_attn_Wq, L1_attn_Wk, L1_attn_Wv, L1_attn_Wo, L1_attn_lq1, L1_attn_lk1, L1_attn_lq2, L1_attn_lk2, L1_xattn_g1, L1_xattn_b1, L1_xattn_g2, L1_xattn_b2, L1_xattn_Wq, L1_xattn_Wkv, L1_xattn_Wout, L1_ffn_router_w, L1_ffn_w1, L1_ffn_b1, L1_ffn_w2, L1_ffn_b2):
    import jax
    import jax.numpy as jnp

    def _L0_attn_ref(x, w_qkv, w_proj, b_proj):
        import jax, jax.numpy as jnp
        import numpy as np
        B, N, DIM = (2, 256, 128)
        H = 16
        HD = DIM // H
        b, n, c = x.shape
        scale = HD ** (-0.5)
        qkv = jnp.einsum('bnc,cd->bnd', x, w_qkv)
        qkv = qkv.reshape(b, n, 3, H, HD).transpose(2, 0, 3, 1, 4)
        q, k, v = (qkv[0], qkv[1], qkv[2])
        q = q * scale
        attn = jnp.einsum('bhnd,bhmd->bhnm', q, k)
        attn = jax.nn.softmax(attn, axis=-1)
        out = jnp.einsum('bhnm,bhmd->bhnd', attn, v)
        out = out.transpose(0, 2, 1, 3).reshape(b, n, c)
        return jnp.einsum('bnc,cd->bnd', out, w_proj) + b_proj

    def _L0_xattn_ref(q, k, v, Wq, Wk, Wv, Wo, bo):
        import jax, jax.numpy as jnp
        import numpy as np
        NUM_HEADS = 16
        B, S, E = q.shape
        H = NUM_HEADS
        D = E // H
        Q = (q @ Wq.T).reshape(B, S, H, D).transpose(0, 2, 1, 3)
        K = (k @ Wk.T).reshape(B, S, H, D).transpose(0, 2, 1, 3)
        V = (v @ Wv.T).reshape(B, S, H, D).transpose(0, 2, 1, 3)
        scores = jnp.einsum('bhsd,bhtd->bhst', Q, K)
        causal = jnp.tril(jnp.ones((S, S), dtype=bool))
        scores = jnp.where(causal, scores, -jnp.inf)
        scores = scores / np.sqrt(D).astype(np.float32)
        attn = jax.nn.softmax(scores, axis=-1)
        out = jnp.einsum('bhst,bhtd->bhsd', attn, V)
        out = out.transpose(0, 2, 1, 3).reshape(B, S, E)
        return out @ Wo.T + bo

    def _L0_ffn_ref(x, fast_b, w_fc, w_proj, u, v, gate):
        import jax, jax.numpy as jnp
        import numpy as np

        def _bitlinear(x, w_latent):
            scale = jax.lax.stop_gradient(jnp.clip(jnp.mean(jnp.abs(w_latent), axis=1, keepdims=True), 1e-05, None))
            tern = jnp.clip(jnp.round(w_latent / scale), -1.0, 1.0)
            w = w_latent + jax.lax.stop_gradient(tern - w_latent)
            return x @ (w * scale).T
        h = _bitlinear(x, w_fc) + gate * (x @ v.T @ fast_b.T @ u.T)
        r = jnp.maximum(h, 0.0)
        return _bitlinear(r * r, w_proj)

    def _L1_attn_ref(x, Wq, Wk, Wv, Wo, lq1, lk1, lq2, lk2):
        import jax, jax.numpy as jnp
        import numpy as np
        D_MODEL = 128
        N_HEADS = 16
        D_HEAD = 64
        LAMBDA_INIT = 0.8
        B, S, D = x.shape
        h, dh = (N_HEADS, D_HEAD)
        q = (x @ Wq).reshape(B, S, 2, h, dh)
        k = (x @ Wk).reshape(B, S, 2, h, dh)
        v = (x @ Wv).reshape(B, S, 2, h, dh)
        q1, q2 = (q[:, :, 0], q[:, :, 1])
        k1, k2 = (k[:, :, 0], k[:, :, 1])
        v1, v2 = (v[:, :, 0], v[:, :, 1])
        scale = 1.0 / jnp.sqrt(jnp.asarray(dh, dtype=x.dtype))
        lam = jnp.exp(jnp.dot(lq1, lk1)) - jnp.exp(jnp.dot(lq2, lk2)) + LAMBDA_INIT
        causal = jnp.tril(jnp.ones((S, S), dtype=bool))
        neg_inf = jnp.asarray(-1e+30, dtype=x.dtype)
        s1 = jnp.einsum('bshd,bthd->bhst', q1, k1) * scale
        s2 = jnp.einsum('bshd,bthd->bhst', q2, k2) * scale
        s1 = jnp.where(causal, s1, neg_inf)
        s2 = jnp.where(causal, s2, neg_inf)
        a1 = jax.nn.softmax(s1, axis=-1)
        a2 = jax.nn.softmax(s2, axis=-1)
        o = jnp.einsum('bhst,bthd->bshd', a1, v1) - lam * jnp.einsum('bhst,bthd->bshd', a2, v2)
        o = o.reshape(B, S, h * dh) * (1.0 - LAMBDA_INIT)
        return o @ Wo

    def _L1_xattn_ref(x, latents, mask, g1, b1, g2, b2, Wq, Wkv, Wout):
        import jax, jax.numpy as jnp
        import numpy as np
        EPS = 1e-05

        def layer_norm(x, g, b):
            mu = jnp.mean(x, axis=-1, keepdims=True)
            var = jnp.mean((x - mu) ** 2, axis=-1, keepdims=True)
            return (x - mu) * jax.lax.rsqrt(var + EPS) * g + b
        heads, dim_head = (16, 64)
        b, n, D = x.shape
        l = latents.shape[1]
        xn = layer_norm(x, g1, b1)
        ln_lat = layer_norm(latents, g2, b2)
        q = ln_lat @ Wq
        kv = jnp.concatenate([xn, ln_lat], axis=1) @ Wkv
        k, v = jnp.split(kv, 2, axis=-1)

        def to_heads(t):
            return t.reshape(t.shape[0], t.shape[1], heads, dim_head).transpose(0, 2, 1, 3)
        q, k, v = (to_heads(q), to_heads(k), to_heads(v))
        scale = 1.0 / np.sqrt(np.sqrt(dim_head)).astype(np.float32)
        weight = jnp.einsum('bhld,bhnd->bhln', q * scale, k * scale)
        full_mask = jnp.concatenate([mask, jnp.ones((b, l), dtype=bool)], axis=1)
        neg = -jnp.finfo(weight.dtype).max
        weight = jnp.where(full_mask[:, None, None, :], weight, neg)
        weight = jax.nn.softmax(weight.astype(jnp.float32), axis=-1).astype(q.dtype)
        out = jnp.einsum('bhln,bhnd->bhld', weight, v)
        out = out.transpose(0, 2, 1, 3).reshape(b, l, heads * dim_head)
        return out @ Wout

    def _L1_ffn_ref(x, router_w, w1, b1, w2, b2):
        import jax, jax.numpy as jnp
        import numpy as np
        MIN_EXPERT_CAPACITY = 4
        CAPACITY_FACTOR = 1.0

        def _moe_forward(x, router_w, w1, b1, w2, b2):
            B, S, D = x.shape
            E = router_w.shape[1]
            G = 1
            T = B * S
            C = max(int(round(CAPACITY_FACTOR * T / E)), MIN_EXPERT_CAPACITY)
            xt = x.reshape(G, T, D)
            logits = jnp.einsum('gtd,de->gte', xt, router_w)
            probs = jax.nn.softmax(logits, axis=-1)
            gate = jnp.max(probs, axis=-1)
            idx = jnp.argmax(probs, axis=-1)
            emask = jax.nn.one_hot(idx, E, dtype=x.dtype)
            pos = jnp.cumsum(emask, axis=1) * emask - 1.0
            pos = pos.astype(jnp.int32)
            slot = jax.nn.one_hot(pos, C, dtype=x.dtype)
            dispatch = emask[..., None] * slot
            combine = dispatch * gate[..., None, None]
            expert_inputs = jnp.einsum('gtd,gtec->gecd', xt, dispatch)
            h = jax.nn.relu(jnp.einsum('gecd,edf->gecf', expert_inputs, w1) + b1[None, :, None, :])
            expert_outputs = jnp.einsum('gecf,efd->gecd', h, w2) + b2[None, :, None, :]
            out = jnp.einsum('gecd,gtec->gtd', expert_outputs, combine)
            return out.reshape(B, S, D)
        return _moe_forward(x, router_w, w1, b1, w2, b2)
    x = _layernorm(x + _L0_attn_ref(x, L0_attn_w_qkv, L0_attn_w_proj, L0_attn_b_proj), axis=-1)
    x = _layernorm(x + _L0_xattn_ref(x, ctx_1024, ctx_1024, L0_xattn_Wq, L0_xattn_Wk, L0_xattn_Wv, L0_xattn_Wo, L0_xattn_bo), axis=-1)
    x = _layernorm(x + _L0_ffn_ref(x, L0_ffn_fast_b, L0_ffn_w_fc, L0_ffn_w_proj, L0_ffn_u, L0_ffn_v, L0_ffn_gate), axis=-1)
    x = _layernorm(x + _L1_attn_ref(x, L1_attn_Wq, L1_attn_Wk, L1_attn_Wv, L1_attn_Wo, L1_attn_lq1, L1_attn_lk1, L1_attn_lq2, L1_attn_lk2), axis=-1)
    x = _layernorm(x + _L1_xattn_ref(ctx_1024, x, mask_BxS2_bk0, L1_xattn_g1, L1_xattn_b1, L1_xattn_g2, L1_xattn_b2, L1_xattn_Wq, L1_xattn_Wkv, L1_xattn_Wout), axis=-1)
    x = _layernorm(x + _L1_ffn_ref(x, L1_ffn_router_w, L1_ffn_w1, L1_ffn_b1, L1_ffn_w2, L1_ffn_b2), axis=-1)
    return x

_drawn_inputs = setup_inputs


def setup_inputs(seed=0):
    import zlib

    import numpy as np

    out = dict(_drawn_inputs(seed))
    spreads = {'L0_xattn_bo': (0.0, 0.1),
     'L1_attn_lq1': (0.0, 2.0),
     'L1_attn_lk1': (0.0, 2.0),
     'L1_attn_lq2': (0.0, 0.689),
     'L1_attn_lk2': (0.0, 0.689),
     'L1_xattn_g1': (1.0, 0.2),
     'L1_xattn_b1': (0.0, 0.1),
     'L1_xattn_g2': (1.0, 0.2),
     'L1_xattn_b2': (0.0, 0.1),
     'L1_ffn_b1': (0.0, 0.324),
     'L1_ffn_b2': (0.0, 0.299)}
    factors = {'L0_xattn_Wq': 8.0,
     'L0_xattn_Wk': 8.0,
     'L0_ffn_fast_b': 8.0,
     'L0_ffn_u': 8.0,
     'L0_ffn_v': 8.0,
     'L1_attn_Wq': 8.0,
     'L1_attn_Wk': 8.0}
    for name, (base, spread) in spreads.items():
        noise = np.random.default_rng([zlib.crc32(name.encode()), seed]).standard_normal(out[name].shape)
        drawn = base * np.exp(spread * noise) if base else spread * noise
        out[name] = jnp.asarray(drawn.astype(out[name].dtype))
    for name, factor in factors.items():
        out[name] = (out[name] * factor).astype(out[name].dtype)
    return out
```

```python
from contextlib import ExitStack

import concourse.bass as bass
from concourse import mybir

F32 = mybir.dt.float32
BF16 = mybir.dt.bfloat16
I32 = mybir.dt.int32
U8 = mybir.dt.uint8
U32 = mybir.dt.uint32
ALU = mybir.AluOpType
ACT = mybir.ActivationFunctionType
AX = mybir.AxisListType

P = 128
B, S, D = 64, 64, 128
NPAIR = B * S // P
H0, HD0 = 16, 8
H1, HD1 = 16, 64
EPS = 1e-5
NEG = -1e30
FF = 512
E, CAP = 8, 512
DUMP = E * CAP


def wait(eng, sem, count):
    if not isinstance(count, int) or count > 0:
        eng.wait_ge(sem, count)


def bcast_rows(ap, rows=P):
    return bass.AP(ap.tensor, ap.offset, [[0, rows]] + list(ap.ap))


class Core:

    def __init__(self, nc, ctx):
        self.nc, self.ctx, self.sems = nc, ctx, {}
        self.bank = [ctx.enter_context(nc.psum_tensor(f"bank{n}", [P, 512], F32)) for n in range(8)]
        self.ident = self.sb("ident", [P, P], F32)
        self.identb = self.sb("identb", [P, P], BF16)
        self.causal = self.sb("causal", [P, S], BF16)
        self.eps_pow = self.sb("eps_pow", [P, 1], F32)

    def sb(self, name, shape, dt=F32, ctx=None):
        return (ctx or self.ctx).enter_context(self.nc.sbuf_tensor(name, shape, dt))

    def sem(self, name, ctx):
        handle = self.nc.alloc_semaphore(name)
        if ctx not in self.sems:
            self.sems[ctx] = []
            ctx.callback(self.give_back, ctx)
        self.sems[ctx].append(handle)
        return handle

    def give_back(self, ctx):
        self.nc.clear_and_free_semaphores(self.sems.pop(ctx))
        self.nc.all_engine_barrier(sem_only=True)


def constants_phase(core):
    nc = core.nc
    with ExitStack() as ctx:
        zero_done = core.sem("const_zero_done", ctx)
        chain = core.sem("const_chain", ctx)
        block = ctx.enter_context(nc.Block())

        @block.vector
        def _(dve):
            nc.vector.memset(core.ident[:, :], 0.0).then_inc(zero_done, 1)
            nc.vector.memset(core.causal[:, :], 0.0).then_inc(zero_done, 1)
            nc.vector.memset(core.eps_pow[:, :], -0.5).then_inc(zero_done, 1)
            dve.wait_ge(chain, 1)
            nc.vector.tensor_copy(core.identb[:, :], core.ident[:, :]).then_inc(zero_done, 1)

        @block.gpsimd
        def _(pool):
            pool.wait_ge(zero_done, 2)
            nc.gpsimd.affine_select(out=core.ident[:, :], in_=core.ident[:, :], compare_op=ALU.not_equal,
                                    fill=1.0, base=0, pattern=[[-1, P]], channel_multiplier=1).then_inc(chain, 1)
            for b in range(2):
                half = core.causal[b * S:(b + 1) * S, :]
                pool.wait_ge(chain, 1 + b)
                nc.gpsimd.affine_select(out=half, in_=half, compare_op=ALU.is_ge, fill=NEG, base=0,
                                        pattern=[[-1, S]], channel_multiplier=1).then_inc(chain, 1)


def low_head_phase(core, tag, x_in, kv_in, x_out, load_weights, bias, causal):
    nc = core.nc
    cross = kv_in is not None
    with ExitStack() as ctx:
        def sb(name, shape, dt=F32):
            return core.sb(f"{tag}_{name}", shape, dt, ctx)

        def sem(name):
            return core.sem(f"{tag}_{name}", ctx)

        wq, wk, wo = sb("wq", [P, P]), sb("wk", [P, P]), sb("wo", [P, P])
        wv = sb("wv", [P, 2, P])
        head_of = sb("head_of", [P, H0])
        bias_rows = sb("bias_rows", [P, D])
        load_weights(ctx, wq, wk, wv, wo, head_of, bias_rows, bias)

        x_t = sb("x_t", [P, 2, 2, P])
        x_res = sb("x_res", [P, 2, P])
        xT = sb("xT", [P, 2, P])
        qT = sb("qT", [P, 2, P])
        kT = sb("kT", [P, 2, P])
        v_blk = sb("v_blk", [P, 2, 2, P])
        k_diag = sb("k_diag", [P, 2, H0, P])
        prob = sb("prob", [P, 2, H0, S])
        probT = sb("probT", [P, 8, P])
        row_max = sb("row_max", [P, 2, H0])
        row_sum = sb("row_sum", [P, 2, H0])
        inv_sum = sb("inv_sum", [P, 2, H0])
        o_norm = sb("o_norm", [P, 2, P])
        oT = sb("oT", [P, P])
        z = sb("z", [P, 2, P])
        stats = sb("stats", [P, 2, 6])
        mean_var = sb("mean_var", [P, 2, 2])
        rstd = sb("rstd", [P, 2, 1])
        y = sb("y", [P, 2, P])

        ps_x, ps_qkv, ps_o, ps_out = core.bank[0], core.bank[1], core.bank[2], core.bank[3]
        ps_s = [core.bank[4], core.bank[5]]
        ps_t = [core.bank[6], core.bank[7]]

        x_loaded = [sem(f"x_loaded{p}") for p in range(2)]
        res_loaded = [sem(f"res_loaded{p}") for p in range(2)]
        stored = [sem(f"stored{p}") for p in range(2)]
        xt_done, xT_ready = sem("xt_done"), sem("xT_ready")
        qkv_done, qT_ready, kT_ready, v_ready = sem("qkv_done"), sem("qT_ready"), sem("kT_ready"), sem("v_ready")
        kd_ready = sem("kd_ready")
        s_done, max_done, sub_done, exp_done = sem("s_done"), sem("max_done"), sem("sub_done"), sem("exp_done")
        sum_done, inv_done = sem("sum_done"), sem("inv_done")
        t_done, pT_ready, av_done, onorm_done = sem("t_done"), sem("pT_ready"), sem("av_done"), sem("onorm_done")
        ot_done, oT_ready, out_done = sem("ot_done"), sem("oT_ready"), sem("out_done")
        z_done, stats_done, mv_done, rstd_done, y_done = (sem("z_done"), sem("stats_done"), sem("mv_done"),
                                                          sem("rstd_done"), sem("y_done"))
        veps_done = sem("veps_done")
        block = ctx.enter_context(nc.Block())

        def slots(eng, slot):
            for i in range(-1, 4):
                slot(i, i // 2, i % 2, lambda j: 0 <= j < NPAIR)
            with eng.Fori(1, NPAIR // 4 - 1) as q:
                for m in range(4):
                    slot(4 * q + m, 2 * q + m // 2, m % 2, lambda j: True)
            for i in range(NPAIR - 4, NPAIR + 3):
                slot(i, i // 2, i % 2, lambda j: 0 <= j < NPAIR)

        def here(on, i, d):
            return on(i + d if isinstance(i, int) else 0)

        @block.sync
        def _(sp):
            def load_x(i, k, par):
                wait(sp, xt_done, i - 1)
                sp.dma_start(x_t[:, par, 0, :], x_in[bass.ds(i, 1), :, :].rearrange("o p d -> p (o d)"))\
                    .then_inc(x_loaded[par], 16)
                if cross:
                    sp.dma_start(x_t[:, par, 1, :], kv_in[bass.ds(i, 1), :, :].rearrange("o p d -> p (o d)"))\
                        .then_inc(x_loaded[par], 16)

            def slot(i, k, par, on):
                if here(on, i, 2):
                    load_x(i + 2, k + 1, par)
                if here(on, i, 0):
                    wait(sp, z_done, i - 1)
                    sp.dma_start(x_res[:, par, :], x_in[bass.ds(i, 1), :, :].rearrange("o p d -> p (o d)"))\
                        .then_inc(res_loaded[par], 16)
                if here(on, i, -3):
                    wait(sp, y_done, i - 2)
                    sp.dma_start(x_out[bass.ds(i - 3, 1), :, :].rearrange("o p d -> p (o d)"), y[:, 1 - par, :])\
                        .then_inc(stored[1 - par], 16)

            load_x(0, 0, 0)
            slots(sp, slot)
            for par in range(2):
                sp.wait_ge(stored[par], 16 * (NPAIR // 2))

        @block.tensor
        def _(pe):
            def scores(i, par, c):
                wait(pe, qT_ready, i + 1)
                wait(pe, kd_ready, 2 * i + 1 + c)
                wait(pe, sub_done, 2 * i - 1 + c)
                if causal:
                    nc.tensor.matmul(ps_s[c][:, :].rearrange("p (h t) -> p h t", h=8), core.identb[:, :],
                                     core.causal[:, None, :].to_broadcast([P, 8, S]), start=True, stop=False)
                for b in range(2):
                    last = nc.tensor.matmul(
                        ps_s[c][b * S:(b + 1) * S, :].rearrange("p (h t) -> p h t", h=8),
                        qT[:, par, b * S:(b + 1) * S], k_diag[:, par, 8 * c:8 * c + 8, b * S:(b + 1) * S],
                        start=not causal, stop=True)
                last.then_inc(s_done, 1)

            def slot(i, k, par, on):
                if here(on, i, 1):
                    wait(pe, x_loaded[1 - par], (32 if cross else 16) * (k + par + 1))
                    wait(pe, xT_ready, i + 1)
                    for m in range(2 if cross else 1):
                        last = nc.tensor.transpose(ps_x[:, m * P:(m + 1) * P], x_t[:, 1 - par, m, :], core.ident[:, :])
                    last.then_inc(xt_done, 1)
                if here(on, i, 0):
                    scores(i, par, 0)
                if here(on, i, 1):
                    wait(pe, xT_ready, i + 2)
                    wait(pe, v_ready, i + 1)
                    kv = xT[:, 1 if cross else 0, :]
                    nc.tensor.matmul(ps_qkv[:, 0:P], wq[:, :], xT[:, 0, :], start=True, stop=True)
                    nc.tensor.matmul(ps_qkv[:, P:2 * P], wk[:, :], kv, start=True, stop=True)
                    for b in range(2):
                        for odd in range(2):
                            last = nc.tensor.matmul(ps_qkv[odd * S:(odd + 1) * S, (2 + b) * P:(3 + b) * P],
                                                    kv[:, b * S:(b + 1) * S], wv[:, odd, :], start=True, stop=True)
                    last.then_inc(qkv_done, 1)
                if here(on, i, 0):
                    scores(i, par, 1)
                if here(on, i, -2):
                    wait(pe, onorm_done, i - 1)
                    wait(pe, z_done, i - 2)
                    nc.tensor.transpose(ps_out[:, 0:P], o_norm[:, par, :], core.ident[:, :]).then_inc(ot_done, 1)
                if here(on, i, -1):
                    wait(pe, exp_done, 2 * i)
                    wait(pe, pT_ready, 2 * i - 2)
                    for c in range(2):
                        for hp in range(4):
                            src = prob[:, 1 - par, 8 * c + 2 * hp:8 * c + 2 * hp + 2, :].rearrange("p h t -> p (h t)")
                            last = nc.tensor.transpose(ps_t[c][:, hp * P:(hp + 1) * P], src, core.ident[:, :])
                        last.then_inc(t_done, 1)
                if here(on, i, -2):
                    wait(pe, oT_ready, i - 1)
                    nc.tensor.matmul(ps_out[:, P:2 * P], oT[:, :], wo[:, :], start=True, stop=True)\
                        .then_inc(out_done, 1)
                if here(on, i, -1):
                    wait(pe, onorm_done, i - 1)
                    wait(pe, v_ready, i)
                    for hp in range(8):
                        if hp % 4 == 0:
                            wait(pe, pT_ready, 2 * i - 1 + hp // 4)
                        for b in range(2):
                            last = nc.tensor.matmul(ps_o[b * S:(b + 1) * S, 16 * hp:16 * hp + 16],
                                                    probT[:, hp, b * S:(b + 1) * S],
                                                    v_blk[:, 1 - par, b, 16 * hp:16 * hp + 16], start=True, stop=True)
                    last.then_inc(av_done, 1)

            slots(pe, slot)

        @block.scalar
        def _(act):
            def slot(i, k, par, on):
                if here(on, i, 1):
                    wait(act, xt_done, i + 2)
                    wait(act, qkv_done, i + 1)
                    n = 2 if cross else 1
                    nc.scalar.activation(xT[:, 0:n, :].rearrange("p m t -> p (m t)"), ps_x[:, 0:n * P], ACT.Copy)\
                        .then_inc(xT_ready, 1)
                if here(on, i, -2):
                    wait(act, ot_done, i - 1)
                    wait(act, out_done, i - 2)
                    nc.scalar.activation(oT[:, :], ps_out[:, 0:P], ACT.Copy).then_inc(oT_ready, 1)
                if here(on, i, 1):
                    wait(act, qkv_done, i + 2)
                    wait(act, s_done, 2 * i)
                    nc.scalar.activation(kT[:, 1 - par, :], ps_qkv[:, P:2 * P], ACT.Copy).then_inc(kT_ready, 1)
                    nc.scalar.activation(qT[:, 1 - par, :], ps_qkv[:, 0:P], ACT.Copy, scale=float(HD0) ** -0.5)\
                        .then_inc(qT_ready, 1)
                if here(on, i, -1):
                    wait(act, av_done, i - 1)
                    for c in range(2):
                        wait(act, t_done, 2 * i - 1 + c)
                        nc.scalar.activation(probT[:, 4 * c:4 * c + 4, :].rearrange("p h e -> p (h e)"), ps_t[c][:, :],
                                             ACT.Copy).then_inc(pT_ready, 1)
                if here(on, i, 0):
                    for c in range(2):
                        wait(act, sub_done, 2 * i + 1 + c)
                        half = prob[:, par, 8 * c:8 * c + 8, :].rearrange("p h t -> p (h t)")
                        nc.scalar.activation(half, half, ACT.Exp).then_inc(exp_done, 1)
                if here(on, i, 1):
                    wait(act, av_done, i)
                    nc.scalar.activation(v_blk[:, 1 - par, :, :].rearrange("p b e -> p (b e)"), ps_qkv[:, 2 * P:4 * P],
                                         ACT.Copy).then_inc(v_ready, 1)

            slots(act, slot)

        @block.vector
        def _(dve):
            def slot(i, k, par, on):
                if here(on, i, -2):
                    wait(dve, av_done, i - 1)
                    wait(dve, inv_done, i - 1)
                    wait(dve, ot_done, i - 3)
                    nc.vector.tensor_tensor(o_norm[:, par, :].rearrange("p (h e) -> p h e", h=H0),
                                            ps_o[:, 0:P].rearrange("p (h e) -> p h e", h=H0),
                                            inv_sum[:, par, :, None].to_broadcast([P, H0, HD0]), ALU.mult)\
                        .then_inc(onorm_done, 1)
                if here(on, i, 0):
                    for c in range(2):
                        half = ps_s[c][:, :].rearrange("p (h t) -> p h t", h=8)
                        wait(dve, s_done, 2 * i + 1 + c)
                        nc.vector.tensor_reduce(row_max[:, par, 8 * c:8 * c + 8], half, AX.X, ALU.max)\
                            .then_inc(max_done, 1)
                        if c == 0:
                            wait(dve, t_done, 2 * i - 2)
                        wait(dve, max_done, 2 * i + 1 + c)
                        nc.vector.tensor_tensor(prob[:, par, 8 * c:8 * c + 8, :], half,
                                                row_max[:, par, 8 * c:8 * c + 8, None].to_broadcast([P, 8, S]),
                                                ALU.subtract).then_inc(sub_done, 1)
                if here(on, i, -1):
                    wait(dve, exp_done, 2 * i)
                    nc.vector.tensor_reduce(row_sum[:, 1 - par, :], prob[:, 1 - par, :, :], AX.X, ALU.add)\
                        .then_inc(sum_done, 1)
                    wait(dve, sum_done, i)
                    nc.vector.reciprocal(inv_sum[:, 1 - par, :], row_sum[:, 1 - par, :]).then_inc(inv_done, 1)
                if here(on, i, -2):
                    wait(dve, res_loaded[par], 16 * k)
                    nc.vector.tensor_tensor(z[:, par, :], x_res[:, par, :], bias_rows[:, :], ALU.add)\
                        .then_inc(veps_done, 1)
                    wait(dve, out_done, i - 1)
                    wait(dve, veps_done, 2 * i - 3)
                    nc.vector.tensor_tensor(z[:, par, :], z[:, par, :], ps_out[:, P:2 * P], ALU.add).then_inc(z_done, 1)
                    wait(dve, z_done, i - 1)
                    nc.vector.bn_stats(stats[:, par, :], z[:, par, :]).then_inc(stats_done, 1)
                    wait(dve, stats_done, i - 1)
                if here(on, i, -3):
                    wait(dve, rstd_done, i - 2)
                    wait(dve, stored[1 - par], 16 * (k - 2 + par))
                    nc.vector.tensor_scalar(y[:, 1 - par, :], z[:, 1 - par, :], mean_var[:, 1 - par, 0:1],
                                            rstd[:, 1 - par, :], ALU.subtract, ALU.mult).then_inc(y_done, 1)
                if here(on, i, -2):
                    nc.vector.bn_aggr(mean_var[:, par, :], stats[:, par, :]).then_inc(mv_done, 1)
                    wait(dve, mv_done, i - 1)
                    nc.vector.tensor_scalar(rstd[:, par, :], mean_var[:, par, 1:2], EPS, None, ALU.add)\
                        .then_inc(veps_done, 1)

            slots(dve, slot)

        @block.gpsimd
        def _(pool):
            def slot(i, k, par, on):
                if here(on, i, 1):
                    wait(pool, kT_ready, i + 2)
                    for c in range(2):
                        wait(pool, s_done, 2 * i - 1 + c)
                        heads = slice(8 * c, 8 * c + 8)
                        nc.gpsimd.tensor_tensor(k_diag[:, 1 - par, heads, :],
                                                kT[:, 1 - par, None, :].to_broadcast([P, 8, P]),
                                                head_of[:, heads, None].to_broadcast([P, 8, P]), ALU.mult)\
                            .then_inc(kd_ready, 1)
                if here(on, i, -2):
                    wait(pool, veps_done, 2 * i - 2)
                    nc.gpsimd.tensor_tensor(rstd[:, par, :], rstd[:, par, :], core.eps_pow[:, :], ALU.pow)\
                        .then_inc(rstd_done, 1)

            slots(pool, slot)


def low_head_weights(nc, core, tag, w_q, w_k, w_v, w_o, transposed):

    def load(ctx, wq, wk, wv, wo, head_of, bias_rows, bias):
        with ExitStack() as own:
            raw = core.sb(f"{tag}_raw", [P, 4, P], F32, own)
            loaded = core.sem(f"{tag}_w_loaded", own)
            flat_done = core.sem(f"{tag}_w_flat", own)
            copied = core.sem(f"{tag}_w_copied", own)
            head_done = core.sem(f"{tag}_head_done", own)
            block = own.enter_context(nc.Block())

            @block.sync
            def _(sp):
                for n, w in enumerate((w_q, w_k, w_v, w_o)):
                    sp.dma_start(raw[:, n, :], w).then_inc(loaded, 16)
                sp.dma_start(bias_rows[:, :], bcast_rows(bias)).then_inc(loaded, 16)
                sp.wait_ge(loaded, 80)

            @block.tensor
            def _(pe):
                if transposed:
                    pe.wait_ge(loaded, 80)
                    for n in range(4):
                        last = nc.tensor.transpose(core.bank[0][:, n * P:(n + 1) * P], raw[:, n, :], core.ident[:, :])
                    last.then_inc(flat_done, 1)

            @block.vector
            def _(dve):
                nc.vector.memset(wv[:, :, :], 0.0).then_inc(copied, 1)
                nc.vector.memset(head_of[:, :], 1.0).then_inc(head_done, 1)
                dve.wait_ge(loaded, 80)
                dve.wait_ge(copied, 1)
                if transposed:
                    dve.wait_ge(flat_done, 1)
                src = [core.bank[0][:, n * P:(n + 1) * P] if transposed else raw[:, n, :] for n in range(4)]
                for dst, n in ((wq, 0), (wk, 1), (wo, 3)):
                    nc.vector.tensor_copy(dst[:, :], src[n]).then_inc(copied, 1)
                for odd in range(2):
                    nc.vector.tensor_copy(
                        wv[:, odd, :].rearrange("p (g o e) -> p g o e", o=2, e=HD0)[:, :, odd, :],
                        src[2].rearrange("p (g o e) -> p g o e", o=2, e=HD0)[:, :, odd, :]).then_inc(copied, 1)

            @block.gpsimd
            def _(pool):
                pool.wait_ge(head_done, 1)
                nc.gpsimd.affine_select(out=head_of[:, :], in_=head_of[:, :], compare_op=ALU.is_ge, fill=0.0,
                                        base=0, pattern=[[-HD0, H0]], channel_multiplier=1).then_inc(head_done, 1)
                pool.wait_ge(head_done, 2)
                nc.gpsimd.affine_select(out=head_of[:, :], in_=head_of[:, :], compare_op=ALU.is_ge, fill=0.0,
                                        base=HD0 - 1, pattern=[[HD0, H0]], channel_multiplier=-1)\
                    .then_inc(head_done, 1)

    return load


def feed_forward_phase(core, x_in, x_out, w_fc, w_proj, u, v, fast_b, gate):
    nc = core.nc
    NT = FF // P
    GP = 2
    NG = NPAIR // GP
    R = u.shape[1]
    with ExitStack() as ctx:
        def sb(name, shape, dt=F32):
            return core.sb(f"ffn_{name}", shape, dt, ctx)

        def sem(name):
            return core.sem(f"ffn_{name}", ctx)

        w_hidden, w_out = sb("w_hidden", [P, FF]), sb("w_out", [P, NT, P])

        with ExitStack() as own:
            def osb(name, shape):
                return core.sb(f"ffnw_{name}", shape, F32, own)

            w, sc = osb("w", [P, 2 * NT, P]), osb("sc", [P, 2 * NT])
            thr, nthr = osb("thr", [P, 2 * NT]), osb("nthr", [P, 2 * NT])
            above, below = osb("above", [P, 2 * NT, P]), osb("below", [P, 2 * NT, P])
            proj_sum, gate_sb = osb("proj_sum", [P, 1]), osb("gate", [P, 1])
            u_sb, v_sb, fb_sb = osb("u", [P, NT, R]), osb("v", [R, D]), osb("fb", [R, R])
            uT, fbT, m_sb = osb("uT", [R, FF]), osb("fbT", [R, R]), osb("m", [R, D])
            loaded, lr_loaded = core.sem("ffnw_loaded", own), core.sem("ffnw_lr_loaded", own)
            q = core.sem("ffnw_quant", own)
            ut_done, m_done, lr_done, wt_done = (core.sem("ffnw_ut_done", own), core.sem("ffnw_m_done", own),
                                                 core.sem("ffnw_lr_done", own), core.sem("ffnw_wt_done", own))
            copied, w_ready = core.sem("ffnw_copied", own), core.sem("ffnw_ready", own)
            block = own.enter_context(nc.Block())

            @block.sync
            def _(sp):
                sp.dma_start(w[:, 0:NT, :], w_fc.rearrange("(t p) d -> p t d", p=P)).then_inc(loaded, 16)
                sp.dma_start(w[:, NT:2 * NT, :].rearrange("p t d -> p (t d)"), w_proj).then_inc(loaded, 16)
                sp.dma_start(u_sb[:, :, :], u.rearrange("(t p) r -> p t r", p=P)).then_inc(lr_loaded, 16)
                sp.dma_start(v_sb[:, :], v).then_inc(lr_loaded, 16)
                sp.dma_start(fb_sb[:, :], fast_b).then_inc(lr_loaded, 16)
                sp.dma_start(gate_sb[:, :], bcast_rows(gate)).then_inc(lr_loaded, 16)
                sp.wait_ge(lr_loaded, 64)

            @block.vector
            def _(dve):
                count = [0]

                def step(ins):
                    ins.then_inc(q, 1)
                    count[0] += 1
                    dve.wait_ge(q, count[0])

                wide = [P, 2 * NT, P]
                dve.wait_ge(loaded, 32)
                step(nc.vector.tensor_reduce(sc[:, :], w[:, :, :], AX.X, ALU.add, apply_absolute_value=True))
                step(nc.vector.tensor_reduce(proj_sum[:, :], sc[:, NT:2 * NT], AX.X, ALU.add))
                step(nc.vector.tensor_scalar(sc[:, 0:NT], sc[:, 0:NT], 1.0 / D, 1e-5, ALU.mult, ALU.max))
                step(nc.vector.tensor_scalar(sc[:, NT:2 * NT], proj_sum[:, :].to_broadcast([P, NT]), 1.0 / FF, 1e-5,
                                             ALU.mult, ALU.max))
                step(nc.vector.tensor_scalar(thr[:, :], sc[:, :], 0.5, None, ALU.mult))
                step(nc.vector.tensor_scalar(nthr[:, :], sc[:, :], -0.5, None, ALU.mult))
                step(nc.vector.tensor_tensor(above[:, :, :], w[:, :, :], thr[:, :, None].to_broadcast(wide), ALU.is_gt))
                step(nc.vector.tensor_tensor(below[:, :, :], w[:, :, :], nthr[:, :, None].to_broadcast(wide), ALU.is_lt))
                step(nc.vector.tensor_tensor(above[:, :, :], above[:, :, :], below[:, :, :], ALU.subtract))
                step(nc.vector.tensor_tensor(below[:, :, :], above[:, :, :], w[:, :, :], ALU.subtract))
                step(nc.vector.tensor_tensor(above[:, :, :], w[:, :, :], below[:, :, :], ALU.add))
                step(nc.vector.tensor_tensor(w[:, :, :], above[:, :, :], sc[:, :, None].to_broadcast(wide), ALU.mult))
                dve.wait_ge(copied, 5)
                dve.wait_ge(lr_done, 1)
                dve.wait_ge(lr_loaded, 64)
                nc.vector.scalar_tensor_tensor(out=w_hidden[:, :], in0=core.bank[3][:, :], scalar=gate_sb[:, :],
                                               in1=above[:, 0:NT, :].rearrange("p t d -> p (t d)"), op0=ALU.mult,
                                               op1=ALU.add).then_inc(w_ready, 1)

            @block.tensor
            def _(pe):
                pe.wait_ge(lr_loaded, 64)
                for t in range(NT):
                    nc.tensor.transpose(core.bank[0][0:R, t * P:(t + 1) * P], u_sb[:, t, :], core.ident[:, :])
                nc.tensor.transpose(core.bank[1][0:R, 0:R], fb_sb[:, :], core.ident[0:R, 0:R]).then_inc(ut_done, 1)
                pe.wait_ge(copied, 2)
                nc.tensor.matmul(core.bank[2][0:R, 0:D], fbT[:, :], v_sb[:, :], start=True, stop=True).then_inc(m_done, 1)
                pe.wait_ge(copied, 3)
                nc.tensor.matmul(core.bank[3][:, :], m_sb[:, :], uT[:, :], start=True, stop=True).then_inc(lr_done, 1)
                pe.wait_ge(q, 12)
                for t in range(2 * NT):
                    last = nc.tensor.transpose(core.bank[4 + t // NT][:, t % NT * P:(t % NT + 1) * P], w[:, t, :],
                                               core.ident[:, :])
                last.then_inc(wt_done, 1)

            @block.scalar
            def _(act):
                act.wait_ge(ut_done, 1)
                nc.scalar.activation(uT[:, :], core.bank[0][0:R, :], ACT.Copy).then_inc(copied, 1)
                nc.scalar.activation(fbT[:, :], core.bank[1][0:R, 0:R], ACT.Copy).then_inc(copied, 1)
                act.wait_ge(m_done, 1)
                nc.scalar.activation(m_sb[:, :], core.bank[2][0:R, 0:D], ACT.Copy).then_inc(copied, 1)
                act.wait_ge(wt_done, 1)
                nc.scalar.activation(above[:, 0:NT, :].rearrange("p t d -> p (t d)"), core.bank[4][:, :], ACT.Copy)\
                    .then_inc(copied, 1)
                nc.scalar.activation(w_out[:, :, :].rearrange("p t d -> p (t d)"), core.bank[5][:, :], ACT.Copy)\
                    .then_inc(copied, 1)

        x = sb("x", [P, 4, GP, P])
        xT = sb("xT", [P, 2, GP * P])
        r = sb("r", [P, 2, NT, GP * P])
        r2 = sb("r2", [P, 2, NT, GP * P])
        z = sb("z", [P, 2, GP, P])
        stats = sb("stats", [P, GP, 6])
        mean_var = sb("mean_var", [P, 2, GP, 2])
        rstd = sb("rstd", [P, 2, GP])
        y = sb("y", [P, 2, GP, P])
        ps_x, ps_out = core.bank[0], core.bank[1]
        ps_h = [core.bank[2], core.bank[3], core.bank[4], core.bank[5]]
        x_loaded = [sem(f"x_loaded{p}") for p in range(4)]
        stored = [sem(f"stored{p}") for p in range(2)]
        xt_done, xT_ready, h_done, relu_done, sq_done, out_done = (sem("xt_done"), sem("xT_ready"), sem("h_done"),
                                                                   sem("relu_done"), sem("sq_done"), sem("out_done"))
        z_done, stats_done, mv_done, veps_done, rstd_done, y_done = (
            sem("z_done"), sem("stats_done"), sem("mv_done"), sem("veps_done"), sem("rstd_done"), sem("y_done"))
        block = ctx.enter_context(nc.Block())

        def slots(eng, slot):
            for g in range(-1, 4):
                slot(g, g // 4, g % 4, lambda j: 0 <= j < NG)
            with eng.Fori(1, NG // 4 - 1) as k:
                for m in range(4):
                    slot(4 * k + m, k, m, lambda j: True)
            for g in range(NG - 4, NG + 2):
                slot(g, g // 4, g % 4, lambda j: 0 <= j < NG)

        def here(on, g, d):
            return on(g + d if isinstance(g, int) else 0)

        @block.sync
        def _(sp):
            def load(g, m):
                wait(sp, z_done, g - 3)
                sp.dma_start(x[:, m, :, :], x_in[bass.ds(GP * g, GP), :, :].rearrange("n p d -> p n d"))\
                    .then_inc(x_loaded[m], 16)

            def slot(g, k, m, on):
                if here(on, g, 2):
                    load(g + 2, (m + 2) % 4)
                if here(on, g, -2):
                    wait(sp, y_done, g - 1)
                    sp.dma_start(x_out[bass.ds(GP * (g - 2), GP), :, :].rearrange("n p d -> p n d"),
                                 y[:, m % 2, :, :]).then_inc(stored[m % 2], 16)

            load(0, 0)
            slots(sp, slot)
            for par in range(2):
                sp.wait_ge(stored[par], 16 * (NG // 2))

        @block.tensor
        def _(pe):
            def slot(g, k, m, on):
                if here(on, g, 1):
                    wait(pe, x_loaded[(m + 1) % 4], 16 * (k + 1 + (m + 1) // 4))
                    wait(pe, xT_ready, g + 1)
                    for n in range(GP):
                        last = nc.tensor.transpose(ps_x[:, n * P:(n + 1) * P], x[:, (m + 1) % 4, n, :], core.ident[:, :])
                    last.then_inc(xt_done, 1)
                if here(on, g, 0):
                    wait(pe, xT_ready, g + 1)
                    for t in range(NT):
                        wait(pe, relu_done, NT * (g - 1) + t + 1)
                        nc.tensor.matmul(ps_h[t][:, 0:GP * P], w_hidden[:, t * P:(t + 1) * P], xT[:, m % 2, :],
                                         start=True, stop=True).then_inc(h_done, 1)
                if here(on, g, -1):
                    wait(pe, sq_done, NT * g)
                    wait(pe, z_done, g - 1)
                    for n in range(GP):
                        for t in range(NT):
                            last = nc.tensor.matmul(ps_out[:, n * P:(n + 1) * P], r2[:, (m + 1) % 2, t, n * P:(n + 1) * P],
                                                    w_out[:, t, :], start=(t == 0), stop=(t == NT - 1))
                    last.then_inc(out_done, 1)

            slots(pe, slot)

        @block.scalar
        def _(act):
            def slot(g, k, m, on):
                if here(on, g, 1):
                    wait(act, xt_done, g + 2)
                    wait(act, h_done, NT * g)
                    nc.scalar.activation(xT[:, (m + 1) % 2, :], ps_x[:, 0:GP * P], ACT.Copy).then_inc(xT_ready, 1)
                if here(on, g, 0):
                    wait(act, sq_done, NT * (g - 1))
                    for t in range(NT):
                        wait(act, h_done, NT * g + t + 1)
                        nc.scalar.activation(r[:, m % 2, t, :], ps_h[t][:, 0:GP * P], ACT.Relu).then_inc(relu_done, 1)

            slots(act, slot)

        @block.vector
        def _(dve):
            def slot(g, k, m, on):
                if here(on, g, 0):
                    wait(dve, out_done, g - 1)
                    for t in range(NT):
                        wait(dve, relu_done, NT * g + t + 1)
                        nc.vector.tensor_tensor(r2[:, m % 2, t, :], r[:, m % 2, t, :], r[:, m % 2, t, :], ALU.mult)\
                            .then_inc(sq_done, 1)
                if here(on, g, -1):
                    o = (m + 1) % 2
                    wait(dve, out_done, g)
                    nc.vector.tensor_tensor(z[:, o, :, :], x[:, (m + 3) % 4, :, :],
                                            ps_out[:, 0:GP * P].rearrange("p (n d) -> p n d", n=GP), ALU.add)\
                        .then_inc(z_done, 1)
                    wait(dve, z_done, g)
                    for n in range(GP):
                        last = nc.vector.bn_stats(stats[:, n, :], z[:, o, n, :])
                    last.then_inc(stats_done, 1)
                    wait(dve, stats_done, g)
                if here(on, g, -2):
                    wait(dve, rstd_done, g - 1)
                    wait(dve, stored[m % 2], 16 * (2 * k + m // 2 - 1))
                    for n in range(GP):
                        last = nc.vector.tensor_scalar(y[:, m % 2, n, :], z[:, m % 2, n, :], mean_var[:, m % 2, n, 0:1],
                                                       rstd[:, m % 2, n:n + 1], ALU.subtract, ALU.mult)
                    last.then_inc(y_done, 1)
                if here(on, g, -1):
                    for n in range(GP):
                        last = nc.vector.bn_aggr(mean_var[:, o, n, :], stats[:, n, :])
                    last.then_inc(mv_done, 1)
                    wait(dve, mv_done, g)
                    nc.vector.tensor_scalar(rstd[:, o, :], mean_var[:, o, :, 1], EPS, None, ALU.add)\
                        .then_inc(veps_done, 1)

            slots(dve, slot)

        @block.gpsimd
        def _(pool):
            def slot(g, k, m, on):
                if here(on, g, -1):
                    wait(pool, veps_done, g)
                    nc.gpsimd.tensor_tensor(rstd[:, (m + 1) % 2, :], rstd[:, (m + 1) % 2, :],
                                            core.eps_pow[:, :].to_broadcast([P, GP]), ALU.pow).then_inc(rstd_done, 1)

            slots(pool, slot)


def head_product_weights(core, tag, pairs_of_heads, w_q, w_k, w_v, w_o, scores_first, w_score, w_vo, lam=None):
    nc = core.nc
    NT = pairs_of_heads
    NQ = NT // 4
    with ExitStack() as own:
        def sb(name, shape):
            return core.sb(f"{tag}w_{name}", shape, F32, own)

        def sem(name):
            return core.sem(f"{tag}w_{name}", own)

        raw, flat = sb("raw", [P, 3, NT, P]), sb("flat", [P, 3, NT, P])
        wo = sb("wo", [P, H1 // 2, D])
        loaded, wo_loaded = [sem(f"loaded{n}") for n in range(3)], sem("wo_loaded")
        t_done, t_copied, prod_done, prod_copied = sem("t_done"), sem("t_copied"), sem("prod_done"), sem("prod_copied")
        if lam is not None:
            lam_in, lam_prod = sb("lam_in", [P, 4, HD1]), sb("lam_prod", [P, 2, HD1])
            lam_dot, lam_exp, vo_scale = sb("lam_dot", [P, 2]), sb("lam_exp", [P, 2]), sb("vo_scale", [P, 1])
            lam_loaded, lam_dot_done, lam_exp_done, lam_done = (sem("lam_loaded"), sem("lam_dot_done"),
                                                                sem("lam_exp_done"), sem("lam_done"))
        block = own.enter_context(nc.Block())
        prods = [("score", q, par) for q in range(NQ) for par in range(2)]
        prods += [("vo", q, par) for q in range(NQ) for par in range(2)]

        @block.sync
        def _(sp):
            for n, w in enumerate((w_q, w_k, w_v)):
                sp.dma_start(raw[:, n, :, :].rearrange("p t d -> p (t d)"), w).then_inc(loaded[n], 16)
            sp.dma_start(wo[:, :, :], w_o.rearrange("(t p) d -> p t d", p=P)).then_inc(wo_loaded, 16)
            if lam is not None:
                for n, v in enumerate(lam):
                    sp.dma_start(lam_in[:, n, :], bcast_rows(v)).then_inc(lam_loaded, 16)
                sp.wait_ge(lam_loaded, 64)

        @block.tensor
        def _(pe):
            for n in range(3):
                pe.wait_ge(loaded[n], 16)
                for q in range(NQ):
                    m = n * NQ + q
                    wait(pe, t_copied, m - 3)
                    for t in range(4):
                        last = nc.tensor.transpose(core.bank[m % 4][:, t * P:(t + 1) * P], raw[:, n, 4 * q + t, :],
                                                   core.ident[:, :])
                    last.then_inc(t_done, 1)
            pe.wait_ge(t_copied, 3 * NQ)
            pe.wait_ge(wo_loaded, 16)
            for m, (kind, q, par) in enumerate(prods):
                wait(pe, prod_copied, m - 3)
                rows = slice(par * HD1, (par + 1) * HD1)
                for t in range(4):
                    hp = 4 * q + t
                    if kind == "vo":
                        left, right = flat[rows, 2, hp, :], wo[rows, hp % (H1 // 2), :]
                    elif scores_first == "k":
                        left, right = flat[rows, 1, hp, :], flat[rows, 0, hp, :]
                    else:
                        left, right = flat[rows, 0, hp, :], flat[rows, 1, hp, :]
                    last = nc.tensor.matmul(core.bank[4 + m % 4][:, t * P:(t + 1) * P], left, right, start=True,
                                            stop=True)
                last.then_inc(prod_done, 1)

        @block.scalar
        def _(act):
            if lam is not None:
                act.wait_ge(lam_dot_done, 1)
                nc.scalar.activation(lam_exp[:, :], lam_dot[:, :], ACT.Exp).then_inc(lam_exp_done, 1)
            for m in range(3 * NQ):
                act.wait_ge(t_done, m + 1)
                nc.scalar.activation(flat[:, m // NQ, m % NQ * 4:m % NQ * 4 + 4, :].rearrange("p t d -> p (t d)"),
                                     core.bank[m % 4][:, :], ACT.Copy).then_inc(t_copied, 1)

        @block.vector
        def _(dve):
            if lam is not None:
                dve.wait_ge(lam_loaded, 64)
                nc.vector.tensor_tensor(lam_prod[:, :, :], lam_in[:, 0:2, :], lam_in[:, 2:4, :], ALU.mult)\
                    .then_inc(lam_done, 1)
                dve.wait_ge(lam_done, 1)
                nc.vector.tensor_reduce(lam_dot[:, :], lam_prod[:, :, :], AX.X, ALU.add).then_inc(lam_dot_done, 1)
                dve.wait_ge(lam_exp_done, 1)
                nc.vector.tensor_tensor(vo_scale[:, :], lam_exp[:, 0:1], lam_exp[:, 1:2], ALU.subtract)\
                    .then_inc(lam_done, 1)
                dve.wait_ge(lam_done, 2)
                nc.vector.tensor_scalar(vo_scale[:, :], vo_scale[:, :], 0.8, -(1.0 - 0.8), ALU.add, ALU.mult)\
                    .then_inc(lam_done, 1)
                dve.wait_ge(lam_done, 3)
            for m, (kind, q, par) in enumerate(prods):
                dve.wait_ge(prod_done, m + 1)
                src = core.bank[4 + m % 4][:, :].rearrange("p (t d) -> p t d", t=4)
                if kind == "score":
                    dst = w_score[:, :, :].rearrange("p (t o) d -> p t o d", o=2)[:, 4 * q:4 * q + 4, par, :]
                    by = float(HD1) ** -0.5
                else:
                    dst = w_vo[:, par, 4 * q:4 * q + 4, :]
                    by = 1.0 if lam is None else (1.0 - 0.8 if q < NQ // 2 else vo_scale[:, :])
                nc.vector.tensor_scalar(dst, src, by, None, ALU.mult).then_inc(prod_copied, 1)


def differential_attention_phase(core, x_in, x_out, cat_out, ctx_in, a):
    nc = core.nc
    NH = 2 * H1
    with ExitStack() as ctx:
        def sb(name, shape, dt=F32):
            return core.sb(f"diff_{name}", shape, dt, ctx)

        def sem(name):
            return core.sem(f"diff_{name}", ctx)

        w_score, w_vo = sb("w_score", [P, NH, D]), sb("w_vo", [P, 2, NH // 2, D])
        head_product_weights(core, "diff", NH // 2, a["L1_attn_Wq"], a["L1_attn_Wk"], a["L1_attn_Wv"],
                             a["L1_attn_Wo"], "k", w_score, w_vo,
                             [a["L1_attn_lq1"], a["L1_attn_lq2"], a["L1_attn_lk1"], a["L1_attn_lk2"]])

        gb = sb("gb", [P, 4, D])
        x_t, x_res, ctx_t = sb("x_t", [P, D]), sb("x_res", [P, D]), sb("ctx_t", [P, D])
        xT = sb("xT", [P, P])
        keys = sb("keys", [P, 2, 8, P])
        vals = sb("vals", [P, 4, 2, 4, D])
        prob = sb("prob", [P, 2, 8, S])
        probT = sb("probT", [P, 4, P])
        row_max, row_sum, inv_sum = sb("row_max", [P, 2, 8]), sb("row_sum", [P, 2, 8]), sb("inv_sum", [P, 2, 8])
        z, y, lat, ctx_n = sb("z", [P, D]), sb("y", [P, D]), sb("lat", [P, D]), sb("ctx_n", [P, D])
        stats, mean_var, rstd = sb("stats", [P, 3, 6]), sb("mean_var", [P, 3, 2]), sb("rstd", [P, 3])

        ps_g, ps_v = [core.bank[0], core.bank[1]], [core.bank[2], core.bank[3]]
        ps_s, ps_t, ps_o, ps_x = core.bank[4], core.bank[5], core.bank[6], core.bank[7]

        gb_loaded, x_loaded, res_loaded, ctx_loaded = (sem("gb_loaded"), sem("x_loaded"), sem("res_loaded"),
                                                       sem("ctx_loaded"))
        y_stored, lat_stored, ctx_stored = sem("y_stored"), sem("lat_stored"), sem("ctx_stored")
        xt_done, xT_ready = sem("xt_done"), sem("xT_ready")
        g_done, g_copied, v_done, v_copied = sem("g_done"), sem("g_copied"), sem("v_done"), sem("v_copied")
        s_done, max_done, sub_done, exp_done = sem("s_done"), sem("max_done"), sem("sub_done"), sem("exp_done")
        sum_done, inv_done, p_done = sem("sum_done"), sem("inv_done"), sem("p_done")
        t_done, pT_copied, av_done = sem("t_done"), sem("pT_copied"), sem("av_done")
        z_done, y_done, lat_n_done, lat_g_done, lat_done = (sem("z_done"), sem("y_done"), sem("lat_n_done"),
                                                            sem("lat_g_done"), sem("lat_done"))
        ctx_n_done, ctx_g_done, ctx_done = sem("ctx_n_done"), sem("ctx_g_done"), sem("ctx_done")
        st_done = [sem(f"st_done{n}") for n in range(3)]
        mv_done = [sem(f"mv_done{n}") for n in range(3)]
        veps_done = [sem(f"veps_done{n}") for n in range(3)]
        rstd_done = [sem(f"rstd_done{n}") for n in range(3)]
        block = ctx.enter_context(nc.Block())

        def slots(eng, slot):
            for c in range(4):
                slot(0, c, True, False)
            with eng.Fori(1, NPAIR - 1) as i:
                for c in range(4):
                    slot(i, c, True, True)
            for c in range(4):
                slot(NPAIR - 1, c, True, True)
            for c in range(4):
                slot(NPAIR, c, False, True)

        def have(n, cur, prev):
            return cur and prev if not isinstance(n, int) else 0 <= n < 4 * NPAIR

        def last_pair(i):
            return isinstance(i, int) and i == NPAIR - 1

        def rows(t, i):
            return t[bass.ds(i, 1), :, :].rearrange("o p d -> p (o d)")

        @block.sync
        def _(sp):
            def store_cat(i, at, tile, sem_):
                for b in range(2):
                    sp.dma_start(cat_out[bass.ds(2 * i + b, 1), at:at + S, :].rearrange("o p d -> p (o d)"),
                                 tile[b * S:(b + 1) * S, :]).then_inc(sem_, 16)

            def pair(i, cur, prev):
                if cur and not last_pair(i):
                    sp.wait_ge(xt_done, i + 1)
                    sp.dma_start(x_t[:, :], rows(x_in, i + 1)).then_inc(x_loaded, 16)
                if cur:
                    wait(sp, z_done, i)
                    sp.dma_start(x_res[:, :], rows(x_in, i)).then_inc(res_loaded, 16)
                    sp.wait_ge(ctx_done, i + 1)
                    store_cat(i, 0, ctx_n, ctx_stored)
                    if not last_pair(i):
                        sp.dma_start(ctx_t[:, :], rows(ctx_in, i + 1)).then_inc(ctx_loaded, 16)
                if prev:
                    sp.wait_ge(y_done, i)
                    sp.dma_start(rows(x_out, i - 1), y[:, :]).then_inc(y_stored, 16)
                    sp.wait_ge(lat_done, i)
                    store_cat(i - 1, S, lat, lat_stored)

            sp.dma_start(x_t[:, :], rows(x_in, 0)).then_inc(x_loaded, 16)
            sp.dma_start(ctx_t[:, :], rows(ctx_in, 0)).then_inc(ctx_loaded, 16)
            for n, name in enumerate(("L1_xattn_g1", "L1_xattn_b1", "L1_xattn_g2", "L1_xattn_b2")):
                sp.dma_start(gb[:, n, :], bcast_rows(a[name])).then_inc(gb_loaded, 16)
            pair(0, True, False)
            with sp.Fori(1, NPAIR - 1) as i:
                pair(i, True, True)
            pair(NPAIR - 1, True, True)
            pair(NPAIR, False, True)
            sp.wait_ge(y_stored, 16 * NPAIR)
            sp.wait_ge(lat_stored, 32 * NPAIR)
            sp.wait_ge(ctx_stored, 32 * NPAIR)

        @block.tensor
        def _(pe):
            def transpose_x(i):
                pe.wait_ge(x_loaded, 16 * (i + 1))
                wait(pe, xT_ready, i)
                nc.tensor.transpose(ps_x[:, 0:P], x_t[:, :], core.ident[:, :]).then_inc(xt_done, 1)

            def slot(i, c, cur, prev):
                n = 4 * i + c
                back = have(n - 2, cur, prev)
                if cur:
                    if c == 3 and not last_pair(i):
                        transpose_x(i + 1)
                    if c == 0:
                        pe.wait_ge(xT_ready, i + 1)
                    for g in range(2):
                        wait(pe, g_copied, 2 * n - 1 + g)
                        for j in range(4):
                            last = nc.tensor.matmul(ps_g[g][:, j * P:(j + 1) * P], w_score[:, 8 * c + 4 * g + j, :],
                                                    xT[:, :], start=True, stop=True)
                        last.then_inc(g_done, 1)
                if back:
                    wait(pe, p_done, n - 1)
                    wait(pe, pT_copied, n - 2)
                    for hp in range(4):
                        src = prob[:, c % 2, 2 * hp:2 * hp + 2, :].rearrange("p h t -> p (h t)")
                        last = nc.tensor.transpose(ps_t[:, hp * P:(hp + 1) * P], src, core.ident[:, :])
                    last.then_inc(t_done, 1)
                if cur:
                    for b in range(2):
                        wait(pe, v_copied, 2 * n - 1 + b)
                        for par in range(2):
                            last = nc.tensor.matmul(ps_v[b][par * S:(par + 1) * S, :], xT[:, b * S:(b + 1) * S],
                                                    w_vo[:, par, 4 * c:4 * c + 4, :].rearrange("p h d -> p (h d)"),
                                                    start=True, stop=True)
                        last.then_inc(v_done, 1)
                    pe.wait_ge(g_copied, 2 * n + 2)
                    wait(pe, sub_done, n)
                    nc.tensor.matmul(ps_s[:, :].rearrange("p (h t) -> p h t", h=8), core.identb[:, :],
                                     core.causal[:, None, :].to_broadcast([P, 8, S]), start=True, stop=False)
                    for b in range(2):
                        last = nc.tensor.matmul(ps_s[b * S:(b + 1) * S, :].rearrange("p (h t) -> p h t", h=8),
                                                xT[:, b * S:(b + 1) * S], keys[:, c % 2, :, b * S:(b + 1) * S],
                                                start=False, stop=True)
                    last.then_inc(s_done, 1)
                if back:
                    wait(pe, pT_copied, n - 1)
                    wait(pe, v_copied, 2 * n - 2)
                    if c == 2:
                        wait(pe, z_done, i)
                    for hp in range(4):
                        for b in range(2):
                            last = nc.tensor.matmul(ps_o[b * S:(b + 1) * S, 0:D], probT[:, hp, b * S:(b + 1) * S],
                                                    vals[:, (c + 2) % 4, b, hp, :], start=(c == 2 and hp == 0),
                                                    stop=(c == 1 and hp == 3))
                    last.then_inc(av_done, 1)

            transpose_x(0)
            slots(pe, slot)

        @block.scalar
        def _(act):
            def copy_xT(i):
                act.wait_ge(xt_done, i + 1)
                wait(act, s_done, 4 * i)
                nc.scalar.activation(xT[:, :], ps_x[:, 0:P], ACT.Copy).then_inc(xT_ready, 1)

            def slot(i, c, cur, prev):
                n = 4 * i + c
                if cur:
                    wait(act, s_done, n - 1)
                    for g in range(2):
                        act.wait_ge(g_done, 2 * n + 1 + g)
                        nc.scalar.activation(keys[:, c % 2, 4 * g:4 * g + 4, :].rearrange("p h t -> p (h t)"),
                                             ps_g[g][:, :], ACT.Copy).then_inc(g_copied, 1)
                if have(n - 1, cur, prev):
                    wait(act, sub_done, n)
                    flat = prob[:, (c + 1) % 2, :, :].rearrange("p h t -> p (h t)")
                    nc.scalar.activation(flat, flat, ACT.Exp).then_inc(exp_done, 1)
                if have(n - 2, cur, prev):
                    wait(act, t_done, n - 1)
                    wait(act, av_done, n - 2)
                    nc.scalar.activation(probT[:, :, :].rearrange("p h t -> p (h t)"), ps_t[:, :], ACT.Copy)\
                        .then_inc(pT_copied, 1)
                if cur:
                    wait(act, av_done, n - 3)
                    for b in range(2):
                        act.wait_ge(v_done, 2 * n + 1 + b)
                        nc.scalar.activation(vals[:, c, b, :, :].rearrange("p h d -> p (h d)"), ps_v[b][:, :],
                                             ACT.Copy).then_inc(v_copied, 1)
                if cur and c == 3 and not last_pair(i):
                    copy_xT(i + 1)

            copy_xT(0)
            slots(act, slot)

        @block.vector
        def _(dve):
            def bn_tail(m, count):
                nc.vector.bn_aggr(mean_var[:, m, :], stats[:, m, :]).then_inc(mv_done[m], 1)
                dve.wait_ge(mv_done[m], count)
                nc.vector.tensor_scalar(rstd[:, m:m + 1], mean_var[:, m, 1:2], EPS, None, ALU.add)\
                    .then_inc(veps_done[m], 1)

            def slot(i, c, cur, prev):
                n = 4 * i + c
                if c == 0 and cur:
                    dve.wait_ge(ctx_loaded, 16 * (i + 1))
                    nc.vector.bn_stats(stats[:, 2, :], ctx_t[:, :]).then_inc(st_done[2], 1)
                    dve.wait_ge(st_done[2], i + 1)
                if c == 2 and prev:
                    dve.wait_ge(st_done[0], i)
                if c == 3 and prev:
                    dve.wait_ge(rstd_done[0], i)
                    wait(dve, y_stored, 16 * (i - 1))
                    nc.vector.tensor_scalar(y[:, :], z[:, :], mean_var[:, 0, 0:1], rstd[:, 0:1], ALU.subtract,
                                            ALU.mult).then_inc(y_done, 1)
                    dve.wait_ge(y_done, i)
                    nc.vector.bn_stats(stats[:, 1, :], y[:, :]).then_inc(st_done[1], 1)
                    dve.wait_ge(st_done[1], i)
                if have(n - 1, cur, prev):
                    wait(dve, exp_done, n)
                    nc.vector.tensor_reduce(row_sum[:, (c + 1) % 2, :], prob[:, (c + 1) % 2, :, :], AX.X, ALU.add)\
                        .then_inc(sum_done, 1)
                    wait(dve, sum_done, n)
                    nc.vector.reciprocal(inv_sum[:, (c + 1) % 2, :], row_sum[:, (c + 1) % 2, :]).then_inc(inv_done, 1)
                    wait(dve, inv_done, n)
                    nc.vector.tensor_tensor(prob[:, (c + 1) % 2, :, :], prob[:, (c + 1) % 2, :, :],
                                            inv_sum[:, (c + 1) % 2, :, None].to_broadcast([P, 8, S]), ALU.mult)\
                        .then_inc(p_done, 1)
                if cur:
                    scores = ps_s[:, :].rearrange("p (h t) -> p h t", h=8)
                    dve.wait_ge(s_done, n + 1)
                    nc.vector.tensor_reduce(row_max[:, c % 2, :], scores, AX.X, ALU.max).then_inc(max_done, 1)
                    wait(dve, t_done, n - 1)
                    dve.wait_ge(max_done, n + 1)
                    nc.vector.tensor_tensor(prob[:, c % 2, :, :], scores,
                                            row_max[:, c % 2, :, None].to_broadcast([P, 8, S]), ALU.subtract)\
                        .then_inc(sub_done, 1)
                if c == 0 and cur:
                    bn_tail(2, i + 1)
                if c == 1 and prev:
                    dve.wait_ge(res_loaded, 16 * i)
                    dve.wait_ge(av_done, 4 * i)
                    nc.vector.tensor_tensor(z[:, :], x_res[:, :], ps_o[:, 0:D], ALU.add).then_inc(z_done, 1)
                    dve.wait_ge(z_done, i)
                    nc.vector.bn_stats(stats[:, 0, :], z[:, :]).then_inc(st_done[0], 1)
                if c == 2 and prev:
                    bn_tail(0, i)
                if c == 3 and prev:
                    bn_tail(1, i)
                    dve.wait_ge(rstd_done[1], i)
                    wait(dve, lat_stored, 32 * (i - 1))
                    nc.vector.tensor_scalar(lat[:, :], y[:, :], mean_var[:, 1, 0:1], rstd[:, 1:2], ALU.subtract,
                                            ALU.mult).then_inc(lat_n_done, 1)
                if c == 1 and cur:
                    dve.wait_ge(rstd_done[2], i + 1)
                    wait(dve, ctx_stored, 32 * i)
                    nc.vector.tensor_scalar(ctx_n[:, :], ctx_t[:, :], mean_var[:, 2, 0:1], rstd[:, 2:3], ALU.subtract,
                                            ALU.mult).then_inc(ctx_n_done, 1)

            slots(dve, slot)

        @block.gpsimd
        def _(pool):
            def power(m, count):
                pool.wait_ge(veps_done[m], count)
                nc.gpsimd.tensor_tensor(rstd[:, m:m + 1], rstd[:, m:m + 1], core.eps_pow[:, :], ALU.pow)\
                    .then_inc(rstd_done[m], 1)

            def scale_shift(tile, m, normed, scaled, done, count):
                pool.wait_ge(normed, count)
                nc.gpsimd.tensor_tensor(tile[:, :], tile[:, :], gb[:, m, :], ALU.mult).then_inc(scaled, 1)
                pool.wait_ge(scaled, count)
                nc.gpsimd.tensor_tensor(tile[:, :], tile[:, :], gb[:, m + 1, :], ALU.add).then_inc(done, 1)

            def slot(i, c, cur, prev):
                if c == 0 and cur:
                    power(2, i + 1)
                if c == 1 and cur:
                    scale_shift(ctx_n, 0, ctx_n_done, ctx_g_done, ctx_done, i + 1)
                if c == 2 and prev:
                    power(0, i)
                if c == 3 and prev:
                    power(1, i)
                    scale_shift(lat, 2, lat_n_done, lat_g_done, lat_done, i)

            pool.wait_ge(gb_loaded, 64)
            slots(pool, slot)


def latent_attention_phase(core, x_in, x_out, cat, mask, a):
    nc = core.nc
    NCH = 4 * NPAIR
    T = 2 * S
    with ExitStack() as ctx:
        def sb(name, shape, dt=F32):
            return core.sb(f"lat_{name}", shape, dt, ctx)

        def sem(name):
            return core.sem(f"lat_{name}", ctx)

        w_score, w_vo = sb("w_score", [P, H1, D]), sb("w_vo", [P, 2, H1 // 2, D])
        w_kv = a["L1_xattn_Wkv"]
        head_product_weights(core, "lat", H1 // 2, a["L1_xattn_Wq"], w_kv[:, 0:H1 * HD1],
                             w_kv[:, H1 * HD1:2 * H1 * HD1], a["L1_xattn_Wout"], "q", w_score, w_vo)

        mask_sb, mask_bias = sb("mask", [P, B, S], U8), sb("mask_bias", [P, B, T], BF16)
        c_t, c_v = sb("c_t", [P, 2, D]), sb("c_v", [P, 2, D])
        x_res = sb("x_res", [P, D])
        catT = sb("catT", [P, 2, T])
        query = sb("query", [P, 2, 2, 4, S])
        prob = sb("prob", [P, 2, 4, T])
        probT = sb("probT", [P, 4, P])
        ctxT = sb("ctxT", [P, 4, 2, S])
        row_max, row_sum, inv_sum = sb("row_max", [P, 2, 4]), sb("row_sum", [P, 2, 4]), sb("inv_sum", [P, 2, 4])
        z, y = sb("z", [P, D]), sb("y", [P, D])
        stats, mean_var, rstd = sb("stats", [P, 6]), sb("mean_var", [P, 2]), sb("rstd", [P, 1])

        ps_g, ps_s = [core.bank[0], core.bank[1]], [core.bank[2], core.bank[3]]
        ps_t, ps_c, ps_o, ps_x = core.bank[4], core.bank[5], core.bank[6], core.bank[7]

        mask_loaded, mask_done = sem("mask_loaded"), sem("mask_done")
        ct_loaded, cv_loaded, res_loaded, y_stored = (sem("ct_loaded"), sem("cv_loaded"), sem("res_loaded"),
                                                      sem("y_stored"))
        ct_done, catT_ready = sem("ct_done"), sem("catT_ready")
        g_done, q_copied = sem("g_done"), sem("q_copied")
        s_done, max_done, sub_done, exp_done = sem("s_done"), sem("max_done"), sem("sub_done"), sem("exp_done")
        sum_done, inv_done, p_done = sem("sum_done"), sem("inv_done"), sem("p_done")
        t_done, pT_copied, c_done, cT_copied, o_done = (sem("t_done"), sem("pT_copied"), sem("c_done"),
                                                        sem("cT_copied"), sem("o_done"))
        z_done, st_done, mv_done, veps_done, rstd_done, y_done = (
            sem("z_done"), sem("st_done"), sem("mv_done"), sem("veps_done"), sem("rstd_done"), sem("y_done"))
        block = ctx.enter_context(nc.Block())

        def have(n):
            return not isinstance(n, int) or 0 <= n < NCH

        def slots(eng, slot):
            for c in range(4):
                slot(0, c)
            with eng.Fori(1, NPAIR - 1) as i:
                for c in range(4):
                    slot(i, c)
            for i in (NPAIR - 1, NPAIR):
                for c in range(4):
                    slot(i, c)

        def rows(t, i):
            return t[bass.ds(i, 1), :, :].rearrange("o p d -> p (o d)")

        @block.sync
        def _(sp):
            def load_c(dst, i, loaded):
                sp.dma_start(dst[:, :, :], cat[bass.ds(2 * i, 2), :, :].rearrange("b t d -> t b d")).then_inc(loaded, 16)

            def pair(i):
                if have(4 * (i + 1)):
                    sp.wait_ge(ct_done, i + 1)
                    load_c(c_t, i + 1, ct_loaded)
                if have(4 * i):
                    wait(sp, c_done, 4 * i)
                    load_c(c_v, i, cv_loaded)
                    wait(sp, z_done, i)
                    sp.dma_start(x_res[:, :], rows(x_in, i)).then_inc(res_loaded, 16)
                if have(4 * (i - 1)):
                    sp.wait_ge(y_done, i)
                    sp.dma_start(rows(x_out, i - 1), y[:, :]).then_inc(y_stored, 16)

            sp.dma_start(mask_sb[:, :, :].rearrange("p b s -> p (b s)"), bcast_rows(mask.rearrange("b s -> (b s)")))\
                .then_inc(mask_loaded, 16)
            load_c(c_t, 0, ct_loaded)
            pair(0)
            with sp.Fori(1, NPAIR - 1) as i:
                pair(i)
            pair(NPAIR - 1)
            pair(NPAIR)
            sp.wait_ge(y_stored, 16 * NPAIR)

        @block.tensor
        def _(pe):
            def transpose_cat(i):
                pe.wait_ge(ct_loaded, 16 * (i + 1))
                wait(pe, catT_ready, i)
                for b in range(2):
                    last = nc.tensor.transpose(ps_x[:, b * T:(b + 1) * T], c_t[:, b, :], core.ident[:, :])
                last.then_inc(ct_done, 1)

            def slot(i, c):
                n = 4 * i + c
                if c == 3 and have(n + 1) and have(n):
                    transpose_cat(i + 1)
                if have(n):
                    if c == 0:
                        pe.wait_ge(catT_ready, i + 1)
                    wait(pe, q_copied, n - 1)
                    for h in range(4):
                        last = nc.tensor.matmul(ps_g[c % 2][:, h * P:(h + 1) * P].rearrange("p (b s) -> p b s", b=2),
                                                w_score[:, 4 * c + h, :], catT[:, :, S:T], start=True, stop=True)
                    last.then_inc(g_done, 1)
                if have(n - 2):
                    wait(pe, p_done, n - 1)
                    wait(pe, pT_copied, n - 2)
                    for m in range(4):
                        last = nc.tensor.transpose(ps_t[:, m * P:(m + 1) * P], prob[:, c % 2, m, :], core.ident[:, :])
                    last.then_inc(t_done, 1)
                if have(n - 3):
                    wait(pe, cT_copied, n - 2)
                    if c == 3:
                        wait(pe, z_done, i)
                    for h in range(4):
                        last = nc.tensor.matmul(ps_o[:, 0:D], ctxT[:, h, :, :].rearrange("p b s -> p (b s)"),
                                                w_vo[:, h % 2, (2 * ((c + 1) % 4)) + h // 2, :],
                                                start=(c == 3 and h == 0), stop=(c == 2 and h == 3))
                    last.then_inc(o_done, 1)
                if have(n):
                    pe.wait_ge(q_copied, n + 1)
                    wait(pe, sub_done, n - 1)
                    if c == 0:
                        pe.wait_ge(mask_done, 2)
                    nc.tensor.matmul(ps_s[c % 2][:, :].rearrange("p (b h t) -> p b h t", b=2, h=2), core.identb[:, :],
                                     mask_bias[:, bass.ds(2 * i, 2), None, :].to_broadcast([P, 2, 2, T]),
                                     start=True, stop=False)
                    for m in range(4):
                        b, hp = m // 2, m % 2
                        last = nc.tensor.matmul(
                            ps_s[c % 2][:, m * T:(m + 1) * T],
                            query[:, c % 2, b, 2 * hp:2 * hp + 2, :].rearrange("p h s -> p (h s)"), catT[:, b, :],
                            start=False, stop=(m == 3))
                    last.then_inc(s_done, 1)
                if have(n - 2):
                    wait(pe, pT_copied, n - 1)
                    wait(pe, cT_copied, n - 2)
                    if c == 2:
                        pe.wait_ge(cv_loaded, 16 * (i + 1))
                    for b in range(2):
                        last = nc.tensor.matmul(ps_c[:, b * 256:(b + 1) * 256], c_v[:, b, :],
                                                probT[:, 2 * b:2 * b + 2, :].rearrange("p h e -> p (h e)"),
                                                start=True, stop=True)
                    last.then_inc(c_done, 1)

            transpose_cat(0)
            slots(pe, slot)

        @block.scalar
        def _(act):
            def copy_catT(i):
                act.wait_ge(ct_done, i + 1)
                wait(act, s_done, 4 * i)
                nc.scalar.activation(catT[:, :, :].rearrange("p b t -> p (b t)"), ps_x[:, 0:2 * T], ACT.Copy)\
                    .then_inc(catT_ready, 1)

            def slot(i, c):
                n = 4 * i + c
                if have(n - 3):
                    wait(act, c_done, n - 2)
                    wait(act, o_done, n - 3)
                    nc.scalar.activation(ctxT[:, :, :, :], ps_c[:, :].rearrange("p (b h s) -> p h b s", b=2, h=4),
                                         ACT.Copy).then_inc(cT_copied, 1)
                if have(n):
                    act.wait_ge(g_done, n + 1)
                    wait(act, s_done, n - 1)
                    nc.scalar.activation(query[:, c % 2, :, :, :],
                                         ps_g[c % 2][:, :].rearrange("p (h b s) -> p b h s", h=4, b=2), ACT.Copy)\
                        .then_inc(q_copied, 1)
                if have(n - 1):
                    wait(act, sub_done, n)
                    flat = prob[:, (c + 1) % 2, :, :].rearrange("p h t -> p (h t)")
                    nc.scalar.activation(flat, flat, ACT.Exp).then_inc(exp_done, 1)
                if have(n - 2):
                    wait(act, t_done, n - 1)
                    wait(act, c_done, n - 2)
                    nc.scalar.activation(probT[:, :, :].rearrange("p h e -> p (h e)"), ps_t[:, :], ACT.Copy)\
                        .then_inc(pT_copied, 1)
                if c == 3 and have(n + 1) and have(n):
                    copy_catT(i + 1)

            copy_catT(0)
            slots(act, slot)

        @block.vector
        def _(dve):
            def slot(i, c):
                n = 4 * i + c
                if c == 3 and have(4 * (i - 1)):
                    dve.wait_ge(res_loaded, 16 * i)
                    dve.wait_ge(o_done, 4 * i)
                    nc.vector.tensor_tensor(z[:, :], x_res[:, :], ps_o[:, 0:D], ALU.add).then_inc(z_done, 1)
                    dve.wait_ge(z_done, i)
                    nc.vector.bn_stats(stats[:, :], z[:, :]).then_inc(st_done, 1)
                    dve.wait_ge(st_done, i)
                if have(n - 1):
                    par = (c + 1) % 2
                    wait(dve, exp_done, n)
                    nc.vector.tensor_reduce(row_sum[:, par, :], prob[:, par, :, :], AX.X, ALU.add).then_inc(sum_done, 1)
                    wait(dve, sum_done, n)
                    nc.vector.reciprocal(inv_sum[:, par, :], row_sum[:, par, :]).then_inc(inv_done, 1)
                    wait(dve, inv_done, n)
                    nc.vector.tensor_tensor(prob[:, par, :, :], prob[:, par, :, :],
                                            inv_sum[:, par, :, None].to_broadcast([P, 4, T]), ALU.mult)\
                        .then_inc(p_done, 1)
                if have(n):
                    scores = ps_s[c % 2][:, :].rearrange("p (h t) -> p h t", h=4)
                    dve.wait_ge(s_done, n + 1)
                    nc.vector.tensor_reduce(row_max[:, c % 2, :], scores, AX.X, ALU.max).then_inc(max_done, 1)
                    wait(dve, t_done, n - 1)
                    dve.wait_ge(max_done, n + 1)
                    nc.vector.tensor_tensor(prob[:, c % 2, :, :], scores,
                                            row_max[:, c % 2, :, None].to_broadcast([P, 4, T]), ALU.subtract)\
                        .then_inc(sub_done, 1)
                if c == 3 and have(4 * (i - 1)):
                    nc.vector.bn_aggr(mean_var[:, :], stats[:, :]).then_inc(mv_done, 1)
                    dve.wait_ge(mv_done, i)
                    nc.vector.tensor_scalar(rstd[:, :], mean_var[:, 1:2], EPS, None, ALU.add).then_inc(veps_done, 1)
                    dve.wait_ge(rstd_done, i)
                    wait(dve, y_stored, 16 * (i - 1) if isinstance(i, int) else 16 * i - 16)
                    nc.vector.tensor_scalar(y[:, :], z[:, :], mean_var[:, 0:1], rstd[:, :], ALU.subtract, ALU.mult)\
                        .then_inc(y_done, 1)

            nc.vector.memset(mask_bias[:, :, :], 0.0).then_inc(mask_done, 1)
            dve.wait_ge(mask_loaded, 16)
            dve.wait_ge(mask_done, 1)
            nc.vector.tensor_scalar(mask_bias[:, :, 0:S], mask_sb[:, :, :], -NEG, NEG, ALU.mult, ALU.add).then_inc(mask_done, 1)
            slots(dve, slot)

        @block.gpsimd
        def _(pool):
            def power(i):
                pool.wait_ge(veps_done, i)
                nc.gpsimd.tensor_tensor(rstd[:, :], rstd[:, :], core.eps_pow[:, :], ALU.pow).then_inc(rstd_done, 1)

            with pool.Fori(1, NPAIR + 1) as i:
                power(i)


def moe_phase(core, x_in, x_out, xe, ye, a):
    nc = core.nc
    T = NPAIR * P
    with ExitStack() as ctx:
        def sb(name, shape, dt=F32):
            return core.sb(f"moe_{name}", shape, dt, ctx)

        x = sb("x", [P, NPAIR, D])
        gate = sb("gate", [P, NPAIR])
        dest, src_row = sb("dest", [P, NPAIR], U32), sb("src_row", [P, NPAIR], U32)
        b1T = sb("b1T", [P, E * FF // P])

        moe_routing(core, x_in, x, gate, dest, src_row, b1T, xe, ye, a, T)
        moe_experts(core, xe, ye, b1T, a)
        moe_combine(core, x_out, x, gate, src_row, ye)


def moe_routing(core, x_in, x, gate, dest, src_row, b1T, xe, ye, a, T):
    nc = core.nc
    GP = 4
    NG = NPAIR // GP
    NB1 = E * FF // P
    with ExitStack() as ctx:
        def sb(name, shape, dt=F32):
            return core.sb(f"route_{name}", shape, dt, ctx)

        def sem(name):
            return core.sem(f"route_{name}", ctx)

        router = sb("router", [P, E])
        b1_raw = sb("b1_raw", [NB1, P])
        xT = sb("xT", [P, 2, GP * P])
        zeros = sb("zeros", [P, 8, D])
        tri, ones = sb("tri", [P, P], BF16), sb("ones", [P, P], BF16)
        order_i, order = sb("order_i", [P, E], I32), sb("order", [P, E])
        dump_i, dump = sb("dump_i", [P, NPAIR], I32), sb("dump", [P, NPAIR])
        wide = [P, NPAIR, E]
        top, total = sb("top", [P, NPAIR]), sb("total", [P, NPAIR])
        diff, expo, sel = sb("diff", wide), sb("expo", wide), sb("sel", wide)
        first = sb("first", [P, NPAIR])
        onehot = sb("onehot", wide, BF16)
        count = [sb(f"count{n}", wide) for n in range(2)]
        pos = sb("pos", wide)
        place, valid = sb("place", [P, NPAIR]), sb("valid", [P, NPAIR])
        ps_x = [core.bank[0], core.bank[1]]
        ps_l, ps_b, ps_cum, ps_tot = core.bank[2], core.bank[3], core.bank[4], core.bank[5]

        x_loaded = [sem(f"x_loaded{g}") for g in range(NG)]
        small_loaded, zeros_done, zeroed, scattered = (sem("small_loaded"), sem("zeros_done"), sem("zeroed"),
                                                       sem("scattered"))
        xt_done, xT_ready, logits_done = sem("xt_done"), sem("xT_ready"), sem("logits_done")
        ranks_done, exp_done = sem("ranks_done"), sem("exp_done")
        q, masks = sem("steps"), sem("masks")
        onehot_done, dest_done = sem("onehot_done"), sem("dest_done")
        block = ctx.enter_context(nc.Block())

        @block.sync
        def _(sp):
            for g in range(NG):
                sp.dma_start(x[:, g * GP:(g + 1) * GP, :], x_in[g * GP:(g + 1) * GP, :, :].rearrange("n p d -> p n d"))\
                    .then_inc(x_loaded[g], 16)
            sp.wait_ge(zeros_done, 1)
            for n in range(CAP * E // (8 * P)):
                sp.dma_start(xe[n * 8 * P:(n + 1) * 8 * P, :].rearrange("(r p) d -> p r d", p=P), zeros[:, :, :])\
                    .then_inc(zeroed, 16)
            sp.dma_start(ye[DUMP:DUMP + 1, :], zeros[0:1, 0, :]).then_inc(zeroed, 16)
            sp.wait_ge(zeroed, 16 * (CAP * E // (8 * P) + 1))
            sp.wait_ge(scattered, 16 * NPAIR)

        @block.tensor
        def _(pe):
            def logits(g):
                pe.wait_ge(xT_ready, g + 1)
                for n in range(GP):
                    t = g * GP + n
                    last = nc.tensor.matmul(ps_l[:, t * E:(t + 1) * E], xT[:, g % 2, n * P:(n + 1) * P], router[:, :],
                                            start=True, stop=True)
                last.then_inc(logits_done, 1)

            pe.wait_ge(small_loaded, 32)
            for g in range(NG):
                pe.wait_ge(x_loaded[g], 16)
                wait(pe, xT_ready, g - 1)
                for n in range(GP):
                    last = nc.tensor.transpose(ps_x[g % 2][:, n * P:(n + 1) * P], x[:, g * GP + n, :], core.ident[:, :])
                last.then_inc(xt_done, 1)
                if g > 0:
                    logits(g - 1)
            logits(NG - 1)
            nc.tensor.transpose(ps_b[:, 0:NB1], b1_raw[:, :], core.ident[0:NB1, 0:NB1]).then_inc(ranks_done, 1)
            pe.wait_ge(onehot_done, 1)
            pe.wait_ge(masks, 6)
            flat = onehot[:, :, :].rearrange("p n e -> p (n e)")
            nc.tensor.matmul(ps_cum[:, 0:NPAIR * E], tri[:, :], flat, start=True, stop=True).then_inc(ranks_done, 1)
            nc.tensor.matmul(ps_tot[:, 0:NPAIR * E], ones[:, :], flat, start=True, stop=True).then_inc(ranks_done, 1)

        @block.scalar
        def _(act):
            act.dma_start(router[:, :], a["L1_ffn_router_w"]).then_inc(small_loaded, 16)
            act.dma_start(b1_raw[:, :], a["L1_ffn_b1"].rearrange("e (t p) -> (e t) p", p=P)).then_inc(small_loaded, 16)
            for g in range(NG):
                act.wait_ge(xt_done, g + 1)
                wait(act, logits_done, g - 1)
                nc.scalar.activation(xT[:, g % 2, :], ps_x[g % 2][:, :], ACT.Copy).then_inc(xT_ready, 1)
            act.wait_ge(q, 2)
            nc.scalar.activation(expo[:, :, :], diff[:, :, :], ACT.Exp).then_inc(exp_done, 1)
            act.wait_ge(ranks_done, 1)
            nc.scalar.activation(b1T[:, :], ps_b[:, 0:NB1], ACT.Copy).then_inc(exp_done, 1)

        @block.vector
        def _(dve):
            steps = [0]

            def step(ins):
                ins.then_inc(q, 1)
                steps[0] += 1
                dve.wait_ge(q, steps[0])

            def over_experts(ap):
                return ap[:, :, None].to_broadcast(wide)

            nc.vector.memset(zeros[:, :, :], 0.0).then_inc(zeros_done, 1)
            nc.vector.memset(tri[:, :], 1.0).then_inc(masks, 1)
            nc.vector.memset(ones[:, :], 1.0).then_inc(masks, 1)
            dve.wait_ge(masks, 5)
            nc.vector.tensor_copy(order[:, :], order_i[:, :]).then_inc(masks, 1)
            nc.vector.tensor_copy(dump[:, :], dump_i[:, :]).then_inc(masks, 1)
            dve.wait_ge(masks, 7)
            dve.wait_ge(logits_done, NG)
            logits = ps_l[:, 0:NPAIR * E].rearrange("p (n e) -> p n e", e=E)
            step(nc.vector.tensor_reduce(top[:, :], logits, AX.X, ALU.max))
            step(nc.vector.tensor_tensor(diff[:, :, :], logits, over_experts(top), ALU.subtract))
            step(nc.vector.tensor_scalar(sel[:, :, :], diff[:, :, :], 0.0, None, ALU.is_ge))
            step(nc.vector.tensor_tensor(sel[:, :, :], sel[:, :, :], order[:, None, :].to_broadcast(wide), ALU.mult))
            step(nc.vector.tensor_reduce(first[:, :], sel[:, :, :], AX.X, ALU.max))
            nc.vector.tensor_tensor(onehot[:, :, :], sel[:, :, :], over_experts(first), ALU.is_equal)\
                .then_inc(onehot_done, 1)
            dve.wait_ge(exp_done, 1)
            step(nc.vector.tensor_reduce(total[:, :], expo[:, :, :], AX.X, ALU.add))
            step(nc.vector.reciprocal(gate[:, :], total[:, :]))
            dve.wait_ge(ranks_done, 3)
            step(nc.vector.tensor_copy(count[0][:, :, :], ps_tot[:, 0:NPAIR * E].rearrange("p (n e) -> p n e", e=E)))
            cur, shift = 0, 1
            while shift < NPAIR:
                src, dst = count[cur], count[1 - cur]
                nc.vector.tensor_copy(dst[:, 0:shift, :], src[:, 0:shift, :]).then_inc(q, 1)
                steps[0] += 1
                step(nc.vector.tensor_tensor(dst[:, shift:, :], src[:, shift:, :], src[:, 0:NPAIR - shift, :], ALU.add))
                cur, shift = 1 - cur, 2 * shift
            step(nc.vector.tensor_tensor(pos[:, :, :], count[cur][:, :, :],
                                         ps_tot[:, 0:NPAIR * E].rearrange("p (n e) -> p n e", e=E), ALU.subtract))
            step(nc.vector.tensor_tensor(pos[:, :, :], pos[:, :, :],
                                         ps_cum[:, 0:NPAIR * E].rearrange("p (n e) -> p n e", e=E), ALU.add))
            dve.wait_ge(onehot_done, 1)
            step(nc.vector.tensor_tensor(pos[:, :, :], pos[:, :, :], onehot[:, :, :], ALU.mult))
            step(nc.vector.tensor_reduce(place[:, :], pos[:, :, :], AX.X, ALU.add))
            step(nc.vector.tensor_scalar(valid[:, :], place[:, :], float(CAP), None, ALU.is_le))
            step(nc.vector.tensor_tensor(gate[:, :], gate[:, :], valid[:, :], ALU.mult))
            step(nc.vector.tensor_scalar(first[:, :], first[:, :], float(-CAP), float(E * CAP - 1), ALU.mult, ALU.add))
            step(nc.vector.tensor_tensor(place[:, :], place[:, :], first[:, :], ALU.add))
            step(nc.vector.tensor_tensor(place[:, :], place[:, :], dump[:, :], ALU.subtract))
            step(nc.vector.tensor_tensor(place[:, :], place[:, :], valid[:, :], ALU.mult))
            step(nc.vector.tensor_tensor(place[:, :], place[:, :], dump[:, :], ALU.add))
            nc.vector.tensor_copy(dest[:, :], place[:, :]).then_inc(dest_done, 1)
            step(nc.vector.tensor_scalar(total[:, :], place[:, :], float(DUMP), None, ALU.min))
            nc.vector.tensor_copy(src_row[:, :], total[:, :]).then_inc(dest_done, 1)

        @block.gpsimd
        def _(pool):
            nc.gpsimd.iota(order_i[:, :], pattern=[[-1, E]], base=E, channel_multiplier=0).then_inc(masks, 1)
            pool.wait_ge(masks, 3)
            nc.gpsimd.iota(dump_i[:, :], pattern=[[P, NPAIR]], base=DUMP, channel_multiplier=1).then_inc(masks, 1)
            pool.wait_ge(masks, 4)
            nc.gpsimd.affine_select(out=tri[:, :], in_=tri[:, :], compare_op=ALU.is_ge, fill=0.0, base=0,
                                    pattern=[[1, P]], channel_multiplier=-1).then_inc(masks, 1)
            pool.wait_ge(zeroed, 16 * (CAP * E // (8 * P) + 1))
            pool.wait_ge(dest_done, 1)
            for g in range(NG):
                pool.wait_ge(x_loaded[g], 16)
            for n in range(NPAIR):
                pool.indirect_dma_start(out=xe, out_offset=bass.IndirectOffsetOnAxis(ap=dest[:, n:n + 1], axis=0),
                                        in_=x[:, n, :], in_offset=None).then_inc(scattered, 16)


def moe_experts(core, xe, ye, b1T, a):
    nc = core.nc
    NT, NR = FF // P, CAP // P
    with ExitStack() as ctx:
        def sb(name, shape, dt=F32):
            return core.sb(f"exp_{name}", shape, dt, ctx)

        def sem(name):
            return core.sem(f"exp_{name}", ctx)

        rows = sb("rows", [P, 2, NR, D])
        w1, w2 = sb("w1", [P, 2, FF]), sb("w2", [P, 2, NT, D])
        b2 = sb("b2", [P, 2, D])
        b1_col = sb("b1_col", [P, 2, NT])
        rT = sb("rT", [P, 2, CAP])
        hidden = sb("hidden", [P, 2, NT, CAP])
        o = sb("o", [P, 2, NR, D])
        ps_x, ps_out = core.bank[0], core.bank[1]
        ps_h = [core.bank[2], core.bank[3], core.bank[4], core.bank[5]]
        rows_loaded = [sem(f"rows_loaded{p}") for p in range(2)]
        w1_loaded = [sem(f"w1_loaded{p}") for p in range(2)]
        w2_loaded = [sem(f"w2_loaded{p}") for p in range(2)]
        stored = [sem(f"stored{p}") for p in range(2)]
        rt_done, rT_ready, h_done, relu_done, out_done, o_done, b1_ready = (
            sem("rt_done"), sem("rT_ready"), sem("h_done"), sem("relu_done"), sem("out_done"), sem("o_done"),
            sem("b1_ready"))
        block = ctx.enter_context(nc.Block())

        def slots(eng, slot):
            for i in range(-1, 3):
                slot(i, i // 2, i % 2, lambda j: 0 <= j < E)
            with eng.Fori(1, E // 2 - 1) as k:
                slot(2 * k + 1, k, 1, lambda j: True)
                slot(2 * k + 2, k + 1, 0, lambda j: True)
            for i in range(E - 1, E + 1):
                slot(i, i // 2, i % 2, lambda j: 0 <= j < E)

        def here(on, i, d):
            return on(i + d if isinstance(i, int) else 0)

        @block.sync
        def _(sp):
            def slot(i, k, par, on):
                if here(on, i, 1):
                    wait(sp, rt_done, i)
                    sp.dma_start(rows[:, 1 - par, :, :], xe[bass.ds((i + 1) * CAP, CAP), :]
                                 .rearrange("(r p) d -> p r d", p=P)).then_inc(rows_loaded[1 - par], 16)
                    wait(sp, h_done, NT * i)
                    sp.dma_start(w1[:, 1 - par, :], a["L1_ffn_w1"][bass.ds(i + 1, 1), :, :]
                                 .rearrange("o p f -> p (o f)")).then_inc(w1_loaded[1 - par], 16)
                wait(sp, o_done, i)
                if here(on, i, -1):
                    sp.dma_start(ye[bass.ds((i - 1) * CAP, CAP), :].rearrange("(r p) d -> p r d", p=P),
                                 o[:, 1 - par, :, :]).then_inc(stored[1 - par], 16)
                if here(on, i, 1):
                    sp.dma_start(w2[:, 1 - par, :, :], a["L1_ffn_w2"][bass.ds(i + 1, 1), :, :]
                                 .rearrange("o (t p) d -> p (o t) d", p=P)).then_inc(w2_loaded[1 - par], 16)
                    sp.dma_start(b2[:, 1 - par, :], a["L1_ffn_b2"][bass.ds(i + 1, 1), :].to_broadcast([P, D]))\
                        .then_inc(w2_loaded[1 - par], 16)

            slots(sp, slot)
            for par in range(2):
                sp.wait_ge(stored[par], 16 * (E // 2))

        @block.tensor
        def _(pe):
            def slot(i, k, par, on):
                if here(on, i, 0):
                    wait(pe, rT_ready, i + 1)
                    wait(pe, w1_loaded[par], 16 * (k + 1))
                    for t in range(NT):
                        wait(pe, relu_done, NT * (i - 1) + t + 1)
                        nc.tensor.matmul(ps_h[t][:, :], w1[:, par, t * P:(t + 1) * P], rT[:, par, :],
                                         start=True, stop=True).then_inc(h_done, 1)
                if here(on, i, 1):
                    wait(pe, rows_loaded[1 - par], 16 * (k + par + 1))
                    wait(pe, rT_ready, i + 1)
                    for r in range(NR):
                        last = nc.tensor.transpose(ps_x[:, r * P:(r + 1) * P], rows[:, 1 - par, r, :], core.ident[:, :])
                    last.then_inc(rt_done, 1)
                if here(on, i, -1):
                    wait(pe, relu_done, NT * i)
                    wait(pe, w2_loaded[1 - par], 32 * (k + par))
                    wait(pe, o_done, i - 1)
                    for r in range(NR):
                        for t in range(NT):
                            last = nc.tensor.matmul(ps_out[:, r * P:(r + 1) * P],
                                                    hidden[:, 1 - par, t, r * P:(r + 1) * P], w2[:, 1 - par, t, :],
                                                    start=(t == 0), stop=(t == NT - 1))
                    last.then_inc(out_done, 1)

            slots(pe, slot)

        @block.scalar
        def _(act):
            def slot(i, k, par, on):
                if here(on, i, 1):
                    wait(act, rt_done, i + 2)
                    wait(act, h_done, NT * i)
                    nc.scalar.activation(rT[:, 1 - par, :], ps_x[:, :], ACT.Copy).then_inc(rT_ready, 1)
                if here(on, i, 0):
                    wait(act, out_done, i - 1)
                    wait(act, b1_ready, i + 1)
                    for t in range(NT):
                        wait(act, h_done, NT * i + t + 1)
                        nc.scalar.activation(hidden[:, par, t, :], ps_h[t][:, :], ACT.Relu,
                                             bias=b1_col[:, par, t:t + 1]).then_inc(relu_done, 1)

            slots(act, slot)

        @block.vector
        def _(dve):
            def slot(i, k, par, on):
                if here(on, i, 0):
                    wait(dve, relu_done, NT * (i - 1))
                    nc.vector.tensor_copy(b1_col[:, par, :], b1T[:, bass.ds(NT * i, NT)]).then_inc(b1_ready, 1)
                if here(on, i, -1):
                    wait(dve, out_done, i)
                    wait(dve, stored[1 - par], 16 * (k + par - 1))
                    nc.vector.tensor_tensor(o[:, 1 - par, :, :], ps_out[:, :].rearrange("p (r d) -> p r d", r=NR),
                                            b2[:, 1 - par, :][:, None, :].to_broadcast([P, NR, D]), ALU.add)\
                        .then_inc(o_done, 1)

            slots(dve, slot)


def moe_combine(core, x_out, x, gate, src_row, ye):
    nc = core.nc
    GP = 4
    NG = NPAIR // GP
    with ExitStack() as ctx:
        def sb(name, shape, dt=F32):
            return core.sb(f"comb_{name}", shape, dt, ctx)

        def sem(name):
            return core.sem(f"comb_{name}", ctx)

        got = sb("got", [P, NPAIR, D])
        stats = sb("stats", [P, NPAIR, 6])
        mean_var = sb("mean_var", [P, NPAIR, 2])
        rstd = sb("rstd", [P, NPAIR])
        y = sb("y", [P, NPAIR, D])
        gathered = [sem(f"gathered{g}") for g in range(NG)]
        stored = sem("stored")
        z_done, stats_done, mv_done, veps_done, rstd_done, y_done = (
            sem("z_done"), sem("stats_done"), sem("mv_done"), sem("veps_done"), sem("rstd_done"), sem("y_done"))
        block = ctx.enter_context(nc.Block())

        @block.sync
        def _(sp):
            for g in range(NG):
                sp.wait_ge(y_done, g + 1)
                sp.dma_start(x_out[g * GP:(g + 1) * GP, :, :].rearrange("n p d -> p n d"), y[:, g * GP:(g + 1) * GP, :])\
                    .then_inc(stored, 16)
            sp.wait_ge(stored, 16 * NG)

        @block.vector
        def _(dve):
            def norm(g):
                dve.wait_ge(rstd_done, g + 1)
                for n in range(g * GP, (g + 1) * GP):
                    last = nc.vector.tensor_scalar(y[:, n, :], got[:, n, :], mean_var[:, n, 0:1], rstd[:, n:n + 1],
                                                   ALU.subtract, ALU.mult)
                last.then_inc(y_done, 1)

            for g in range(NG):
                group = range(g * GP, (g + 1) * GP)
                dve.wait_ge(gathered[g], 16 * GP)
                for n in group:
                    last = nc.vector.scalar_tensor_tensor(out=got[:, n, :], in0=got[:, n, :], scalar=gate[:, n:n + 1],
                                                          in1=x[:, n, :], op0=ALU.mult, op1=ALU.add)
                last.then_inc(z_done, 1)
                dve.wait_ge(z_done, g + 1)
                for n in group:
                    last = nc.vector.bn_stats(stats[:, n, :], got[:, n, :])
                last.then_inc(stats_done, 1)
                dve.wait_ge(stats_done, g + 1)
                for n in group:
                    last = nc.vector.bn_aggr(mean_var[:, n, :], stats[:, n, :])
                last.then_inc(mv_done, 1)
                dve.wait_ge(mv_done, g + 1)
                nc.vector.tensor_scalar(rstd[:, g * GP:(g + 1) * GP], mean_var[:, g * GP:(g + 1) * GP, 1], EPS, None,
                                        ALU.add).then_inc(veps_done, 1)
                if g > 0:
                    norm(g - 1)
            norm(NG - 1)

        @block.gpsimd
        def _(pool):
            def gather(g):
                for n in range(g * GP, (g + 1) * GP):
                    pool.indirect_dma_start(out=got[:, n, :], out_offset=None, in_=ye,
                                            in_offset=bass.IndirectOffsetOnAxis(ap=src_row[:, n:n + 1], axis=0))\
                        .then_inc(gathered[g], 16)

            gather(0)
            gather(1)
            for g in range(NG):
                if g + 2 < NG:
                    gather(g + 2)
                pool.wait_ge(veps_done, g + 1)
                cols = rstd[:, g * GP:(g + 1) * GP]
                nc.gpsimd.tensor_tensor(cols, cols, core.eps_pow[:, :].to_broadcast([P, GP]), ALU.pow)\
                    .then_inc(rstd_done, 1)


def decoder(nc, a, out):
    stage = [nc.dram_tensor(f"stage{n}", (NPAIR, P, D), F32, kind="Internal").ap() for n in range(5)]
    cat = nc.dram_tensor("cat", (B, 2 * S, D), F32, kind="Internal").ap()
    pairs = lambda t: t.rearrange("(n b) s d -> n (b s) d", b=2)
    with ExitStack() as ctx:
        core = Core(nc, ctx)
        constants_phase(core)
        wqkv = a["L0_attn_w_qkv"]
        low_head_phase(core, "self", pairs(a["x"]), None, stage[0],
                       low_head_weights(nc, core, "self", wqkv[:, 0:D], wqkv[:, D:2 * D], wqkv[:, 2 * D:3 * D],
                                        a["L0_attn_w_proj"], False), a["L0_attn_b_proj"], False)
        low_head_phase(core, "cross", stage[0], pairs(a["ctx_1024"]), stage[1],
                       low_head_weights(nc, core, "cross", a["L0_xattn_Wq"], a["L0_xattn_Wk"], a["L0_xattn_Wv"],
                                        a["L0_xattn_Wo"], True), a["L0_xattn_bo"], True)
        feed_forward_phase(core, stage[1], stage[2], a["L0_ffn_w_fc"], a["L0_ffn_w_proj"], a["L0_ffn_u"],
                           a["L0_ffn_v"], a["L0_ffn_fast_b"], a["L0_ffn_gate"])
        differential_attention_phase(core, stage[2], stage[3], cat, pairs(a["ctx_1024"]), a)
        latent_attention_phase(core, stage[3], stage[4], cat, a["mask_BxS2_bk0"], a)
        xe = nc.dram_tensor("expert_rows", (DUMP + B * S, D), F32, kind="Internal").ap()
        ye = nc.dram_tensor("expert_outputs", (DUMP + 1, D), F32, kind="Internal").ap()
        moe_phase(core, stage[4], pairs(out), xe, ye, a)

_INS = ['x', 'ctx_1024', 'mask_BxS2_bk0', 'L0_attn_w_qkv', 'L0_attn_w_proj', 'L0_attn_b_proj', 'L0_xattn_Wq',
        'L0_xattn_Wk', 'L0_xattn_Wv', 'L0_xattn_Wo', 'L0_xattn_bo', 'L0_ffn_fast_b', 'L0_ffn_w_fc', 'L0_ffn_w_proj',
        'L0_ffn_u', 'L0_ffn_v', 'L0_ffn_gate', 'L1_attn_Wq', 'L1_attn_Wk', 'L1_attn_Wv', 'L1_attn_Wo', 'L1_attn_lq1',
        'L1_attn_lk1', 'L1_attn_lq2', 'L1_attn_lk2', 'L1_xattn_g1', 'L1_xattn_b1', 'L1_xattn_g2', 'L1_xattn_b2',
        'L1_xattn_Wq', 'L1_xattn_Wkv', 'L1_xattn_Wout', 'L1_ffn_router_w', 'L1_ffn_w1', 'L1_ffn_b1', 'L1_ffn_w2',
        'L1_ffn_b2']


def kernel(**inputs):
    import numpy as _np
    import concourse.bacc as _bacc
    from concourse import mybir as _mybir
    from concourse.bass_utils import run_bass_kernel_spmd as _run

    nc = _bacc.Bacc("TRN2", target_bir_lowering=False, num_devices=1)
    arrays, args = {}, {}
    for name in _INS:
        a = _np.ascontiguousarray(inputs[name])
        if a.ndim == 0:
            a = a.reshape(1)
        arrays[f"in_{name}_dram"] = a
        args[name] = nc.dram_tensor(f"in_{name}_dram", a.shape, _mybir.dt.from_np(a.dtype), kind="ExternalInput").ap()
    out = nc.dram_tensor("out_0_dram", (B, S, D), _mybir.dt.float32, kind="ExternalOutput").ap()
    decoder(nc, args, out)
    r = _run(nc, [arrays], core_ids=[0])
    return r.results[0]["out_0_dram"]
```

```python
from contextlib import ExitStack

import concourse.bass as bass
from concourse import mybir

F32 = mybir.dt.float32
BF16 = mybir.dt.bfloat16
I32 = mybir.dt.int32
U8 = mybir.dt.uint8
U32 = mybir.dt.uint32
ALU = mybir.AluOpType
ACT = mybir.ActivationFunctionType
AX = mybir.AxisListType

P = 128
B, S, D = 64, 64, 128
NPAIR = B * S // P
H0, HD0 = 16, 8
H1, HD1 = 16, 64
EPS = 1e-5
NEG = -1e30
FF = 512
E, CAP = 8, 512
DUMP = E * CAP


def wait(eng, sem, count):
    if not isinstance(count, int) or count > 0:
        eng.wait_ge(sem, count)


def bcast_rows(ap, rows=P):
    return bass.AP(ap.tensor, ap.offset, [[0, rows]] + list(ap.ap))


class Core:

    def __init__(self, nc, ctx):
        self.nc, self.ctx, self.sems = nc, ctx, {}
        self.bank = [ctx.enter_context(nc.psum_tensor(f"bank{n}", [P, 512], F32)) for n in range(8)]
        self.ident = self.sb("ident", [P, P], F32)
        self.identb = self.sb("identb", [P, P], BF16)
        self.causal = self.sb("causal", [P, S], BF16)
        self.eps_pow = self.sb("eps_pow", [P, 1], F32)

    def sb(self, name, shape, dt=F32, ctx=None):
        return (ctx or self.ctx).enter_context(self.nc.sbuf_tensor(name, shape, dt))

    def sem(self, name, ctx):
        handle = self.nc.alloc_semaphore(name)
        if ctx not in self.sems:
            self.sems[ctx] = []
            ctx.callback(self.give_back, ctx)
        self.sems[ctx].append(handle)
        return handle

    def give_back(self, ctx):
        self.nc.clear_and_free_semaphores(self.sems.pop(ctx))
        self.nc.all_engine_barrier(sem_only=True)


class EarlyLoads:

    def __init__(self, core, ctx, tag, parts):
        self.loaded, self.all, self.parts = core.sem(f"{tag}_loaded", ctx), 16 * len(parts), []
        self.tile = {}
        for name, shape, source, view in parts:
            if name not in self.tile:
                self.tile[name] = core.sb(f"{tag}_{name}", shape, F32, ctx)
            self.parts.append((view(self.tile[name]), source))

    def start(self, eng):
        for tile, source in self.parts:
            eng.dma_start(tile, source).then_inc(self.loaded, 16)


def low_head_loads(core, ctx, tag, w_q, w_k, w_v, w_o, bias):
    parts = [("raw", [P, 4, P], w, lambda t, n=n: t[:, n, :]) for n, w in enumerate((w_q, w_k, w_v, w_o))]
    parts += [("bias_rows", [P, D], bcast_rows(bias), lambda t: t[:, :])]
    return EarlyLoads(core, ctx, tag, parts)


def constants_phase(core, early):
    nc = core.nc
    with ExitStack() as ctx:
        zero_done = core.sem("const_zero_done", ctx)
        chain = core.sem("const_chain", ctx)
        block = ctx.enter_context(nc.Block())

        @block.sync
        def _(sp):
            early.start(sp)

        @block.vector
        def _(dve):
            nc.vector.memset(core.ident[:, :], 0.0).then_inc(zero_done, 1)
            nc.vector.memset(core.causal[:, :], 0.0).then_inc(zero_done, 1)
            nc.vector.memset(core.eps_pow[:, :], -0.5).then_inc(zero_done, 1)
            dve.wait_ge(chain, 1)
            nc.vector.tensor_copy(core.identb[:, :], core.ident[:, :]).then_inc(zero_done, 1)

        @block.gpsimd
        def _(pool):
            pool.wait_ge(zero_done, 2)
            nc.gpsimd.affine_select(out=core.ident[:, :], in_=core.ident[:, :], compare_op=ALU.not_equal,
                                    fill=1.0, base=0, pattern=[[-1, P]], channel_multiplier=1).then_inc(chain, 1)
            for b in range(2):
                half = core.causal[b * S:(b + 1) * S, :]
                pool.wait_ge(chain, 1 + b)
                nc.gpsimd.affine_select(out=half, in_=half, compare_op=ALU.is_ge, fill=NEG, base=0,
                                        pattern=[[-1, S]], channel_multiplier=1).then_inc(chain, 1)


def low_head_phase(core, tag, x_in, kv_in, x_out, loads, transposed, causal, early):
    nc = core.nc
    cross = kv_in is not None
    with ExitStack() as ctx:
        def sb(name, shape, dt=F32):
            return core.sb(f"{tag}_{name}", shape, dt, ctx)

        def sem(name):
            return core.sem(f"{tag}_{name}", ctx)

        wq, wk, wo = sb("wq", [P, P]), sb("wk", [P, P]), sb("wo", [P, P])
        wv = sb("wv", [P, 2, P])
        head_of = sb("head_of", [P, H0])
        bias_rows = loads.tile["bias_rows"]
        low_head_weights(core, tag, loads, transposed, wq, wk, wv, wo, head_of)

        x_t = sb("x_t", [P, 2, 2, P])
        x_res = sb("x_res", [P, 2, P])
        xT = sb("xT", [P, 2, P])
        qT = sb("qT", [P, 2, P])
        kT = sb("kT", [P, 2, P])
        v_blk = sb("v_blk", [P, 2, 2, P])
        k_diag = sb("k_diag", [P, 2, H0, P])
        prob = sb("prob", [P, 2, H0, S])
        probT = sb("probT", [P, 8, P])
        row_max = sb("row_max", [P, 2, H0])
        row_sum = sb("row_sum", [P, 2, H0])
        inv_sum = sb("inv_sum", [P, 2, H0])
        o_norm = sb("o_norm", [P, 2, P])
        oT = sb("oT", [P, P])
        z = sb("z", [P, 2, P])
        stats = sb("stats", [P, 2, 6])
        mean_var = sb("mean_var", [P, 2, 2])
        rstd = sb("rstd", [P, 2, 1])
        y = sb("y", [P, 2, P])

        ps_x, ps_qkv, ps_o, ps_out = core.bank[0], core.bank[1], core.bank[2], core.bank[3]
        ps_s = [core.bank[4], core.bank[5]]
        ps_t = [core.bank[6], core.bank[7]]

        x_loaded = [sem(f"x_loaded{p}") for p in range(2)]
        res_loaded = [sem(f"res_loaded{p}") for p in range(2)]
        stored = [sem(f"stored{p}") for p in range(2)]
        xt_done, xT_ready = sem("xt_done"), sem("xT_ready")
        qkv_done, qT_ready, kT_ready, v_ready = sem("qkv_done"), sem("qT_ready"), sem("kT_ready"), sem("v_ready")
        kd_ready = sem("kd_ready")
        s_done, max_done, sub_done, exp_done = sem("s_done"), sem("max_done"), sem("sub_done"), sem("exp_done")
        sum_done, inv_done = sem("sum_done"), sem("inv_done")
        t_done, pT_ready, av_done, onorm_done = sem("t_done"), sem("pT_ready"), sem("av_done"), sem("onorm_done")
        ot_done, oT_ready, out_done = sem("ot_done"), sem("oT_ready"), sem("out_done")
        z_done, stats_done, mv_done, rstd_done, y_done = (sem("z_done"), sem("stats_done"), sem("mv_done"),
                                                          sem("rstd_done"), sem("y_done"))
        veps_done, zb_done = sem("veps_done"), sem("zb_done")
        block = ctx.enter_context(nc.Block())

        def slots(eng, slot):
            for i in range(-1, 4):
                slot(i, i // 2, i % 2, lambda j: 0 <= j < NPAIR)
            with eng.Fori(1, NPAIR // 4 - 1) as q:
                for m in range(4):
                    slot(4 * q + m, 2 * q + m // 2, m % 2, lambda j: True)
            for i in range(NPAIR - 4, NPAIR + 3):
                slot(i, i // 2, i % 2, lambda j: 0 <= j < NPAIR)

        def here(on, i, d):
            return on(i + d if isinstance(i, int) else 0)

        @block.sync
        def _(sp):
            def load_x(i, k, par):
                wait(sp, xt_done, i - 1)
                sp.dma_start(x_t[:, par, 0, :], x_in[bass.ds(i, 1), :, :].rearrange("o p d -> p (o d)"))\
                    .then_inc(x_loaded[par], 16)
                if cross:
                    sp.dma_start(x_t[:, par, 1, :], kv_in[bass.ds(i, 1), :, :].rearrange("o p d -> p (o d)"))\
                        .then_inc(x_loaded[par], 16)

            def slot(i, k, par, on):
                if here(on, i, 2):
                    load_x(i + 2, k + 1, par)
                if here(on, i, 0):
                    wait(sp, z_done, i - 1)
                    sp.dma_start(x_res[:, par, :], x_in[bass.ds(i, 1), :, :].rearrange("o p d -> p (o d)"))\
                        .then_inc(res_loaded[par], 16)
                if here(on, i, -3):
                    wait(sp, y_done, i - 2)
                    sp.dma_start(x_out[bass.ds(i - 3, 1), :, :].rearrange("o p d -> p (o d)"), y[:, 1 - par, :])\
                        .then_inc(stored[1 - par], 16)

            load_x(0, 0, 0)
            slots(sp, slot)
            for par in range(2):
                sp.wait_ge(stored[par], 16 * (NPAIR // 2))

        @block.tensor
        def _(pe):
            def scores(i, par, c):
                wait(pe, qT_ready, i + 1)
                wait(pe, kd_ready, 2 * i + 1 + c)
                wait(pe, sub_done, 2 * i - 1 + c)
                if causal:
                    nc.tensor.matmul(ps_s[c][:, :].rearrange("p (h t) -> p h t", h=8), core.identb[:, :],
                                     core.causal[:, None, :].to_broadcast([P, 8, S]), start=True, stop=False)
                for b in range(2):
                    last = nc.tensor.matmul(
                        ps_s[c][b * S:(b + 1) * S, :].rearrange("p (h t) -> p h t", h=8),
                        qT[:, par, b * S:(b + 1) * S], k_diag[:, par, 8 * c:8 * c + 8, b * S:(b + 1) * S],
                        start=not causal, stop=True)
                last.then_inc(s_done, 1)

            def slot(i, k, par, on):
                if here(on, i, 1):
                    wait(pe, x_loaded[1 - par], (32 if cross else 16) * (k + par + 1))
                    wait(pe, xT_ready, i + 1)
                    for m in range(2 if cross else 1):
                        last = nc.tensor.transpose(ps_x[:, m * P:(m + 1) * P], x_t[:, 1 - par, m, :], core.ident[:, :])
                    last.then_inc(xt_done, 1)
                if here(on, i, 0):
                    scores(i, par, 0)
                if here(on, i, 1):
                    wait(pe, xT_ready, i + 2)
                    wait(pe, v_ready, i + 1)
                    kv = xT[:, 1 if cross else 0, :]
                    nc.tensor.matmul(ps_qkv[:, 0:P], wq[:, :], xT[:, 0, :], start=True, stop=True)
                    nc.tensor.matmul(ps_qkv[:, P:2 * P], wk[:, :], kv, start=True, stop=True)
                    for b in range(2):
                        for odd in range(2):
                            last = nc.tensor.matmul(ps_qkv[odd * S:(odd + 1) * S, (2 + b) * P:(3 + b) * P],
                                                    kv[:, b * S:(b + 1) * S], wv[:, odd, :], start=True, stop=True)
                    last.then_inc(qkv_done, 1)
                if here(on, i, 0):
                    scores(i, par, 1)
                if here(on, i, -2):
                    wait(pe, onorm_done, i - 1)
                    wait(pe, z_done, i - 2)
                    nc.tensor.transpose(ps_out[:, 0:P], o_norm[:, par, :], core.ident[:, :]).then_inc(ot_done, 1)
                if here(on, i, -1):
                    wait(pe, exp_done, 2 * i)
                    wait(pe, pT_ready, 2 * i - 2)
                    for c in range(2):
                        for hp in range(4):
                            src = prob[:, 1 - par, 8 * c + 2 * hp:8 * c + 2 * hp + 2, :].rearrange("p h t -> p (h t)")
                            last = nc.tensor.transpose(ps_t[c][:, hp * P:(hp + 1) * P], src, core.ident[:, :])
                        last.then_inc(t_done, 1)
                if here(on, i, -2):
                    wait(pe, oT_ready, i - 1)
                    nc.tensor.matmul(ps_out[:, P:2 * P], oT[:, :], wo[:, :], start=True, stop=True)\
                        .then_inc(out_done, 1)
                if here(on, i, -1):
                    wait(pe, onorm_done, i - 1)
                    wait(pe, v_ready, i)
                    for hp in range(8):
                        if hp % 4 == 0:
                            wait(pe, pT_ready, 2 * i - 1 + hp // 4)
                        for b in range(2):
                            last = nc.tensor.matmul(ps_o[b * S:(b + 1) * S, 16 * hp:16 * hp + 16],
                                                    probT[:, hp, b * S:(b + 1) * S],
                                                    v_blk[:, 1 - par, b, 16 * hp:16 * hp + 16], start=True, stop=True)
                    last.then_inc(av_done, 1)

            slots(pe, slot)

        @block.scalar
        def _(act):
            def slot(i, k, par, on):
                if here(on, i, 1):
                    wait(act, xt_done, i + 2)
                    wait(act, qkv_done, i + 1)
                    n = 2 if cross else 1
                    nc.scalar.activation(xT[:, 0:n, :].rearrange("p m t -> p (m t)"), ps_x[:, 0:n * P], ACT.Copy)\
                        .then_inc(xT_ready, 1)
                if here(on, i, -2):
                    wait(act, ot_done, i - 1)
                    wait(act, out_done, i - 2)
                    nc.scalar.activation(oT[:, :], ps_out[:, 0:P], ACT.Copy).then_inc(oT_ready, 1)
                if here(on, i, 1):
                    wait(act, qkv_done, i + 2)
                    wait(act, s_done, 2 * i)
                    nc.scalar.activation(kT[:, 1 - par, :], ps_qkv[:, P:2 * P], ACT.Copy).then_inc(kT_ready, 1)
                    nc.scalar.activation(qT[:, 1 - par, :], ps_qkv[:, 0:P], ACT.Copy, scale=float(HD0) ** -0.5)\
                        .then_inc(qT_ready, 1)
                if here(on, i, -1):
                    wait(act, av_done, i - 1)
                    for c in range(2):
                        wait(act, t_done, 2 * i - 1 + c)
                        nc.scalar.activation(probT[:, 4 * c:4 * c + 4, :].rearrange("p h e -> p (h e)"), ps_t[c][:, :],
                                             ACT.Copy).then_inc(pT_ready, 1)
                if here(on, i, 0):
                    for c in range(2):
                        wait(act, sub_done, 2 * i + 1 + c)
                        half = prob[:, par, 8 * c:8 * c + 8, :].rearrange("p h t -> p (h t)")
                        nc.scalar.activation(half, half, ACT.Exp).then_inc(exp_done, 1)
                if here(on, i, 1):
                    wait(act, av_done, i)
                    nc.scalar.activation(v_blk[:, 1 - par, :, :].rearrange("p b e -> p (b e)"), ps_qkv[:, 2 * P:4 * P],
                                         ACT.Copy).then_inc(v_ready, 1)

            for weights in early:
                weights.start(act)
            slots(act, slot)

        @block.vector
        def _(dve):
            def slot(i, k, par, on):
                if here(on, i, -2):
                    wait(dve, av_done, i - 1)
                    wait(dve, inv_done, i - 1)
                    wait(dve, ot_done, i - 3)
                    nc.vector.tensor_tensor(o_norm[:, par, :].rearrange("p (h e) -> p h e", h=H0),
                                            ps_o[:, 0:P].rearrange("p (h e) -> p h e", h=H0),
                                            inv_sum[:, par, :, None].to_broadcast([P, H0, HD0]), ALU.mult)\
                        .then_inc(onorm_done, 1)
                if here(on, i, 0):
                    for c in range(2):
                        half = ps_s[c][:, :].rearrange("p (h t) -> p h t", h=8)
                        wait(dve, s_done, 2 * i + 1 + c)
                        nc.vector.tensor_reduce(row_max[:, par, 8 * c:8 * c + 8], half, AX.X, ALU.max)\
                            .then_inc(max_done, 1)
                        if c == 0:
                            wait(dve, t_done, 2 * i - 2)
                        wait(dve, max_done, 2 * i + 1 + c)
                        nc.vector.tensor_tensor(prob[:, par, 8 * c:8 * c + 8, :], half,
                                                row_max[:, par, 8 * c:8 * c + 8, None].to_broadcast([P, 8, S]),
                                                ALU.subtract).then_inc(sub_done, 1)
                if here(on, i, -1):
                    wait(dve, exp_done, 2 * i)
                    nc.vector.tensor_reduce(row_sum[:, 1 - par, :], prob[:, 1 - par, :, :], AX.X, ALU.add)\
                        .then_inc(sum_done, 1)
                if here(on, i, -2):
                    wait(dve, zb_done, i - 1)
                    wait(dve, out_done, i - 1)
                    nc.vector.tensor_tensor(z[:, par, :], z[:, par, :], ps_out[:, P:2 * P], ALU.add).then_inc(z_done, 1)
                if here(on, i, -1):
                    wait(dve, sum_done, i)
                    nc.vector.reciprocal(inv_sum[:, 1 - par, :], row_sum[:, 1 - par, :]).then_inc(inv_done, 1)
                if here(on, i, -2):
                    wait(dve, z_done, i - 1)
                    nc.vector.bn_stats(stats[:, par, :], z[:, par, :]).then_inc(stats_done, 1)
                    wait(dve, stats_done, i - 1)
                if here(on, i, -3):
                    wait(dve, rstd_done, i - 2)
                    wait(dve, stored[1 - par], 16 * (k - 2 + par))
                    nc.vector.tensor_scalar(y[:, 1 - par, :], z[:, 1 - par, :], mean_var[:, 1 - par, 0:1],
                                            rstd[:, 1 - par, :], ALU.subtract, ALU.mult).then_inc(y_done, 1)
                if here(on, i, -2):
                    nc.vector.bn_aggr(mean_var[:, par, :], stats[:, par, :]).then_inc(mv_done, 1)
                    wait(dve, mv_done, i - 1)
                    nc.vector.tensor_scalar(rstd[:, par, :], mean_var[:, par, 1:2], EPS, None, ALU.add)\
                        .then_inc(veps_done, 1)

            slots(dve, slot)

        @block.gpsimd
        def _(pool):
            def slot(i, k, par, on):
                if here(on, i, -2):
                    wait(pool, res_loaded[par], 16 * k)
                    wait(pool, y_done, i - 3)
                    nc.gpsimd.tensor_tensor(z[:, par, :], x_res[:, par, :], bias_rows[:, :], ALU.add)\
                        .then_inc(zb_done, 1)
                if here(on, i, 1):
                    wait(pool, kT_ready, i + 2)
                    for c in range(2):
                        wait(pool, s_done, 2 * i - 1 + c)
                        heads = slice(8 * c, 8 * c + 8)
                        nc.gpsimd.tensor_tensor(k_diag[:, 1 - par, heads, :],
                                                kT[:, 1 - par, None, :].to_broadcast([P, 8, P]),
                                                head_of[:, heads, None].to_broadcast([P, 8, P]), ALU.mult)\
                            .then_inc(kd_ready, 1)
                if here(on, i, -2):
                    wait(pool, veps_done, i - 1)
                    nc.gpsimd.tensor_tensor(rstd[:, par, :], rstd[:, par, :], core.eps_pow[:, :], ALU.pow)\
                        .then_inc(rstd_done, 1)

            slots(pool, slot)


def low_head_weights(core, tag, loads, transposed, wq, wk, wv, wo, head_of):
    nc = core.nc
    with ExitStack() as own:
        raw, loaded = loads.tile["raw"], loads.loaded
        flat_done = core.sem(f"{tag}_w_flat", own)
        copied = core.sem(f"{tag}_w_copied", own)
        head_done = core.sem(f"{tag}_head_done", own)
        block = own.enter_context(nc.Block())

        @block.tensor
        def _(pe):
            if transposed:
                pe.wait_ge(loaded, loads.all)
                for n in range(4):
                    last = nc.tensor.transpose(core.bank[0][:, n * P:(n + 1) * P], raw[:, n, :], core.ident[:, :])
                last.then_inc(flat_done, 1)

        @block.vector
        def _(dve):
            nc.vector.memset(wv[:, :, :], 0.0).then_inc(copied, 1)
            nc.vector.memset(head_of[:, :], 1.0).then_inc(head_done, 1)
            dve.wait_ge(loaded, loads.all)
            dve.wait_ge(copied, 1)
            if transposed:
                dve.wait_ge(flat_done, 1)
            src = [core.bank[0][:, n * P:(n + 1) * P] if transposed else raw[:, n, :] for n in range(4)]
            for dst, n in ((wq, 0), (wk, 1), (wo, 3)):
                nc.vector.tensor_copy(dst[:, :], src[n]).then_inc(copied, 1)
            for odd in range(2):
                nc.vector.tensor_copy(
                    wv[:, odd, :].rearrange("p (g o e) -> p g o e", o=2, e=HD0)[:, :, odd, :],
                    src[2].rearrange("p (g o e) -> p g o e", o=2, e=HD0)[:, :, odd, :]).then_inc(copied, 1)

        @block.gpsimd
        def _(pool):
            pool.wait_ge(head_done, 1)
            nc.gpsimd.affine_select(out=head_of[:, :], in_=head_of[:, :], compare_op=ALU.is_ge, fill=0.0,
                                    base=0, pattern=[[-HD0, H0]], channel_multiplier=1).then_inc(head_done, 1)
            pool.wait_ge(head_done, 2)
            nc.gpsimd.affine_select(out=head_of[:, :], in_=head_of[:, :], compare_op=ALU.is_ge, fill=0.0,
                                    base=HD0 - 1, pattern=[[HD0, H0]], channel_multiplier=-1)\
                .then_inc(head_done, 1)



def feed_forward_loads(core, ctx, w_fc, w_proj, u, v, fast_b, gate):
    NT, R = FF // P, u.shape[1]
    whole = lambda t: t[:, :]
    return (EarlyLoads(core, ctx, "ffn_w", [
        ("w", [P, 2 * NT, P], w_fc.rearrange("(t p) d -> p t d", p=P), lambda t: t[:, 0:NT, :]),
        ("w", [P, 2 * NT, P], w_proj, lambda t: t[:, NT:2 * NT, :].rearrange("p t d -> p (t d)"))]),
            EarlyLoads(core, ctx, "ffn_lr", [
                ("u", [P, NT, R], u.rearrange("(t p) r -> p t r", p=P), lambda t: t[:, :, :]),
                ("v", [R, D], v, whole), ("fb", [R, R], fast_b, whole), ("gate", [P, 1], bcast_rows(gate), whole)]))


def feed_forward_phase(core, x_in, x_out, loads):
    nc = core.nc
    NT = FF // P
    GP = 2
    NG = NPAIR // GP
    ternary, low_rank = loads
    R = low_rank.tile["fb"].shape[1]
    with ExitStack() as ctx:
        def sb(name, shape, dt=F32):
            return core.sb(f"ffn_{name}", shape, dt, ctx)

        def sem(name):
            return core.sem(f"ffn_{name}", ctx)

        w_hidden, w_out = sb("w_hidden", [P, FF]), sb("w_out", [P, NT, P])

        with ExitStack() as own:
            def osb(name, shape):
                return core.sb(f"ffnw_{name}", shape, F32, own)

            w, sc = ternary.tile["w"], osb("sc", [P, 2 * NT])
            thr, nthr = osb("thr", [P, 2 * NT]), osb("nthr", [P, 2 * NT])
            above, below = osb("above", [P, 2 * NT, P]), osb("below", [P, 2 * NT, P])
            proj_sum, gate_sb = osb("proj_sum", [P, 1]), low_rank.tile["gate"]
            u_sb, v_sb, fb_sb = low_rank.tile["u"], low_rank.tile["v"], low_rank.tile["fb"]
            uT, fbT, m_sb = osb("uT", [R, FF]), osb("fbT", [R, R]), osb("m", [R, D])
            loaded, lr_loaded = ternary.loaded, low_rank.loaded
            q = core.sem("ffnw_quant", own)
            ut_done, m_done, lr_done, wt_done = (core.sem("ffnw_ut_done", own), core.sem("ffnw_m_done", own),
                                                 core.sem("ffnw_lr_done", own), core.sem("ffnw_wt_done", own))
            copied, w_ready = core.sem("ffnw_copied", own), core.sem("ffnw_ready", own)
            block = own.enter_context(nc.Block())

            @block.vector
            def _(dve):
                count = [0]

                def step(ins):
                    ins.then_inc(q, 1)
                    count[0] += 1
                    dve.wait_ge(q, count[0])

                wide = [P, 2 * NT, P]
                dve.wait_ge(loaded, ternary.all)
                step(nc.vector.tensor_reduce(sc[:, :], w[:, :, :], AX.X, ALU.add, apply_absolute_value=True))
                step(nc.vector.tensor_reduce(proj_sum[:, :], sc[:, NT:2 * NT], AX.X, ALU.add))
                step(nc.vector.tensor_scalar(sc[:, 0:NT], sc[:, 0:NT], 1.0 / D, 1e-5, ALU.mult, ALU.max))
                step(nc.vector.tensor_scalar(sc[:, NT:2 * NT], proj_sum[:, :].to_broadcast([P, NT]), 1.0 / FF, 1e-5,
                                             ALU.mult, ALU.max))
                step(nc.vector.tensor_scalar(thr[:, :], sc[:, :], 0.5, None, ALU.mult))
                step(nc.vector.tensor_scalar(nthr[:, :], sc[:, :], -0.5, None, ALU.mult))
                step(nc.vector.tensor_tensor(above[:, :, :], w[:, :, :], thr[:, :, None].to_broadcast(wide), ALU.is_gt))
                step(nc.vector.tensor_tensor(below[:, :, :], w[:, :, :], nthr[:, :, None].to_broadcast(wide), ALU.is_lt))
                step(nc.vector.tensor_tensor(above[:, :, :], above[:, :, :], below[:, :, :], ALU.subtract))
                step(nc.vector.tensor_tensor(below[:, :, :], above[:, :, :], w[:, :, :], ALU.subtract))
                step(nc.vector.tensor_tensor(above[:, :, :], w[:, :, :], below[:, :, :], ALU.add))
                step(nc.vector.tensor_tensor(w[:, :, :], above[:, :, :], sc[:, :, None].to_broadcast(wide), ALU.mult))
                dve.wait_ge(copied, 5)
                dve.wait_ge(lr_done, 1)
                dve.wait_ge(lr_loaded, low_rank.all)
                nc.vector.scalar_tensor_tensor(out=w_hidden[:, :], in0=core.bank[3][:, :], scalar=gate_sb[:, :],
                                               in1=above[:, 0:NT, :].rearrange("p t d -> p (t d)"), op0=ALU.mult,
                                               op1=ALU.add).then_inc(w_ready, 1)

            @block.tensor
            def _(pe):
                pe.wait_ge(lr_loaded, low_rank.all)
                for t in range(NT):
                    nc.tensor.transpose(core.bank[0][0:R, t * P:(t + 1) * P], u_sb[:, t, :], core.ident[:, :])
                nc.tensor.transpose(core.bank[1][0:R, 0:R], fb_sb[:, :], core.ident[0:R, 0:R]).then_inc(ut_done, 1)
                pe.wait_ge(copied, 2)
                nc.tensor.matmul(core.bank[2][0:R, 0:D], fbT[:, :], v_sb[:, :], start=True, stop=True).then_inc(m_done, 1)
                pe.wait_ge(copied, 3)
                nc.tensor.matmul(core.bank[3][:, :], m_sb[:, :], uT[:, :], start=True, stop=True).then_inc(lr_done, 1)
                pe.wait_ge(q, 12)
                for t in range(2 * NT):
                    last = nc.tensor.transpose(core.bank[4 + t // NT][:, t % NT * P:(t % NT + 1) * P], w[:, t, :],
                                               core.ident[:, :])
                last.then_inc(wt_done, 1)

            @block.scalar
            def _(act):
                act.wait_ge(ut_done, 1)
                nc.scalar.activation(uT[:, :], core.bank[0][0:R, :], ACT.Copy).then_inc(copied, 1)
                nc.scalar.activation(fbT[:, :], core.bank[1][0:R, 0:R], ACT.Copy).then_inc(copied, 1)
                act.wait_ge(m_done, 1)
                nc.scalar.activation(m_sb[:, :], core.bank[2][0:R, 0:D], ACT.Copy).then_inc(copied, 1)
                act.wait_ge(wt_done, 1)
                nc.scalar.activation(above[:, 0:NT, :].rearrange("p t d -> p (t d)"), core.bank[4][:, :], ACT.Copy)\
                    .then_inc(copied, 1)
                nc.scalar.activation(w_out[:, :, :].rearrange("p t d -> p (t d)"), core.bank[5][:, :], ACT.Copy)\
                    .then_inc(copied, 1)

        x = sb("x", [P, 4, GP, P])
        xT = sb("xT", [P, 2, GP * P])
        r = sb("r", [P, 2, NT, GP * P])
        r2 = sb("r2", [P, 2, NT, GP * P])
        z = sb("z", [P, 2, GP, P])
        stats = sb("stats", [P, GP, 6])
        mean_var = sb("mean_var", [P, 2, GP, 2])
        rstd = sb("rstd", [P, 2, GP])
        y = sb("y", [P, 2, GP, P])
        ps_x, ps_out = core.bank[0], core.bank[1]
        ps_h = [core.bank[2], core.bank[3], core.bank[4], core.bank[5]]
        x_loaded = [sem(f"x_loaded{p}") for p in range(4)]
        stored = [sem(f"stored{p}") for p in range(2)]
        xt_done, xT_ready, h_done, relu_done, sq_done, out_done = (sem("xt_done"), sem("xT_ready"), sem("h_done"),
                                                                   sem("relu_done"), sem("sq_done"), sem("out_done"))
        z_done, stats_done, mv_done, veps_done, rstd_done, y_done = (
            sem("z_done"), sem("stats_done"), sem("mv_done"), sem("veps_done"), sem("rstd_done"), sem("y_done"))
        block = ctx.enter_context(nc.Block())

        def slots(eng, slot):
            for g in range(-1, 4):
                slot(g, g // 4, g % 4, lambda j: 0 <= j < NG)
            with eng.Fori(1, NG // 4 - 1) as k:
                for m in range(4):
                    slot(4 * k + m, k, m, lambda j: True)
            for g in range(NG - 4, NG + 2):
                slot(g, g // 4, g % 4, lambda j: 0 <= j < NG)

        def here(on, g, d):
            return on(g + d if isinstance(g, int) else 0)

        @block.sync
        def _(sp):
            def load(g, m):
                wait(sp, z_done, g - 3)
                sp.dma_start(x[:, m, :, :], x_in[bass.ds(GP * g, GP), :, :].rearrange("n p d -> p n d"))\
                    .then_inc(x_loaded[m], 16)

            def slot(g, k, m, on):
                if here(on, g, 2):
                    load(g + 2, (m + 2) % 4)
                if here(on, g, -2):
                    wait(sp, y_done, g - 1)
                    sp.dma_start(x_out[bass.ds(GP * (g - 2), GP), :, :].rearrange("n p d -> p n d"),
                                 y[:, m % 2, :, :]).then_inc(stored[m % 2], 16)

            load(0, 0)
            slots(sp, slot)
            for par in range(2):
                sp.wait_ge(stored[par], 16 * (NG // 2))

        @block.tensor
        def _(pe):
            def slot(g, k, m, on):
                if here(on, g, 1):
                    wait(pe, x_loaded[(m + 1) % 4], 16 * (k + 1 + (m + 1) // 4))
                    wait(pe, xT_ready, g + 1)
                    for n in range(GP):
                        last = nc.tensor.transpose(ps_x[:, n * P:(n + 1) * P], x[:, (m + 1) % 4, n, :], core.ident[:, :])
                    last.then_inc(xt_done, 1)
                if here(on, g, 0):
                    wait(pe, xT_ready, g + 1)
                    for t in range(NT):
                        wait(pe, relu_done, NT * (g - 1) + t + 1)
                        nc.tensor.matmul(ps_h[t][:, 0:GP * P], w_hidden[:, t * P:(t + 1) * P], xT[:, m % 2, :],
                                         start=True, stop=True).then_inc(h_done, 1)
                if here(on, g, -1):
                    wait(pe, sq_done, NT * g)
                    wait(pe, z_done, g - 1)
                    for n in range(GP):
                        for t in range(NT):
                            last = nc.tensor.matmul(ps_out[:, n * P:(n + 1) * P], r2[:, (m + 1) % 2, t, n * P:(n + 1) * P],
                                                    w_out[:, t, :], start=(t == 0), stop=(t == NT - 1))
                    last.then_inc(out_done, 1)

            slots(pe, slot)

        @block.scalar
        def _(act):
            def slot(g, k, m, on):
                if here(on, g, 1):
                    wait(act, xt_done, g + 2)
                    wait(act, h_done, NT * g)
                    nc.scalar.activation(xT[:, (m + 1) % 2, :], ps_x[:, 0:GP * P], ACT.Copy).then_inc(xT_ready, 1)
                if here(on, g, 0):
                    wait(act, sq_done, NT * (g - 1))
                    for t in range(NT):
                        wait(act, h_done, NT * g + t + 1)
                        nc.scalar.activation(r[:, m % 2, t, :], ps_h[t][:, 0:GP * P], ACT.Relu).then_inc(relu_done, 1)

            slots(act, slot)

        @block.vector
        def _(dve):
            def slot(g, k, m, on):
                if here(on, g, 0):
                    wait(dve, out_done, g - 1)
                    for t in range(NT):
                        wait(dve, relu_done, NT * g + t + 1)
                        nc.vector.tensor_tensor(r2[:, m % 2, t, :], r[:, m % 2, t, :], r[:, m % 2, t, :], ALU.mult)\
                            .then_inc(sq_done, 1)
                if here(on, g, -1):
                    o = (m + 1) % 2
                    wait(dve, out_done, g)
                    nc.vector.tensor_tensor(z[:, o, :, :], x[:, (m + 3) % 4, :, :],
                                            ps_out[:, 0:GP * P].rearrange("p (n d) -> p n d", n=GP), ALU.add)\
                        .then_inc(z_done, 1)
                    wait(dve, z_done, g)
                    for n in range(GP):
                        last = nc.vector.bn_stats(stats[:, n, :], z[:, o, n, :])
                    last.then_inc(stats_done, 1)
                    wait(dve, stats_done, g)
                if here(on, g, -2):
                    wait(dve, rstd_done, g - 1)
                    wait(dve, stored[m % 2], 16 * (2 * k + m // 2 - 1))
                    for n in range(GP):
                        last = nc.vector.tensor_scalar(y[:, m % 2, n, :], z[:, m % 2, n, :], mean_var[:, m % 2, n, 0:1],
                                                       rstd[:, m % 2, n:n + 1], ALU.subtract, ALU.mult)
                    last.then_inc(y_done, 1)
                if here(on, g, -1):
                    for n in range(GP):
                        last = nc.vector.bn_aggr(mean_var[:, o, n, :], stats[:, n, :])
                    last.then_inc(mv_done, 1)
                    wait(dve, mv_done, g)
                    nc.vector.tensor_scalar(rstd[:, o, :], mean_var[:, o, :, 1], EPS, None, ALU.add)\
                        .then_inc(veps_done, 1)

            slots(dve, slot)

        @block.gpsimd
        def _(pool):
            def slot(g, k, m, on):
                if here(on, g, -1):
                    wait(pool, veps_done, g)
                    nc.gpsimd.tensor_tensor(rstd[:, (m + 1) % 2, :], rstd[:, (m + 1) % 2, :],
                                            core.eps_pow[:, :].to_broadcast([P, GP]), ALU.pow).then_inc(rstd_done, 1)

            slots(pool, slot)


class EarlyWeights:

    def __init__(self, core, ctx, tag, pairs_of_heads, w_q, w_k, w_v, w_o):
        self.raw = core.sb(f"{tag}_raw_qkv", [P, 3, pairs_of_heads, P], F32, ctx)
        self.wo = core.sb(f"{tag}_raw_o", [P, H1 // 2, D], F32, ctx)
        self.loaded = [core.sem(f"{tag}_w_loaded{n}", ctx) for n in range(3)]
        self.wo_loaded = core.sem(f"{tag}_wo_loaded", ctx)
        self.sources = (w_q, w_k, w_v, w_o)

    def start(self, eng):
        for n, w in enumerate(self.sources[:3]):
            eng.dma_start(self.raw[:, n, :, :].rearrange("p t d -> p (t d)"), w).then_inc(self.loaded[n], 16)
        eng.dma_start(self.wo[:, :, :], self.sources[3].rearrange("(t p) d -> p t d", p=P)).then_inc(self.wo_loaded, 16)


def head_product_weights(core, tag, pairs_of_heads, early, scores_first, w_score, w_vo, lam=None):
    nc = core.nc
    NT = pairs_of_heads
    NQ = NT // 4
    with ExitStack() as own:
        def sb(name, shape):
            return core.sb(f"{tag}w_{name}", shape, F32, own)

        def sem(name):
            return core.sem(f"{tag}w_{name}", own)

        raw, wo, loaded, wo_loaded = early.raw, early.wo, early.loaded, early.wo_loaded
        flat = sb("flat", [P, 3, NT, P])
        t_done, t_copied, prod_done, prod_copied = sem("t_done"), sem("t_copied"), sem("prod_done"), sem("prod_copied")
        if lam is not None:
            lam_in, lam_prod = sb("lam_in", [P, 4, HD1]), sb("lam_prod", [P, 2, HD1])
            lam_dot, lam_exp, vo_scale = sb("lam_dot", [P, 2]), sb("lam_exp", [P, 2]), sb("vo_scale", [P, 1])
            lam_loaded, lam_dot_done, lam_exp_done, lam_done = (sem("lam_loaded"), sem("lam_dot_done"),
                                                                sem("lam_exp_done"), sem("lam_done"))
        block = own.enter_context(nc.Block())
        prods = [("score", q, par) for q in range(NQ) for par in range(2)]
        prods += [("vo", q, par) for q in range(NQ) for par in range(2)]

        @block.sync
        def _(sp):
            if lam is not None:
                for n, v in enumerate(lam):
                    sp.dma_start(lam_in[:, n, :], bcast_rows(v)).then_inc(lam_loaded, 16)
                sp.wait_ge(lam_loaded, 64)

        @block.tensor
        def _(pe):
            for n in range(3):
                pe.wait_ge(loaded[n], 16)
                for q in range(NQ):
                    m = n * NQ + q
                    wait(pe, t_copied, m - 3)
                    for t in range(4):
                        last = nc.tensor.transpose(core.bank[m % 4][:, t * P:(t + 1) * P], raw[:, n, 4 * q + t, :],
                                                   core.ident[:, :])
                    last.then_inc(t_done, 1)
            pe.wait_ge(t_copied, 3 * NQ)
            pe.wait_ge(wo_loaded, 16)
            for m, (kind, q, par) in enumerate(prods):
                wait(pe, prod_copied, m - 3)
                rows = slice(par * HD1, (par + 1) * HD1)
                for t in range(4):
                    hp = 4 * q + t
                    if kind == "vo":
                        left, right = flat[rows, 2, hp, :], wo[rows, hp % (H1 // 2), :]
                    elif scores_first == "k":
                        left, right = flat[rows, 1, hp, :], flat[rows, 0, hp, :]
                    else:
                        left, right = flat[rows, 0, hp, :], flat[rows, 1, hp, :]
                    last = nc.tensor.matmul(core.bank[4 + m % 4][:, t * P:(t + 1) * P], left, right, start=True,
                                            stop=True)
                last.then_inc(prod_done, 1)

        @block.scalar
        def _(act):
            if lam is not None:
                act.wait_ge(lam_dot_done, 1)
                nc.scalar.activation(lam_exp[:, :], lam_dot[:, :], ACT.Exp).then_inc(lam_exp_done, 1)
            for m in range(3 * NQ):
                act.wait_ge(t_done, m + 1)
                nc.scalar.activation(flat[:, m // NQ, m % NQ * 4:m % NQ * 4 + 4, :].rearrange("p t d -> p (t d)"),
                                     core.bank[m % 4][:, :], ACT.Copy).then_inc(t_copied, 1)

        @block.vector
        def _(dve):
            if lam is not None:
                dve.wait_ge(lam_loaded, 64)
                nc.vector.tensor_tensor(lam_prod[:, :, :], lam_in[:, 0:2, :], lam_in[:, 2:4, :], ALU.mult)\
                    .then_inc(lam_done, 1)
                dve.wait_ge(lam_done, 1)
                nc.vector.tensor_reduce(lam_dot[:, :], lam_prod[:, :, :], AX.X, ALU.add).then_inc(lam_dot_done, 1)
                dve.wait_ge(lam_exp_done, 1)
                nc.vector.tensor_tensor(vo_scale[:, :], lam_exp[:, 0:1], lam_exp[:, 1:2], ALU.subtract)\
                    .then_inc(lam_done, 1)
                dve.wait_ge(lam_done, 2)
                nc.vector.tensor_scalar(vo_scale[:, :], vo_scale[:, :], 0.8, -(1.0 - 0.8), ALU.add, ALU.mult)\
                    .then_inc(lam_done, 1)
                dve.wait_ge(lam_done, 3)
            for m, (kind, q, par) in enumerate(prods):
                dve.wait_ge(prod_done, m + 1)
                src = core.bank[4 + m % 4][:, :].rearrange("p (t d) -> p t d", t=4)
                if kind == "score":
                    dst = w_score[:, :, :].rearrange("p (t o) d -> p t o d", o=2)[:, 4 * q:4 * q + 4, par, :]
                    by = float(HD1) ** -0.5
                else:
                    dst = w_vo[:, par, 4 * q:4 * q + 4, :]
                    by = 1.0 if lam is None else (1.0 - 0.8 if q < NQ // 2 else vo_scale[:, :])
                nc.vector.tensor_scalar(dst, src, by, None, ALU.mult).then_inc(prod_copied, 1)


def differential_attention_phase(core, x_in, x_out, cat_out, ctx_in, a, early):
    nc = core.nc
    NH = 2 * H1
    with ExitStack() as ctx:
        def sb(name, shape, dt=F32):
            return core.sb(f"diff_{name}", shape, dt, ctx)

        def sem(name):
            return core.sem(f"diff_{name}", ctx)

        w_score, w_vo = sb("w_score", [P, NH, D]), sb("w_vo", [P, 2, NH // 2, D])
        head_product_weights(core, "diff", NH // 2, early, "k", w_score, w_vo,
                             [a["L1_attn_lq1"], a["L1_attn_lq2"], a["L1_attn_lk1"], a["L1_attn_lk2"]])

        gb = sb("gb", [P, 4, D])
        x_t, x_res, ctx_t = sb("x_t", [P, D]), sb("x_res", [P, D]), sb("ctx_t", [P, D])
        xT = sb("xT", [P, P])
        keys = sb("keys", [P, 2, 8, P])
        vals = sb("vals", [P, 4, 2, 4, D])
        prob = sb("prob", [P, 2, 8, S])
        probT = sb("probT", [P, 4, P])
        row_max, row_sum, inv_sum = sb("row_max", [P, 2, 8]), sb("row_sum", [P, 2, 8]), sb("inv_sum", [P, 2, 8])
        z, y, lat, ctx_n = sb("z", [P, D]), sb("y", [P, D]), sb("lat", [P, D]), sb("ctx_n", [P, D])
        stats, mean_var, rstd = sb("stats", [P, 3, 6]), sb("mean_var", [P, 3, 2]), sb("rstd", [P, 3])

        ps_g, ps_v = [core.bank[0], core.bank[1]], [core.bank[2], core.bank[3]]
        ps_s, ps_t, ps_o, ps_x = core.bank[4], core.bank[5], core.bank[6], core.bank[7]

        gb_loaded, x_loaded, res_loaded, ctx_loaded = (sem("gb_loaded"), sem("x_loaded"), sem("res_loaded"),
                                                       sem("ctx_loaded"))
        y_stored, lat_stored, ctx_stored = sem("y_stored"), sem("lat_stored"), sem("ctx_stored")
        xt_done, xT_ready = sem("xt_done"), sem("xT_ready")
        g_done, g_copied, v_done, v_copied = sem("g_done"), sem("g_copied"), sem("v_done"), sem("v_copied")
        s_done, max_done, sub_done, exp_done = sem("s_done"), sem("max_done"), sem("sub_done"), sem("exp_done")
        sum_done, inv_done, p_done = sem("sum_done"), sem("inv_done"), sem("p_done")
        t_done, pT_copied, av_done = sem("t_done"), sem("pT_copied"), sem("av_done")
        z_done, y_done, lat_n_done, lat_g_done, lat_done = (sem("z_done"), sem("y_done"), sem("lat_n_done"),
                                                            sem("lat_g_done"), sem("lat_done"))
        ctx_n_done, ctx_g_done, ctx_done = sem("ctx_n_done"), sem("ctx_g_done"), sem("ctx_done")
        st_done = [sem(f"st_done{n}") for n in range(3)]
        mv_done = [sem(f"mv_done{n}") for n in range(3)]
        veps_done = [sem(f"veps_done{n}") for n in range(3)]
        rstd_done = [sem(f"rstd_done{n}") for n in range(3)]
        block = ctx.enter_context(nc.Block())

        def slots(eng, slot):
            for c in range(4):
                slot(0, c, True, False)
            with eng.Fori(1, NPAIR - 1) as i:
                for c in range(4):
                    slot(i, c, True, True)
            for c in range(4):
                slot(NPAIR - 1, c, True, True)
            for c in range(4):
                slot(NPAIR, c, False, True)

        def have(n, cur, prev):
            return cur and prev if not isinstance(n, int) else 0 <= n < 4 * NPAIR

        def last_pair(i):
            return isinstance(i, int) and i == NPAIR - 1

        def rows(t, i):
            return t[bass.ds(i, 1), :, :].rearrange("o p d -> p (o d)")

        @block.sync
        def _(sp):
            def store_cat(i, at, tile, sem_):
                for b in range(2):
                    sp.dma_start(cat_out[bass.ds(2 * i + b, 1), at:at + S, :].rearrange("o p d -> p (o d)"),
                                 tile[b * S:(b + 1) * S, :]).then_inc(sem_, 16)

            def pair(i, cur, prev):
                if cur and not last_pair(i):
                    sp.wait_ge(xt_done, i + 1)
                    sp.dma_start(x_t[:, :], rows(x_in, i + 1)).then_inc(x_loaded, 16)
                if cur:
                    wait(sp, z_done, i)
                    sp.dma_start(x_res[:, :], rows(x_in, i)).then_inc(res_loaded, 16)
                    sp.wait_ge(ctx_done, i + 1)
                    store_cat(i, 0, ctx_n, ctx_stored)
                    if not last_pair(i):
                        sp.dma_start(ctx_t[:, :], rows(ctx_in, i + 1)).then_inc(ctx_loaded, 16)
                if prev:
                    sp.wait_ge(y_done, i)
                    sp.dma_start(rows(x_out, i - 1), y[:, :]).then_inc(y_stored, 16)
                    sp.wait_ge(lat_done, i)
                    store_cat(i - 1, S, lat, lat_stored)

            sp.dma_start(x_t[:, :], rows(x_in, 0)).then_inc(x_loaded, 16)
            sp.dma_start(ctx_t[:, :], rows(ctx_in, 0)).then_inc(ctx_loaded, 16)
            for n, name in enumerate(("L1_xattn_g1", "L1_xattn_b1", "L1_xattn_g2", "L1_xattn_b2")):
                sp.dma_start(gb[:, n, :], bcast_rows(a[name])).then_inc(gb_loaded, 16)
            pair(0, True, False)
            with sp.Fori(1, NPAIR - 1) as i:
                pair(i, True, True)
            pair(NPAIR - 1, True, True)
            pair(NPAIR, False, True)
            sp.wait_ge(y_stored, 16 * NPAIR)
            sp.wait_ge(lat_stored, 32 * NPAIR)
            sp.wait_ge(ctx_stored, 32 * NPAIR)

        @block.tensor
        def _(pe):
            def transpose_x(i):
                pe.wait_ge(x_loaded, 16 * (i + 1))
                wait(pe, xT_ready, i)
                nc.tensor.transpose(ps_x[:, 0:P], x_t[:, :], core.ident[:, :]).then_inc(xt_done, 1)

            def slot(i, c, cur, prev):
                n = 4 * i + c
                back = have(n - 2, cur, prev)
                if cur:
                    if c == 3 and not last_pair(i):
                        transpose_x(i + 1)
                    if c == 0:
                        pe.wait_ge(xT_ready, i + 1)
                    for g in range(2):
                        wait(pe, g_copied, 2 * n - 1 + g)
                        for j in range(4):
                            last = nc.tensor.matmul(ps_g[g][:, j * P:(j + 1) * P], w_score[:, 8 * c + 4 * g + j, :],
                                                    xT[:, :], start=True, stop=True)
                        last.then_inc(g_done, 1)
                if back:
                    wait(pe, p_done, n - 1)
                    wait(pe, pT_copied, n - 2)
                    for hp in range(4):
                        src = prob[:, c % 2, 2 * hp:2 * hp + 2, :].rearrange("p h t -> p (h t)")
                        last = nc.tensor.transpose(ps_t[:, hp * P:(hp + 1) * P], src, core.ident[:, :])
                    last.then_inc(t_done, 1)
                if cur:
                    for b in range(2):
                        wait(pe, v_copied, 2 * n - 1 + b)
                        for par in range(2):
                            last = nc.tensor.matmul(ps_v[b][par * S:(par + 1) * S, :], xT[:, b * S:(b + 1) * S],
                                                    w_vo[:, par, 4 * c:4 * c + 4, :].rearrange("p h d -> p (h d)"),
                                                    start=True, stop=True)
                        last.then_inc(v_done, 1)
                    pe.wait_ge(g_copied, 2 * n + 2)
                    wait(pe, sub_done, n)
                    nc.tensor.matmul(ps_s[:, :].rearrange("p (h t) -> p h t", h=8), core.identb[:, :],
                                     core.causal[:, None, :].to_broadcast([P, 8, S]), start=True, stop=False)
                    for b in range(2):
                        last = nc.tensor.matmul(ps_s[b * S:(b + 1) * S, :].rearrange("p (h t) -> p h t", h=8),
                                                xT[:, b * S:(b + 1) * S], keys[:, c % 2, :, b * S:(b + 1) * S],
                                                start=False, stop=True)
                    last.then_inc(s_done, 1)
                if back:
                    wait(pe, pT_copied, n - 1)
                    wait(pe, v_copied, 2 * n - 2)
                    if c == 2:
                        wait(pe, z_done, i)
                    for hp in range(4):
                        for b in range(2):
                            last = nc.tensor.matmul(ps_o[b * S:(b + 1) * S, 0:D], probT[:, hp, b * S:(b + 1) * S],
                                                    vals[:, (c + 2) % 4, b, hp, :], start=(c == 2 and hp == 0),
                                                    stop=(c == 1 and hp == 3))
                    last.then_inc(av_done, 1)

            transpose_x(0)
            slots(pe, slot)

        @block.scalar
        def _(act):
            def copy_xT(i):
                act.wait_ge(xt_done, i + 1)
                wait(act, s_done, 4 * i)
                nc.scalar.activation(xT[:, :], ps_x[:, 0:P], ACT.Copy).then_inc(xT_ready, 1)

            def slot(i, c, cur, prev):
                n = 4 * i + c
                if cur:
                    wait(act, s_done, n - 1)
                    for g in range(2):
                        act.wait_ge(g_done, 2 * n + 1 + g)
                        nc.scalar.activation(keys[:, c % 2, 4 * g:4 * g + 4, :].rearrange("p h t -> p (h t)"),
                                             ps_g[g][:, :], ACT.Copy).then_inc(g_copied, 1)
                if have(n - 1, cur, prev):
                    wait(act, sub_done, n)
                    flat = prob[:, (c + 1) % 2, :, :].rearrange("p h t -> p (h t)")
                    nc.scalar.activation(flat, flat, ACT.Exp).then_inc(exp_done, 1)
                if have(n - 2, cur, prev):
                    wait(act, t_done, n - 1)
                    wait(act, av_done, n - 2)
                    nc.scalar.activation(probT[:, :, :].rearrange("p h t -> p (h t)"), ps_t[:, :], ACT.Copy)\
                        .then_inc(pT_copied, 1)
                if cur:
                    wait(act, av_done, n - 3)
                    for b in range(2):
                        act.wait_ge(v_done, 2 * n + 1 + b)
                        nc.scalar.activation(vals[:, c, b, :, :].rearrange("p h d -> p (h d)"), ps_v[b][:, :],
                                             ACT.Copy).then_inc(v_copied, 1)
                if cur and c == 3 and not last_pair(i):
                    copy_xT(i + 1)

            copy_xT(0)
            slots(act, slot)

        @block.vector
        def _(dve):
            def bn_tail(m, count):
                nc.vector.bn_aggr(mean_var[:, m, :], stats[:, m, :]).then_inc(mv_done[m], 1)
                dve.wait_ge(mv_done[m], count)
                nc.vector.tensor_scalar(rstd[:, m:m + 1], mean_var[:, m, 1:2], EPS, None, ALU.add)\
                    .then_inc(veps_done[m], 1)

            def slot(i, c, cur, prev):
                n = 4 * i + c
                if c == 0 and cur:
                    dve.wait_ge(ctx_loaded, 16 * (i + 1))
                    nc.vector.bn_stats(stats[:, 2, :], ctx_t[:, :]).then_inc(st_done[2], 1)
                    dve.wait_ge(st_done[2], i + 1)
                if c == 2 and prev:
                    dve.wait_ge(st_done[0], i)
                if c == 3 and prev:
                    dve.wait_ge(rstd_done[0], i)
                    wait(dve, y_stored, 16 * (i - 1))
                    nc.vector.tensor_scalar(y[:, :], z[:, :], mean_var[:, 0, 0:1], rstd[:, 0:1], ALU.subtract,
                                            ALU.mult).then_inc(y_done, 1)
                    dve.wait_ge(y_done, i)
                    nc.vector.bn_stats(stats[:, 1, :], y[:, :]).then_inc(st_done[1], 1)
                    dve.wait_ge(st_done[1], i)
                if have(n - 1, cur, prev):
                    wait(dve, exp_done, n)
                    nc.vector.tensor_reduce(row_sum[:, (c + 1) % 2, :], prob[:, (c + 1) % 2, :, :], AX.X, ALU.add)\
                        .then_inc(sum_done, 1)
                    wait(dve, sum_done, n)
                    nc.vector.reciprocal(inv_sum[:, (c + 1) % 2, :], row_sum[:, (c + 1) % 2, :]).then_inc(inv_done, 1)
                    wait(dve, inv_done, n)
                    nc.vector.tensor_tensor(prob[:, (c + 1) % 2, :, :], prob[:, (c + 1) % 2, :, :],
                                            inv_sum[:, (c + 1) % 2, :, None].to_broadcast([P, 8, S]), ALU.mult)\
                        .then_inc(p_done, 1)
                if cur:
                    scores = ps_s[:, :].rearrange("p (h t) -> p h t", h=8)
                    dve.wait_ge(s_done, n + 1)
                    nc.vector.tensor_reduce(row_max[:, c % 2, :], scores, AX.X, ALU.max).then_inc(max_done, 1)
                    wait(dve, t_done, n - 1)
                    dve.wait_ge(max_done, n + 1)
                    nc.vector.tensor_tensor(prob[:, c % 2, :, :], scores,
                                            row_max[:, c % 2, :, None].to_broadcast([P, 8, S]), ALU.subtract)\
                        .then_inc(sub_done, 1)
                if c == 0 and cur:
                    bn_tail(2, i + 1)
                if c == 1 and prev:
                    dve.wait_ge(res_loaded, 16 * i)
                    dve.wait_ge(av_done, 4 * i)
                    nc.vector.tensor_tensor(z[:, :], x_res[:, :], ps_o[:, 0:D], ALU.add).then_inc(z_done, 1)
                    dve.wait_ge(z_done, i)
                    nc.vector.bn_stats(stats[:, 0, :], z[:, :]).then_inc(st_done[0], 1)
                if c == 2 and prev:
                    bn_tail(0, i)
                if c == 3 and prev:
                    bn_tail(1, i)
                    dve.wait_ge(rstd_done[1], i)
                    wait(dve, lat_stored, 32 * (i - 1))
                    nc.vector.tensor_scalar(lat[:, :], y[:, :], mean_var[:, 1, 0:1], rstd[:, 1:2], ALU.subtract,
                                            ALU.mult).then_inc(lat_n_done, 1)
                if c == 1 and cur:
                    dve.wait_ge(rstd_done[2], i + 1)
                    wait(dve, ctx_stored, 32 * i)
                    nc.vector.tensor_scalar(ctx_n[:, :], ctx_t[:, :], mean_var[:, 2, 0:1], rstd[:, 2:3], ALU.subtract,
                                            ALU.mult).then_inc(ctx_n_done, 1)

            slots(dve, slot)

        @block.gpsimd
        def _(pool):
            def power(m, count):
                pool.wait_ge(veps_done[m], count)
                nc.gpsimd.tensor_tensor(rstd[:, m:m + 1], rstd[:, m:m + 1], core.eps_pow[:, :], ALU.pow)\
                    .then_inc(rstd_done[m], 1)

            def scale_shift(tile, m, normed, scaled, done, count):
                pool.wait_ge(normed, count)
                nc.gpsimd.tensor_tensor(tile[:, :], tile[:, :], gb[:, m, :], ALU.mult).then_inc(scaled, 1)
                pool.wait_ge(scaled, count)
                nc.gpsimd.tensor_tensor(tile[:, :], tile[:, :], gb[:, m + 1, :], ALU.add).then_inc(done, 1)

            def slot(i, c, cur, prev):
                if c == 0 and cur:
                    power(2, i + 1)
                if c == 1 and cur:
                    scale_shift(ctx_n, 0, ctx_n_done, ctx_g_done, ctx_done, i + 1)
                if c == 2 and prev:
                    power(0, i)
                if c == 3 and prev:
                    power(1, i)
                    scale_shift(lat, 2, lat_n_done, lat_g_done, lat_done, i)

            pool.wait_ge(gb_loaded, 64)
            slots(pool, slot)


def latent_attention_phase(core, x_in, x_out, cat, mask, a, early, route, xe, ye):
    nc = core.nc
    NCH = 4 * NPAIR
    T = 2 * S
    with ExitStack() as ctx:
        def sb(name, shape, dt=F32):
            return core.sb(f"lat_{name}", shape, dt, ctx)

        def sem(name):
            return core.sem(f"lat_{name}", ctx)

        w_score, w_vo = sb("w_score", [P, H1, D]), sb("w_vo", [P, 2, H1 // 2, D])
        head_product_weights(core, "lat", H1 // 2, early, "q", w_score, w_vo)

        mask_sb, mask_bias = sb("mask", [P, B, S], U8), sb("mask_bias", [P, B, T], BF16)
        c_t, c_v = sb("c_t", [P, 2, D]), sb("c_v", [P, 2, D])
        x_res = sb("x_res", [P, D])
        catT = sb("catT", [P, 2, T])
        query = sb("query", [P, 2, 2, 4, S])
        prob = sb("prob", [P, 2, 4, T])
        probT = sb("probT", [P, 4, P])
        ctxT = sb("ctxT", [P, 4, 2, S])
        row_max, row_sum, inv_sum = sb("row_max", [P, 2, 4]), sb("row_sum", [P, 2, 4]), sb("inv_sum", [P, 2, 4])
        z, y = sb("z", [P, D]), sb("y", [P, D])
        stats, mean_var, rstd = sb("stats", [P, 6]), sb("mean_var", [P, 2]), sb("rstd", [P, 1])

        ps_g, ps_s = [core.bank[0], core.bank[1]], [core.bank[2], core.bank[3]]
        ps_t, ps_c, ps_o, ps_x = core.bank[4], core.bank[5], core.bank[6], core.bank[7]

        NB1 = E * FF // P
        b1_raw, router = sb("b1_raw", [NB1, P]), sb("router", [P, E])
        zeros = sb("zeros", [P, 8, D])
        tri, ones = sb("tri", [P, P], BF16), sb("ones", [P, P], BF16)
        order_i, order = sb("order_i", [P, E], I32), sb("order", [P, E])
        dump_i, dump, dump_step = sb("dump_i", [P, 1], I32), sb("dump", [P, 1]), sb("dump_step", [P, 1])
        y_s, yT = sb("y_s", [P, D]), sb("yT", [P, P])
        top, first, place, valid = sb("top", [P, 1]), sb("first", [P, 1]), sb("place", [P, 1]), sb("valid", [P, 1])
        sel, rank, base = sb("sel", [P, E]), sb("rank", [P, E]), sb("base", [P, E])
        onehot = sb("onehot", [P, E], BF16)
        dest = sb("dest", [P, 1], U32)
        NZ = DUMP // (8 * P)
        STEPS = 14
        r_loaded, r_const, zeros_done, zeroed, scattered = (sem("r_loaded"), sem("r_const"), sem("zeros_done"),
                                                            sem("zeroed"), sem("scattered"))
        b1_done, b1_copied = sem("b1_done"), sem("b1_copied")
        step_done, dump_done, rows_ready = sem("step_done"), sem("dump_done"), sem("rows_ready")
        yt_done, yT_ready, logits_done, rank_done, dest_done = (sem("yt_done"), sem("yT_ready"), sem("logits_done"),
                                                                sem("rank_done"), sem("dest_done"))

        mask_loaded, mask_done = sem("mask_loaded"), sem("mask_done")
        ct_loaded, cv_loaded, res_loaded, y_stored = (sem("ct_loaded"), sem("cv_loaded"), sem("res_loaded"),
                                                      sem("y_stored"))
        ct_done, catT_ready = sem("ct_done"), sem("catT_ready")
        g_done, q_copied = sem("g_done"), sem("q_copied")
        s_done, max_done, sub_done, exp_done = sem("s_done"), sem("max_done"), sem("sub_done"), sem("exp_done")
        sum_done, inv_done, p_done = sem("sum_done"), sem("inv_done"), sem("p_done")
        t_done, pT_copied, c_done, cT_copied, o_done = (sem("t_done"), sem("pT_copied"), sem("c_done"),
                                                        sem("cT_copied"), sem("o_done"))
        z_done, st_done, mv_done, veps_done, rstd_done, y_done = (
            sem("z_done"), sem("st_done"), sem("mv_done"), sem("veps_done"), sem("rstd_done"), sem("y_done"))
        block = ctx.enter_context(nc.Block())

        def have(n):
            return not isinstance(n, int) or 0 <= n < NCH

        def routed(i):
            return not isinstance(i, int) or 0 <= i - 2 < NPAIR

        def slots(eng, slot):
            for i in (0, 1):
                for c in range(4):
                    slot(i, c)
            with eng.Fori(2, NPAIR - 1) as i:
                for c in range(4):
                    slot(i, c)
            for i in (NPAIR - 1, NPAIR, NPAIR + 1):
                for c in range(4):
                    slot(i, c)

        def rows(t, i):
            return t[bass.ds(i, 1), :, :].rearrange("o p d -> p (o d)")

        @block.sync
        def _(sp):
            def load_c(dst, i, loaded):
                sp.dma_start(dst[:, :, :], cat[bass.ds(2 * i, 2), :, :].rearrange("b t d -> t b d")).then_inc(loaded, 16)

            def pair(i):
                if have(4 * (i + 1)):
                    sp.wait_ge(ct_done, i + 1)
                    load_c(c_t, i + 1, ct_loaded)
                if have(4 * i):
                    wait(sp, c_done, 4 * i)
                    load_c(c_v, i, cv_loaded)
                    wait(sp, z_done, i)
                    sp.dma_start(x_res[:, :], rows(x_in, i)).then_inc(res_loaded, 16)
                if have(4 * (i - 1)):
                    sp.wait_ge(y_done, i)
                    sp.dma_start(rows(x_out, i - 1), y[:, :]).then_inc(y_stored, 16)

            sp.dma_start(mask_sb[:, :, :].rearrange("p b s -> p (b s)"), bcast_rows(mask.rearrange("b s -> (b s)")))\
                .then_inc(mask_loaded, 16)
            load_c(c_t, 0, ct_loaded)
            sp.dma_start(router[:, :], a["L1_ffn_router_w"]).then_inc(r_loaded, 16)
            sp.dma_start(b1_raw[:, :], a["L1_ffn_b1"].rearrange("e (t p) -> (e t) p", p=P)).then_inc(r_loaded, 16)
            sp.wait_ge(zeros_done, 1)
            for n in range(NZ):
                sp.dma_start(xe[n * 8 * P:(n + 1) * 8 * P, :].rearrange("(r p) d -> p r d", p=P), zeros[:, :, :])\
                    .then_inc(zeroed, 16)
            sp.dma_start(ye[DUMP:DUMP + 1, :], zeros[0:1, 0, :]).then_inc(zeroed, 16)
            pair(0)
            with sp.Fori(1, NPAIR - 1) as i:
                pair(i)
            pair(NPAIR - 1)
            pair(NPAIR)
            sp.wait_ge(y_stored, 16 * NPAIR)
            sp.wait_ge(zeroed, 16 * (NZ + 1))
            sp.wait_ge(scattered, 16 * NPAIR)

        @block.tensor
        def _(pe):
            def transpose_cat(i):
                pe.wait_ge(ct_loaded, 16 * (i + 1))
                wait(pe, catT_ready, i)
                for b in range(2):
                    last = nc.tensor.transpose(ps_x[:, b * T:(b + 1) * T], c_t[:, b, :], core.ident[:, :])
                last.then_inc(ct_done, 1)

            def slot(i, c):
                n = 4 * i + c
                if c == 1 and routed(i):
                    pe.wait_ge(yT_ready, i - 1)
                    nc.tensor.matmul(ps_x[:, 384:384 + E], yT[:, :], router[:, :], start=True, stop=True)\
                        .then_inc(logits_done, 1)
                if have(n):
                    if c == 0:
                        pe.wait_ge(catT_ready, i + 1)
                    wait(pe, q_copied, n - 1)
                    for h in range(4):
                        last = nc.tensor.matmul(ps_g[c % 2][:, h * P:(h + 1) * P].rearrange("p (b s) -> p b s", b=2),
                                                w_score[:, 4 * c + h, :], catT[:, :, S:T], start=True, stop=True)
                    last.then_inc(g_done, 1)
                if have(n - 2):
                    wait(pe, p_done, n - 1)
                    wait(pe, pT_copied, n - 2)
                    for m in range(4):
                        last = nc.tensor.transpose(ps_t[:, m * P:(m + 1) * P], prob[:, c % 2, m, :], core.ident[:, :])
                    last.then_inc(t_done, 1)
                if have(n - 3):
                    wait(pe, cT_copied, n - 2)
                    if c == 3:
                        wait(pe, z_done, i)
                    for h in range(4):
                        last = nc.tensor.matmul(ps_o[:, 0:D], ctxT[:, h, :, :].rearrange("p b s -> p (b s)"),
                                                w_vo[:, h % 2, (2 * ((c + 1) % 4)) + h // 2, :],
                                                start=(c == 3 and h == 0), stop=(c == 2 and h == 3))
                    last.then_inc(o_done, 1)
                if have(n):
                    pe.wait_ge(q_copied, n + 1)
                    wait(pe, sub_done, n - 1)
                    if c == 0:
                        pe.wait_ge(mask_done, 2)
                    nc.tensor.matmul(ps_s[c % 2][:, :].rearrange("p (b h t) -> p b h t", b=2, h=2), core.identb[:, :],
                                     mask_bias[:, bass.ds(2 * i, 2), None, :].to_broadcast([P, 2, 2, T]),
                                     start=True, stop=False)
                    for m in range(4):
                        b, hp = m // 2, m % 2
                        last = nc.tensor.matmul(
                            ps_s[c % 2][:, m * T:(m + 1) * T],
                            query[:, c % 2, b, 2 * hp:2 * hp + 2, :].rearrange("p h s -> p (h s)"), catT[:, b, :],
                            start=False, stop=(m == 3))
                    last.then_inc(s_done, 1)
                if c == 3 and have(n + 1) and have(n):
                    if routed(i):
                        pe.wait_ge(step_done, STEPS * (i - 2) + 8)
                    transpose_cat(i + 1)
                if c == 2 and routed(i):
                    pe.wait_ge(step_done, STEPS * (i - 2) + 6)
                    nc.tensor.matmul(ps_x[:, 400:400 + E], tri[:, :], onehot[:, :], start=True, stop=True)
                    nc.tensor.matmul(ps_x[:, 416:416 + E], ones[:, :], onehot[:, :], start=True, stop=True)\
                        .then_inc(rank_done, 1)
                if c == 0 and routed(i):
                    pe.wait_ge(y_done, i - 1)
                    nc.tensor.transpose(ps_x[:, 256:256 + P], y[:, :], core.ident[:, :]).then_inc(yt_done, 1)
                if have(n - 2):
                    wait(pe, pT_copied, n - 1)
                    wait(pe, cT_copied, n - 2)
                    if c == 2:
                        pe.wait_ge(cv_loaded, 16 * (i + 1))
                    for b in range(2):
                        last = nc.tensor.matmul(ps_c[:, b * 256:(b + 1) * 256], c_v[:, b, :],
                                                probT[:, 2 * b:2 * b + 2, :].rearrange("p h e -> p (h e)"),
                                                start=True, stop=True)
                    last.then_inc(c_done, 1)

            pe.wait_ge(r_loaded, 32)
            nc.tensor.transpose(ps_g[0][:, 0:NB1], b1_raw[:, :], core.ident[0:NB1, 0:NB1]).then_inc(b1_done, 1)
            transpose_cat(0)
            pe.wait_ge(b1_copied, 1)
            pe.wait_ge(r_const, 9)
            slots(pe, slot)

        @block.scalar
        def _(act):
            def copy_catT(i):
                act.wait_ge(ct_done, i + 1)
                wait(act, s_done, 4 * i)
                nc.scalar.activation(catT[:, :, :].rearrange("p b t -> p (b t)"), ps_x[:, 0:2 * T], ACT.Copy)\
                    .then_inc(catT_ready, 1)

            def slot(i, c):
                n = 4 * i + c
                if have(n - 3):
                    wait(act, c_done, n - 2)
                    wait(act, o_done, n - 3)
                    nc.scalar.activation(ctxT[:, :, :, :], ps_c[:, :].rearrange("p (b h s) -> p h b s", b=2, h=4),
                                         ACT.Copy).then_inc(cT_copied, 1)
                if have(n):
                    act.wait_ge(g_done, n + 1)
                    wait(act, s_done, n - 1)
                    nc.scalar.activation(query[:, c % 2, :, :, :],
                                         ps_g[c % 2][:, :].rearrange("p (h b s) -> p b h s", h=4, b=2), ACT.Copy)\
                        .then_inc(q_copied, 1)
                if have(n - 1):
                    wait(act, sub_done, n)
                    flat = prob[:, (c + 1) % 2, :, :].rearrange("p h t -> p (h t)")
                    nc.scalar.activation(flat, flat, ACT.Exp).then_inc(exp_done, 1)
                if have(n - 2):
                    wait(act, t_done, n - 1)
                    wait(act, c_done, n - 2)
                    nc.scalar.activation(probT[:, :, :].rearrange("p h e -> p (h e)"), ps_t[:, :], ACT.Copy)\
                        .then_inc(pT_copied, 1)
                if c == 0 and routed(i):
                    act.wait_ge(yt_done, i - 1)
                    wait(act, logits_done, i - 2)
                    nc.scalar.activation(yT[:, :], ps_x[:, 256:256 + P], ACT.Copy).then_inc(yT_ready, 1)
                if c == 3 and have(n + 1) and have(n):
                    copy_catT(i + 1)

            act.wait_ge(b1_done, 1)
            nc.scalar.activation(route.b1T[:, :], ps_g[0][:, 0:NB1], ACT.Copy).then_inc(b1_copied, 1)
            copy_catT(0)
            slots(act, slot)

        @block.vector
        def _(dve):
            def steps(i, at, ins):
                ins.then_inc(step_done, 1)
                dve.wait_ge(step_done, STEPS * (i - 2) + at)

            def choose_expert(i):
                logits = ps_x[:, 384:384 + E]
                diff = route.diff[:, bass.ds(i - 2, 1), :].rearrange("p o e -> p (o e)")
                dve.wait_ge(logits_done, i - 1)
                steps(i, 1, nc.vector.tensor_reduce(top[:, :], logits, AX.X, ALU.max))
                steps(i, 2, nc.vector.tensor_scalar(diff, logits, top[:, :], None, ALU.subtract))
                steps(i, 3, nc.vector.tensor_scalar(sel[:, :], logits, top[:, :], 0.0, ALU.subtract, ALU.is_ge))
                steps(i, 4, nc.vector.tensor_tensor(sel[:, :], sel[:, :], order[:, :], ALU.mult))
                steps(i, 5, nc.vector.tensor_reduce(first[:, :], sel[:, :], AX.X, ALU.max))
                steps(i, 6, nc.vector.tensor_tensor(onehot[:, :], sel[:, :], first[:, :].to_broadcast([P, E]),
                                                    ALU.is_equal))

            def count_ranks(i):
                dve.wait_ge(rank_done, i - 1)
                steps(i, 7, nc.vector.tensor_tensor(rank[:, :], base[:, :], ps_x[:, 400:400 + E], ALU.add))
                steps(i, 8, nc.vector.tensor_tensor(base[:, :], base[:, :], ps_x[:, 416:416 + E], ALU.add))

            def choose_row(i):
                wait(dve, scattered, 16 * (i - 2))
                nc.vector.tensor_copy(y_s[:, :], y[:, :]).then_inc(rows_ready, 1)
                steps(i, 9, nc.vector.tensor_tensor(rank[:, :], rank[:, :], onehot[:, :], ALU.mult))
                steps(i, 10, nc.vector.tensor_reduce(place[:, :], rank[:, :], AX.X, ALU.add))
                steps(i, 11, nc.vector.tensor_scalar(valid[:, :], place[:, :], float(CAP), None, ALU.is_le))
                wait(dve, dump_done, i - 2)
                steps(i, 12, nc.vector.scalar_tensor_tensor(out=place[:, :], in0=first[:, :], scalar=float(-CAP),
                                                            in1=place[:, :], op0=ALU.mult, op1=ALU.add))
                steps(i, 13, nc.vector.tensor_scalar(place[:, :], place[:, :], float(E * CAP - 1), dump[:, :],
                                                     ALU.add, ALU.subtract))
                steps(i, 14, nc.vector.tensor_scalar(place[:, :], place[:, :], valid[:, :], dump[:, :],
                                                     ALU.mult, ALU.add))
                nc.vector.tensor_copy(dest[:, :], place[:, :]).then_inc(dest_done, 1)
                nc.vector.tensor_copy(route.row[:, bass.ds(i - 2, 1)], place[:, :]).then_inc(dest_done, 1)

            def slot(i, c):
                n = 4 * i + c
                if c == 3 and routed(i):
                    count_ranks(i)
                if have(n - 1):
                    par = (c + 1) % 2
                    wait(dve, exp_done, n)
                    nc.vector.tensor_reduce(row_sum[:, par, :], prob[:, par, :, :], AX.X, ALU.add).then_inc(sum_done, 1)
                    wait(dve, sum_done, n)
                    nc.vector.reciprocal(inv_sum[:, par, :], row_sum[:, par, :]).then_inc(inv_done, 1)
                if c == 2 and have(4 * (i - 1)):
                    dve.wait_ge(res_loaded, 16 * i)
                    dve.wait_ge(o_done, 4 * i)
                    nc.vector.tensor_tensor(z[:, :], x_res[:, :], ps_o[:, 0:D], ALU.add).then_inc(z_done, 1)
                    dve.wait_ge(z_done, i)
                    nc.vector.bn_stats(stats[:, :], z[:, :]).then_inc(st_done, 1)
                    dve.wait_ge(st_done, i)
                if have(n):
                    scores = ps_s[c % 2][:, :].rearrange("p (h t) -> p h t", h=4)
                    dve.wait_ge(s_done, n + 1)
                    nc.vector.tensor_reduce(row_max[:, c % 2, :], scores, AX.X, ALU.max).then_inc(max_done, 1)
                    wait(dve, t_done, n - 1)
                    dve.wait_ge(max_done, n + 1)
                    nc.vector.tensor_tensor(prob[:, c % 2, :, :], scores,
                                            row_max[:, c % 2, :, None].to_broadcast([P, 4, T]), ALU.subtract)\
                        .then_inc(sub_done, 1)
                if c == 1 and routed(i):
                    choose_expert(i)
                if c == 2 and have(4 * (i - 1)):
                    nc.vector.bn_aggr(mean_var[:, :], stats[:, :]).then_inc(mv_done, 1)
                    dve.wait_ge(mv_done, i)
                    nc.vector.tensor_scalar(rstd[:, :], mean_var[:, 1:2], EPS, None, ALU.add).then_inc(veps_done, 1)
                if c == 3 and routed(i):
                    choose_row(i)
                if c == 3 and have(4 * (i - 1)):
                    dve.wait_ge(rstd_done, i)
                    wait(dve, y_stored, 16 * (i - 1) if isinstance(i, int) else 16 * i - 16)
                    nc.vector.tensor_scalar(y[:, :], z[:, :], mean_var[:, 0:1], rstd[:, :], ALU.subtract, ALU.mult)\
                        .then_inc(y_done, 1)

            for tile in (tri, ones, base):
                nc.vector.memset(tile[:, :], 0.0 if tile is base else 1.0).then_inc(r_const, 1)
            nc.vector.memset(dump_step[:, :], float(P)).then_inc(r_const, 1)
            nc.vector.memset(zeros[:, :, :], 0.0).then_inc(zeros_done, 1)
            dve.wait_ge(r_const, 7)
            nc.vector.tensor_copy(order[:, :], order_i[:, :]).then_inc(r_const, 1)
            nc.vector.tensor_copy(dump[:, :], dump_i[:, :]).then_inc(r_const, 1)
            dve.wait_ge(r_const, 9)
            nc.vector.memset(mask_bias[:, :, :], 0.0).then_inc(mask_done, 1)
            dve.wait_ge(mask_loaded, 16)
            dve.wait_ge(mask_done, 1)
            nc.vector.tensor_scalar(mask_bias[:, :, 0:S], mask_sb[:, :, :], -NEG, NEG, ALU.mult, ALU.add).then_inc(mask_done, 1)
            slots(dve, slot)

        @block.gpsimd
        def _(pool):
            def power(i):
                pool.wait_ge(veps_done, i)
                nc.gpsimd.tensor_tensor(rstd[:, :], rstd[:, :], core.eps_pow[:, :], ALU.pow).then_inc(rstd_done, 1)

            def slot(i, c):
                n = 4 * i + c
                if c == 3 and have(4 * (i - 1)):
                    power(i)
                if have(n - 1):
                    par = (c + 1) % 2
                    wait(pool, inv_done, n)
                    nc.gpsimd.tensor_tensor(prob[:, par, :, :], prob[:, par, :, :],
                                            inv_sum[:, par, :, None].to_broadcast([P, 4, T]), ALU.mult)\
                        .then_inc(p_done, 1)
                if c == 3 and routed(i):
                    scatter(i)

            def scatter(i):
                pool.wait_ge(rows_ready, i - 1)
                pool.wait_ge(dest_done, 2 * (i - 1))
                nc.gpsimd.tensor_tensor(dump[:, :], dump[:, :], dump_step[:, :], ALU.add).then_inc(dump_done, 1)
                pool.indirect_dma_start(out=xe, out_offset=bass.IndirectOffsetOnAxis(ap=dest[:, 0:1], axis=0),
                                        in_=y_s[:, :], in_offset=None).then_inc(scattered, 16)

            pool.wait_ge(r_const, 4)
            nc.gpsimd.iota(order_i[:, :], pattern=[[-1, E]], base=E, channel_multiplier=0).then_inc(r_const, 1)
            pool.wait_ge(r_const, 5)
            nc.gpsimd.iota(dump_i[:, :], pattern=[[P, 1]], base=DUMP, channel_multiplier=1).then_inc(r_const, 1)
            pool.wait_ge(r_const, 6)
            nc.gpsimd.affine_select(out=tri[:, :], in_=tri[:, :], compare_op=ALU.is_ge, fill=0.0, base=0,
                                    pattern=[[1, P]], channel_multiplier=-1).then_inc(r_const, 1)
            pool.wait_ge(zeroed, 16 * (NZ + 1))
            slots(pool, slot)


class Routing:

    def __init__(self, core, ctx):
        self.diff = core.sb("route_diff", [P, NPAIR, E], F32, ctx)
        self.row = core.sb("route_row", [P, NPAIR], F32, ctx)
        self.b1T = core.sb("route_b1T", [P, E * FF // P], F32, ctx)


def moe_phase(core, x_in, x_out, xe, ye, a, route):
    with ExitStack() as ctx:
        gate = core.sb("moe_gate", [P, NPAIR], F32, ctx)
        src_row = core.sb("moe_src_row", [P, NPAIR], U32, ctx)
        moe_experts(core, xe, ye, a, route, gate, src_row)
        moe_combine(core, x_in, x_out, gate, src_row, ye)


def moe_experts(core, xe, ye, a, route, gate, src_row):
    nc = core.nc
    NT, NR = FF // P, CAP // P
    with ExitStack() as ctx:
        def sb(name, shape, dt=F32):
            return core.sb(f"exp_{name}", shape, dt, ctx)

        def sem(name):
            return core.sem(f"exp_{name}", ctx)

        rows = sb("rows", [P, 2, NR, D])
        w1, w2 = sb("w1", [P, 2, FF]), sb("w2", [P, 2, NT, D])
        b2 = sb("b2", [P, 2, D])
        b1_col = sb("b1_col", [P, 2, NT])
        rT = sb("rT", [P, 2, CAP])
        hidden = sb("hidden", [P, 2, NT, CAP])
        o = sb("o", [P, 2, NR, D])
        expo, total, valid = sb("expo", [P, NPAIR, E]), sb("total", [P, NPAIR]), sb("valid", [P, NPAIR])
        exp_done, g_steps = sem("exp_done"), sem("gate_steps")
        ps_x, ps_out = core.bank[0], core.bank[1]
        ps_h = [core.bank[2], core.bank[3], core.bank[4], core.bank[5]]
        rows_loaded = [sem(f"rows_loaded{p}") for p in range(2)]
        w1_loaded = [sem(f"w1_loaded{p}") for p in range(2)]
        w2_loaded = [sem(f"w2_loaded{p}") for p in range(2)]
        stored = [sem(f"stored{p}") for p in range(2)]
        rt_done, rT_ready, h_done, relu_done, out_done, o_done, b1_ready = (
            sem("rt_done"), sem("rT_ready"), sem("h_done"), sem("relu_done"), sem("out_done"), sem("o_done"),
            sem("b1_ready"))
        block = ctx.enter_context(nc.Block())

        def slots(eng, slot):
            for i in range(-1, 1):
                slot(i, i // 2, i % 2, lambda j: 0 <= j < E)
            with eng.Fori(0, E // 2 - 2) as k:
                slot(2 * k + 1, k, 1, lambda j: True)
                slot(2 * k + 2, k + 1, 0, lambda j: True)
            for i in range(E - 3, E + 1):
                slot(i, i // 2, i % 2, lambda j: 0 <= j < E)

        def here(on, i, d):
            return on(i + d if isinstance(i, int) else 0)

        @block.sync
        def _(sp):
            def load_rows(i, par):
                wait(sp, rt_done, i - 1)
                sp.dma_start(rows[:, par, :, :], xe[bass.ds(i * CAP, CAP), :].rearrange("(r p) d -> p r d", p=P))\
                    .then_inc(rows_loaded[par], 16)

            def slot(i, k, par, on):
                if here(on, i, 2):
                    load_rows(i + 2, par)
                if here(on, i, 1):
                    wait(sp, h_done, NT * i)
                    sp.dma_start(w1[:, 1 - par, :], a["L1_ffn_w1"][bass.ds(i + 1, 1), :, :]
                                 .rearrange("o p f -> p (o f)")).then_inc(w1_loaded[1 - par], 16)
                wait(sp, o_done, i)
                if here(on, i, -1):
                    sp.dma_start(ye[bass.ds((i - 1) * CAP, CAP), :].rearrange("(r p) d -> p r d", p=P),
                                 o[:, 1 - par, :, :]).then_inc(stored[1 - par], 16)
                if here(on, i, 1):
                    sp.dma_start(w2[:, 1 - par, :, :], a["L1_ffn_w2"][bass.ds(i + 1, 1), :, :]
                                 .rearrange("o (t p) d -> p (o t) d", p=P)).then_inc(w2_loaded[1 - par], 16)
                    sp.dma_start(b2[:, 1 - par, :], a["L1_ffn_b2"][bass.ds(i + 1, 1), :].to_broadcast([P, D]))\
                        .then_inc(w2_loaded[1 - par], 16)

            load_rows(0, 0)
            slots(sp, slot)
            for par in range(2):
                sp.wait_ge(stored[par], 16 * (E // 2))

        @block.tensor
        def _(pe):
            def slot(i, k, par, on):
                if here(on, i, 0):
                    wait(pe, rT_ready, i + 1)
                    wait(pe, w1_loaded[par], 16 * (k + 1))
                    for t in range(NT):
                        wait(pe, relu_done, NT * (i - 1) + t + 1)
                        nc.tensor.matmul(ps_h[t][:, :], w1[:, par, t * P:(t + 1) * P], rT[:, par, :],
                                         start=True, stop=True).then_inc(h_done, 1)
                if here(on, i, 1):
                    wait(pe, rows_loaded[1 - par], 16 * (k + par + 1))
                    wait(pe, rT_ready, i + 1)
                    for r in range(NR):
                        last = nc.tensor.transpose(ps_x[:, r * P:(r + 1) * P], rows[:, 1 - par, r, :], core.ident[:, :])
                    last.then_inc(rt_done, 1)
                if here(on, i, -1):
                    wait(pe, relu_done, NT * i)
                    wait(pe, w2_loaded[1 - par], 32 * (k + par))
                    wait(pe, o_done, i - 1)
                    for r in range(NR):
                        for t in range(NT):
                            last = nc.tensor.matmul(ps_out[:, r * P:(r + 1) * P],
                                                    hidden[:, 1 - par, t, r * P:(r + 1) * P], w2[:, 1 - par, t, :],
                                                    start=(t == 0), stop=(t == NT - 1))
                    last.then_inc(out_done, 1)

            slots(pe, slot)

        @block.scalar
        def _(act):
            def slot(i, k, par, on):
                if here(on, i, 1):
                    wait(act, rt_done, i + 2)
                    wait(act, h_done, NT * i)
                    nc.scalar.activation(rT[:, 1 - par, :], ps_x[:, :], ACT.Copy).then_inc(rT_ready, 1)
                if here(on, i, 0):
                    wait(act, out_done, i - 1)
                    wait(act, b1_ready, i + 1)
                    for t in range(NT):
                        wait(act, h_done, NT * i + t + 1)
                        nc.scalar.activation(hidden[:, par, t, :], ps_h[t][:, :], ACT.Relu,
                                             bias=b1_col[:, par, t:t + 1]).then_inc(relu_done, 1)

            nc.scalar.activation(expo[:, :, :], route.diff[:, :, :], ACT.Exp).then_inc(exp_done, 1)
            slots(act, slot)

        @block.vector
        def _(dve):
            def slot(i, k, par, on):
                if here(on, i, 0):
                    wait(dve, relu_done, NT * (i - 1))
                    nc.vector.tensor_copy(b1_col[:, par, :], route.b1T[:, bass.ds(NT * i, NT)]).then_inc(b1_ready, 1)
                if here(on, i, -1):
                    wait(dve, out_done, i)
                    wait(dve, stored[1 - par], 16 * (k + par - 1))
                    nc.vector.tensor_tensor(o[:, 1 - par, :, :], ps_out[:, :].rearrange("p (r d) -> p r d", r=NR),
                                            b2[:, 1 - par, :][:, None, :].to_broadcast([P, NR, D]), ALU.add)\
                        .then_inc(o_done, 1)

            dve.wait_ge(exp_done, 1)
            nc.vector.tensor_reduce(total[:, :], expo[:, :, :], AX.X, ALU.add).then_inc(g_steps, 1)
            nc.vector.tensor_scalar(valid[:, :], route.row[:, :], float(DUMP), None, ALU.is_lt).then_inc(g_steps, 1)
            dve.wait_ge(g_steps, 2)
            nc.vector.reciprocal(gate[:, :], total[:, :]).then_inc(g_steps, 1)
            dve.wait_ge(g_steps, 3)
            nc.vector.tensor_tensor(gate[:, :], gate[:, :], valid[:, :], ALU.mult).then_inc(g_steps, 1)
            nc.vector.tensor_scalar(total[:, :], route.row[:, :], float(DUMP), None, ALU.min).then_inc(g_steps, 1)
            dve.wait_ge(g_steps, 5)
            nc.vector.tensor_copy(src_row[:, :], total[:, :]).then_inc(g_steps, 1)
            slots(dve, slot)


def moe_combine(core, x_in, x_out, gate, src_row, ye):
    nc = core.nc
    GP = 4
    NG = NPAIR // GP
    with ExitStack() as ctx:
        def sb(name, shape, dt=F32):
            return core.sb(f"comb_{name}", shape, dt, ctx)

        def sem(name):
            return core.sem(f"comb_{name}", ctx)

        x, got = sb("x", [P, NPAIR, D]), sb("got", [P, NPAIR, D])
        stats = sb("stats", [P, NPAIR, 6])
        mean_var = sb("mean_var", [P, NPAIR, 2])
        rstd = sb("rstd", [P, NPAIR])
        y = sb("y", [P, NPAIR, D])
        gathered = [sem(f"gathered{g}") for g in range(NG)]
        x_loaded = [sem(f"x_loaded{g}") for g in range(NG)]
        stored = sem("stored")
        z_done, stats_done, mv_done, veps_done, rstd_done, y_done = (
            sem("z_done"), sem("stats_done"), sem("mv_done"), sem("veps_done"), sem("rstd_done"), sem("y_done"))
        block = ctx.enter_context(nc.Block())

        @block.sync
        def _(sp):
            for g in range(NG):
                sp.dma_start(x[:, g * GP:(g + 1) * GP, :], x_in[g * GP:(g + 1) * GP, :, :].rearrange("n p d -> p n d"))\
                    .then_inc(x_loaded[g], 16)
            for g in range(NG):
                sp.wait_ge(y_done, g + 1)
                sp.dma_start(x_out[g * GP:(g + 1) * GP, :, :].rearrange("n p d -> p n d"), y[:, g * GP:(g + 1) * GP, :])\
                    .then_inc(stored, 16)
            sp.wait_ge(stored, 16 * NG)

        @block.vector
        def _(dve):
            def norm(g):
                dve.wait_ge(rstd_done, g + 1)
                for n in range(g * GP, (g + 1) * GP):
                    last = nc.vector.tensor_scalar(y[:, n, :], got[:, n, :], mean_var[:, n, 0:1], rstd[:, n:n + 1],
                                                   ALU.subtract, ALU.mult)
                last.then_inc(y_done, 1)

            for g in range(NG):
                group = range(g * GP, (g + 1) * GP)
                dve.wait_ge(x_loaded[g], 16)
                dve.wait_ge(gathered[g], 16 * GP)
                for n in group:
                    last = nc.vector.scalar_tensor_tensor(out=got[:, n, :], in0=got[:, n, :], scalar=gate[:, n:n + 1],
                                                          in1=x[:, n, :], op0=ALU.mult, op1=ALU.add)
                last.then_inc(z_done, 1)
                dve.wait_ge(z_done, g + 1)
                for n in group:
                    last = nc.vector.bn_stats(stats[:, n, :], got[:, n, :])
                last.then_inc(stats_done, 1)
                dve.wait_ge(stats_done, g + 1)
                for n in group:
                    last = nc.vector.bn_aggr(mean_var[:, n, :], stats[:, n, :])
                last.then_inc(mv_done, 1)
                dve.wait_ge(mv_done, g + 1)
                nc.vector.tensor_scalar(rstd[:, g * GP:(g + 1) * GP], mean_var[:, g * GP:(g + 1) * GP, 1], EPS, None,
                                        ALU.add).then_inc(veps_done, 1)
                if g > 0:
                    norm(g - 1)
            norm(NG - 1)

        @block.gpsimd
        def _(pool):
            def gather(g):
                for n in range(g * GP, (g + 1) * GP):
                    pool.indirect_dma_start(out=got[:, n, :], out_offset=None, in_=ye,
                                            in_offset=bass.IndirectOffsetOnAxis(ap=src_row[:, n:n + 1], axis=0))\
                        .then_inc(gathered[g], 16)

            gather(0)
            gather(1)
            for g in range(NG):
                if g + 2 < NG:
                    gather(g + 2)
                pool.wait_ge(veps_done, g + 1)
                cols = rstd[:, g * GP:(g + 1) * GP]
                nc.gpsimd.tensor_tensor(cols, cols, core.eps_pow[:, :].to_broadcast([P, GP]), ALU.pow)\
                    .then_inc(rstd_done, 1)


def decoder(nc, a, out):
    stage = [nc.dram_tensor(f"stage{n}", (NPAIR, P, D), F32, kind="Internal").ap() for n in range(5)]
    cat = nc.dram_tensor("cat", (B, 2 * S, D), F32, kind="Internal").ap()
    pairs = lambda t: t.rearrange("(n b) s d -> n (b s) d", b=2)
    with ExitStack() as ctx:
        core = Core(nc, ctx)
        wqkv = a["L0_attn_w_qkv"]
        self_loads = low_head_loads(core, ctx, "self", wqkv[:, 0:D], wqkv[:, D:2 * D], wqkv[:, 2 * D:3 * D],
                                    a["L0_attn_w_proj"], a["L0_attn_b_proj"])
        cross_loads = low_head_loads(core, ctx, "cross", a["L0_xattn_Wq"], a["L0_xattn_Wk"], a["L0_xattn_Wv"],
                                     a["L0_xattn_Wo"], a["L0_xattn_bo"])
        ffn_loads = feed_forward_loads(core, ctx, a["L0_ffn_w_fc"], a["L0_ffn_w_proj"], a["L0_ffn_u"],
                                       a["L0_ffn_v"], a["L0_ffn_fast_b"], a["L0_ffn_gate"])
        w_kv = a["L1_xattn_Wkv"]
        diff_weights = EarlyWeights(core, ctx, "diff", H1, a["L1_attn_Wq"], a["L1_attn_Wk"], a["L1_attn_Wv"],
                                    a["L1_attn_Wo"])
        latent_weights = EarlyWeights(core, ctx, "lat", H1 // 2, a["L1_xattn_Wq"], w_kv[:, 0:H1 * HD1],
                                      w_kv[:, H1 * HD1:2 * H1 * HD1], a["L1_xattn_Wout"])
        constants_phase(core, self_loads)
        low_head_phase(core, "self", pairs(a["x"]), None, stage[0], self_loads, False, False,
                       (cross_loads,) + ffn_loads)
        low_head_phase(core, "cross", stage[0], pairs(a["ctx_1024"]), stage[1], cross_loads, True, True,
                       (diff_weights, latent_weights))
        feed_forward_phase(core, stage[1], stage[2], ffn_loads)
        differential_attention_phase(core, stage[2], stage[3], cat, pairs(a["ctx_1024"]), a, diff_weights)
        xe = nc.dram_tensor("expert_rows", (DUMP + B * S, D), F32, kind="Internal").ap()
        ye = nc.dram_tensor("expert_outputs", (DUMP + 1, D), F32, kind="Internal").ap()
        route = Routing(core, ctx)
        latent_attention_phase(core, stage[3], stage[4], cat, a["mask_BxS2_bk0"], a, latent_weights, route, xe, ye)
        moe_phase(core, stage[4], pairs(out), xe, ye, a, route)


_INS = ['x', 'ctx_1024', 'mask_BxS2_bk0', 'L0_attn_w_qkv', 'L0_attn_w_proj', 'L0_attn_b_proj', 'L0_xattn_Wq',
        'L0_xattn_Wk', 'L0_xattn_Wv', 'L0_xattn_Wo', 'L0_xattn_bo', 'L0_ffn_fast_b', 'L0_ffn_w_fc', 'L0_ffn_w_proj',
        'L0_ffn_u', 'L0_ffn_v', 'L0_ffn_gate', 'L1_attn_Wq', 'L1_attn_Wk', 'L1_attn_Wv', 'L1_attn_Wo', 'L1_attn_lq1',
        'L1_attn_lk1', 'L1_attn_lq2', 'L1_attn_lk2', 'L1_xattn_g1', 'L1_xattn_b1', 'L1_xattn_g2', 'L1_xattn_b2',
        'L1_xattn_Wq', 'L1_xattn_Wkv', 'L1_xattn_Wout', 'L1_ffn_router_w', 'L1_ffn_w1', 'L1_ffn_b1', 'L1_ffn_w2',
        'L1_ffn_b2']


def kernel(**inputs):
    import numpy as _np
    import concourse.bacc as _bacc
    from concourse import mybir as _mybir
    from concourse.bass_utils import run_bass_kernel_spmd as _run

    nc = _bacc.Bacc("TRN2", target_bir_lowering=False, num_devices=1)
    arrays, args = {}, {}
    for name in _INS:
        a = _np.ascontiguousarray(inputs[name])
        if a.ndim == 0:
            a = a.reshape(1)
        arrays[f"in_{name}_dram"] = a
        args[name] = nc.dram_tensor(f"in_{name}_dram", a.shape, _mybir.dt.from_np(a.dtype), kind="ExternalInput").ap()
    out = nc.dram_tensor("out_0_dram", (B, S, D), _mybir.dt.float32, kind="ExternalOutput").ap()
    decoder(nc, args, out)
    r = _run(nc, [arrays], core_ids=[0])
    return r.results[0]["out_0_dram"]
```
